# Optimizing a Trainium2 kernel written in Bass

```python
import numpy as np
import jax
import jax.numpy as jnp

def _softmax(x, axis=-1):
    return jax.nn.softmax(x, axis=axis)

def _gelu(x):
    return jax.nn.gelu(x, approximate=True)

def _silu(x):
    return jax.nn.silu(x)

def _sigmoid(x):
    return jax.nn.sigmoid(x)

def _layernorm(x, axis=-1, eps=1e-05):
    m = jnp.mean(x, axis=axis, keepdims=True)
    v = jnp.var(x, axis=axis, keepdims=True)
    return (x - m) / jnp.sqrt(v + eps)

def _scatter_add(tgt, idx, src, axis=0):
    return tgt.at[idx].add(src)

def _segment_sum(src, seg, n):
    return jax.ops.segment_sum(src, seg, n)
kernel_name = 'mk_adaln_attn_ffn_d2_seqx_r4_0ed9b6'

def setup_inputs(seed: int=0):
    np.random.seed(seed)
    _w = jnp.asarray

    def _rec_inputs():
        import jax
        import jax.numpy as jnp
        _rk = jax.random.key(seed)
        x = -0.000125 + 0.9999 * jax.random.normal(jax.random.fold_in(_rk, 1), (4, 512, 512), jnp.float32)
        _lenS = 512 - jax.random.randint(jax.random.fold_in(_rk, 7), (4,), 0, max(1, 512 // 4) + 1, jnp.int32)
        _lenS2 = 512 - jax.random.randint(jax.random.fold_in(_rk, 8), (4,), 0, max(1, 512 // 4) + 1, jnp.int32)
        fside_BxSxS_0 = -1.52775e-05 + 0.999936 * jax.random.normal(jax.random.fold_in(_rk, 11), (4, 512, 512), jnp.float32)
        cond_512 = -5.03954e-05 + 1.00559 * jax.random.normal(jax.random.fold_in(_rk, 12), (4, 128), jnp.float32)
        return (x, fside_BxSxS_0, cond_512)
    x, fside_BxSxS_0, cond_512 = _rec_inputs()

    def _L0_cond_setup():
        import jax, jax.numpy as jnp
        from jax import lax
        import numpy as np
        B, T, C, TD = (8, 512, 512, 128)

        def _bi_wkv(r, k, v, w, u, time_emb):
            tf = jax.nn.sigmoid(jnp.sum(time_emb, axis=-1))[:, None, None]
            decay = jnp.exp(-jnp.exp(w.astype(jnp.float32)))[None, :] * (0.5 + 0.5 * tf[:, :, 0])
            kf = k.astype(jnp.float32)
            vf = v.astype(jnp.float32)
            ek = jnp.exp(jnp.minimum(kf, 30.0))
            ekv = ek * vf

            def step(carry, x):
                a, b = carry
                ekv_t, ek_t = x
                a = a * decay + ekv_t
                b = b * decay + ek_t
                return ((a, b), (a, b))
            ekv_t = jnp.swapaxes(ekv, 0, 1)
            ek_t = jnp.swapaxes(ek, 0, 1)
            init = (jnp.zeros_like(decay), jnp.zeros_like(decay))
            _, (nf, df) = lax.scan(step, init, (ekv_t, ek_t))
            _, (nb, db) = lax.scan(step, init, (ekv_t, ek_t), reverse=True)
            nf = jnp.swapaxes(nf, 0, 1)
            df = jnp.swapaxes(df, 0, 1)
            nb = jnp.swapaxes(nb, 0, 1)
            db = jnp.swapaxes(db, 0, 1)
            euk = jnp.exp(jnp.minimum(u.astype(jnp.float32)[None, None, :] + kf, 30.0))
            num = nf + nb - ekv + euk * vf
            den = df + db - ek + euk
            base = jax.nn.sigmoid(r.astype(jnp.float32)) * (num / jnp.maximum(den, 1e-08))
            out = base * (0.8 + 0.2 * tf)
            return out.astype(r.dtype)
        key = jax.random.key(seed)
        ks = jax.random.split(key, 6)
        return {'r': jax.random.normal(ks[0], (B, T, C), dtype=jnp.float32), 'k': jax.random.normal(ks[1], (B, T, C), dtype=jnp.float32), 'v': jax.random.normal(ks[2], (B, T, C), dtype=jnp.float32), 'w': jax.random.normal(ks[3], (C,), dtype=jnp.float32), 'u': jax.random.normal(ks[4], (C,), dtype=jnp.float32), 'time_emb': jax.random.normal(ks[5], (B, TD), dtype=jnp.float32)}
    _L0_cond_all = _L0_cond_setup()
    _L0_cond_in = {k: v for k, v in _L0_cond_all.items() if k in ('w', 'u')}
    del _L0_cond_all

    def _L0_attn_setup():
        import jax, jax.numpy as jnp
        import numpy as np
        H = 16
        HD = 128
        BS = 64
        SEL = 8
        WIN = 64
        BASE = 10000.0

        def _rope(t):
            n, hd = (t.shape[1], t.shape[-1])
            half = hd // 2
            inv = 1.0 / BASE ** (jnp.arange(half, dtype=jnp.float32) / half)
            th = jnp.arange(n, dtype=jnp.float32)[:, None] * inv[None, :]
            cos = jnp.cos(th)[None, :, None, :]
            sin = jnp.sin(th)[None, :, None, :]
            t1, t2 = (t[..., :half], t[..., half:])
            return jnp.concatenate([t1 * cos - t2 * sin, t1 * sin + t2 * cos], axis=-1)

        def _nsa_forward(x, Wq, Wk, Wv, Wg, Wo):
            b, n, d = x.shape
            nb = n // BS
            scale = HD ** (-0.5)
            q = (x @ Wq).reshape(b, n, H, HD)
            k = (x @ Wk).reshape(b, n, H, HD)
            v = (x @ Wv).reshape(b, n, H, HD)
            g = jax.nn.sigmoid(x @ Wg)
            g_cmp, g_slc, g_swa = jnp.split(g, 3, axis=-1)
            q = _rope(q)
            k = _rope(k)
            idx = jnp.arange(n)
            k_cmp = k.reshape(b, nb, BS, H, HD).mean(axis=2)
            v_cmp = v.reshape(b, nb, BS, H, HD).mean(axis=2)
            s_cmp = jnp.einsum('bnhd,bmhd->bhnm', q, k_cmp) * scale
            blk_end = (jnp.arange(nb) + 1) * BS - 1
            cmp_mask = idx[:, None] >= blk_end[None, :]
            p_cmp = jax.nn.softmax(jnp.where(cmp_mask[None, None], s_cmp, -1e+30), axis=-1)
            p_cmp = p_cmp * cmp_mask.any(-1)[None, None, :, None]
            o_cmp = jnp.einsum('bhnm,bmhd->bnhd', p_cmp, v_cmp)
            cur_blk = jax.nn.one_hot(idx // BS, nb, dtype=jnp.float32)
            imp = p_cmp + 2.0 * cur_blk[None, None]
            sel = jax.lax.top_k(imp, SEL)[1]
            blk_sel = jax.nn.one_hot(sel, nb).sum(-2) > 0
            causal = idx[:, None] >= idx[None, :]
            slc_mask = blk_sel[..., idx // BS] & causal[None, None]
            s_full = jnp.einsum('bnhd,bmhd->bhnm', q, k) * scale
            p_slc = jax.nn.softmax(jnp.where(slc_mask, s_full, -1e+30), axis=-1)
            o_slc = jnp.einsum('bhnm,bmhd->bnhd', p_slc, v)
            swa_mask = causal & (idx[:, None] - idx[None, :] <= WIN)
            p_swa = jax.nn.softmax(jnp.where(swa_mask[None, None], s_full, -1e+30), axis=-1)
            o_swa = jnp.einsum('bhnm,bmhd->bnhd', p_swa, v)
            o = o_cmp * g_cmp[..., None] + o_slc * g_slc[..., None] + o_swa * g_swa[..., None]
            return o.reshape(b, n, H * HD) @ Wo
        key = jax.random.key(seed)
        ks = jax.random.split(key, 6)
        B, N, D = (2, 256, 512)
        std = 0.02
        return {'x': jax.random.normal(ks[0], (B, N, D), jnp.float32), 'Wq': jax.random.normal(ks[1], (D, H * HD), jnp.float32) * std, 'Wk': jax.random.normal(ks[2], (D, H * HD), jnp.float32) * std, 'Wv': jax.random.normal(ks[3], (D, H * HD), jnp.float32) * std, 'Wg': jax.random.normal(ks[4], (D, 3 * H), jnp.float32) * std, 'Wo': jax.random.normal(ks[5], (H * HD, D), jnp.float32) * std}
    _L0_attn_all = _L0_attn_setup()
    _L0_attn_in = {k: v for k, v in _L0_attn_all.items() if k in ('Wq', 'Wk', 'Wv', 'Wg', 'Wo')}
    del _L0_attn_all

    def _L0_cond2_setup():
        import jax, jax.numpy as jnp
        from jax import lax
        import numpy as np
        B, T, C, TD = (8, 512, 512, 128)

        def _bi_wkv(r, k, v, w, u, time_emb):
            tf = jax.nn.sigmoid(jnp.sum(time_emb, axis=-1))[:, None, None]
            decay = jnp.exp(-jnp.exp(w.astype(jnp.float32)))[None, :] * (0.5 + 0.5 * tf[:, :, 0])
            kf = k.astype(jnp.float32)
            vf = v.astype(jnp.float32)
            ek = jnp.exp(jnp.minimum(kf, 30.0))
            ekv = ek * vf

            def step(carry, x):
                a, b = carry
                ekv_t, ek_t = x
                a = a * decay + ekv_t
                b = b * decay + ek_t
                return ((a, b), (a, b))
            ekv_t = jnp.swapaxes(ekv, 0, 1)
            ek_t = jnp.swapaxes(ek, 0, 1)
            init = (jnp.zeros_like(decay), jnp.zeros_like(decay))
            _, (nf, df) = lax.scan(step, init, (ekv_t, ek_t))
            _, (nb, db) = lax.scan(step, init, (ekv_t, ek_t), reverse=True)
            nf = jnp.swapaxes(nf, 0, 1)
            df = jnp.swapaxes(df, 0, 1)
            nb = jnp.swapaxes(nb, 0, 1)
            db = jnp.swapaxes(db, 0, 1)
            euk = jnp.exp(jnp.minimum(u.astype(jnp.float32)[None, None, :] + kf, 30.0))
            num = nf + nb - ekv + euk * vf
            den = df + db - ek + euk
            base = jax.nn.sigmoid(r.astype(jnp.float32)) * (num / jnp.maximum(den, 1e-08))
            out = base * (0.8 + 0.2 * tf)
            return out.astype(r.dtype)
        key = jax.random.key(seed)
        ks = jax.random.split(key, 6)
        return {'r': jax.random.normal(ks[0], (B, T, C), dtype=jnp.float32), 'k': jax.random.normal(ks[1], (B, T, C), dtype=jnp.float32), 'v': jax.random.normal(ks[2], (B, T, C), dtype=jnp.float32), 'w': jax.random.normal(ks[3], (C,), dtype=jnp.float32), 'u': jax.random.normal(ks[4], (C,), dtype=jnp.float32), 'time_emb': jax.random.normal(ks[5], (B, TD), dtype=jnp.float32)}
    _L0_cond2_all = _L0_cond2_setup()
    _L0_cond2_in = {k: v for k, v in _L0_cond2_all.items() if k in ('w', 'u')}
    del _L0_cond2_all

    def _L0_ffn_setup():
        import jax, jax.numpy as jnp
        import numpy as np
        B, S, H, I, E = (2, 512, 512, 352, 8)
        TOP_K = 2
        key = jax.random.key(seed)
        k0, k1, k2, k3, k4 = jax.random.split(key, 5)
        scale = float(np.sqrt(2.0 / (H + I)))
        return {'hidden_states': jax.random.normal(k0, (B, S, H), dtype=jnp.float32), 'router_w': jax.random.normal(k1, (E, H), dtype=jnp.float32) * H ** (-0.5), 'gate_w': jax.random.normal(k2, (E, I, H), dtype=jnp.float32) * scale, 'up_w': jax.random.normal(k3, (E, I, H), dtype=jnp.float32) * scale, 'down_w': jax.random.normal(k4, (E, H, I), dtype=jnp.float32) * scale}
    _L0_ffn_all = _L0_ffn_setup()
    _L0_ffn_in = {k: v for k, v in _L0_ffn_all.items() if k in ('router_w', 'gate_w', 'up_w', 'down_w')}
    del _L0_ffn_all

    def _L1_cond_setup():
        import jax, jax.numpy as jnp
        from jax import lax
        import numpy as np
        B, T, C, TD = (8, 512, 512, 128)

        def _bi_wkv(r, k, v, w, u, time_emb):
            tf = jax.nn.sigmoid(jnp.sum(time_emb, axis=-1))[:, None, None]
            decay = jnp.exp(-jnp.exp(w.astype(jnp.float32)))[None, :] * (0.5 + 0.5 * tf[:, :, 0])
            kf = k.astype(jnp.float32)
            vf = v.astype(jnp.float32)
            ek = jnp.exp(jnp.minimum(kf, 30.0))
            ekv = ek * vf

            def step(carry, x):
                a, b = carry
                ekv_t, ek_t = x
                a = a * decay + ekv_t
                b = b * decay + ek_t
                return ((a, b), (a, b))
            ekv_t = jnp.swapaxes(ekv, 0, 1)
            ek_t = jnp.swapaxes(ek, 0, 1)
            init = (jnp.zeros_like(decay), jnp.zeros_like(decay))
            _, (nf, df) = lax.scan(step, init, (ekv_t, ek_t))
            _, (nb, db) = lax.scan(step, init, (ekv_t, ek_t), reverse=True)
            nf = jnp.swapaxes(nf, 0, 1)
            df = jnp.swapaxes(df, 0, 1)
            nb = jnp.swapaxes(nb, 0, 1)
            db = jnp.swapaxes(db, 0, 1)
            euk = jnp.exp(jnp.minimum(u.astype(jnp.float32)[None, None, :] + kf, 30.0))
            num = nf + nb - ekv + euk * vf
            den = df + db - ek + euk
            base = jax.nn.sigmoid(r.astype(jnp.float32)) * (num / jnp.maximum(den, 1e-08))
            out = base * (0.8 + 0.2 * tf)
            return out.astype(r.dtype)
        key = jax.random.key(seed)
        ks = jax.random.split(key, 6)
        return {'r': jax.random.normal(ks[0], (B, T, C), dtype=jnp.float32), 'k': jax.random.normal(ks[1], (B, T, C), dtype=jnp.float32), 'v': jax.random.normal(ks[2], (B, T, C), dtype=jnp.float32), 'w': jax.random.normal(ks[3], (C,), dtype=jnp.float32), 'u': jax.random.normal(ks[4], (C,), dtype=jnp.float32), 'time_emb': jax.random.normal(ks[5], (B, TD), dtype=jnp.float32)}
    _L1_cond_all = _L1_cond_setup()
    _L1_cond_in = {k: v for k, v in _L1_cond_all.items() if k in ('w', 'u')}
    del _L1_cond_all

    def _L1_attn_setup():
        import jax, jax.numpy as jnp
        import numpy as np
        B, T, C = (4, 512, 512)
        N_HEAD = 16
        HEAD_DIM = C // N_HEAD
        key = jax.random.key(seed)
        k1, k2, k3, k4, k5 = jax.random.split(key, 5)
        s = 1.0 / np.sqrt(C)
        return {'x': jax.random.normal(k1, (B, T, C), dtype=jnp.float32), 'w_attn': jax.random.normal(k2, (C, 3 * C), dtype=jnp.float32) * s, 'b_attn': jax.random.normal(k3, (3 * C,), dtype=jnp.float32) * 0.02, 'w_proj': jax.random.normal(k4, (C, C), dtype=jnp.float32) * s, 'b_proj': jax.random.normal(k5, (C,), dtype=jnp.float32) * 0.02}
    _L1_attn_all = _L1_attn_setup()
    _L1_attn_in = {k: v for k, v in _L1_attn_all.items() if k in ('w_attn', 'b_attn', 'w_proj', 'b_proj')}
    del _L1_attn_all

    def _L1_cond2_setup():
        import jax, jax.numpy as jnp
        from jax import lax
        import numpy as np
        B, T, C, TD = (8, 512, 512, 128)

        def _bi_wkv(r, k, v, w, u, time_emb):
            tf = jax.nn.sigmoid(jnp.sum(time_emb, axis=-1))[:, None, None]
            decay = jnp.exp(-jnp.exp(w.astype(jnp.float32)))[None, :] * (0.5 + 0.5 * tf[:, :, 0])
            kf = k.astype(jnp.float32)
            vf = v.astype(jnp.float32)
            ek = jnp.exp(jnp.minimum(kf, 30.0))
            ekv = ek * vf

            def step(carry, x):
                a, b = carry
                ekv_t, ek_t = x
                a = a * decay + ekv_t
                b = b * decay + ek_t
                return ((a, b), (a, b))
            ekv_t = jnp.swapaxes(ekv, 0, 1)
            ek_t = jnp.swapaxes(ek, 0, 1)
            init = (jnp.zeros_like(decay), jnp.zeros_like(decay))
            _, (nf, df) = lax.scan(step, init, (ekv_t, ek_t))
            _, (nb, db) = lax.scan(step, init, (ekv_t, ek_t), reverse=True)
            nf = jnp.swapaxes(nf, 0, 1)
            df = jnp.swapaxes(df, 0, 1)
            nb = jnp.swapaxes(nb, 0, 1)
            db = jnp.swapaxes(db, 0, 1)
            euk = jnp.exp(jnp.minimum(u.astype(jnp.float32)[None, None, :] + kf, 30.0))
            num = nf + nb - ekv + euk * vf
            den = df + db - ek + euk
            base = jax.nn.sigmoid(r.astype(jnp.float32)) * (num / jnp.maximum(den, 1e-08))
            out = base * (0.8 + 0.2 * tf)
            return out.astype(r.dtype)
        key = jax.random.key(seed)
        ks = jax.random.split(key, 6)
        return {'r': jax.random.normal(ks[0], (B, T, C), dtype=jnp.float32), 'k': jax.random.normal(ks[1], (B, T, C), dtype=jnp.float32), 'v': jax.random.normal(ks[2], (B, T, C), dtype=jnp.float32), 'w': jax.random.normal(ks[3], (C,), dtype=jnp.float32), 'u': jax.random.normal(ks[4], (C,), dtype=jnp.float32), 'time_emb': jax.random.normal(ks[5], (B, TD), dtype=jnp.float32)}
    _L1_cond2_all = _L1_cond2_setup()
    _L1_cond2_in = {k: v for k, v in _L1_cond2_all.items() if k in ('w', 'u')}
    del _L1_cond2_all

    def _L1_ffn_setup():
        import jax, jax.numpy as jnp
        import numpy as np
        key = jax.random.key(seed)
        k1, k2, k3, k4, k5 = jax.random.split(key, 5)
        B, L, H, N = (2, 512, 512, 2048)
        x = jax.random.normal(k1, (B, L, H), dtype=jnp.float32)
        W0 = jax.random.normal(k2, (N, H), dtype=jnp.float32) * (1.0 / np.sqrt(H))
        bias0 = jax.random.normal(k3, (N,), dtype=jnp.float32) * 0.02
        W1 = jax.random.normal(k4, (H, N), dtype=jnp.float32) * (1.0 / np.sqrt(N))
        bias1 = jax.random.normal(k5, (H,), dtype=jnp.float32) * 0.02
        return {'x': x, 'W0': W0, 'bias0': bias0, 'W1': W1, 'bias1': bias1}
    _L1_ffn_all = _L1_ffn_setup()
    _L1_ffn_in = {k: v for k, v in _L1_ffn_all.items() if k in ('W0', 'bias0', 'W1', 'bias1')}
    del _L1_ffn_all
    return {'x': x, 'fside_BxSxS_0': fside_BxSxS_0, 'cond_512': cond_512, 'L0_cond_w': _L0_cond_in['w'], 'L0_cond_u': _L0_cond_in['u'], 'L0_attn_Wq': _L0_attn_in['Wq'], 'L0_attn_Wk': _L0_attn_in['Wk'], 'L0_attn_Wv': _L0_attn_in['Wv'], 'L0_attn_Wg': _L0_attn_in['Wg'], 'L0_attn_Wo': _L0_attn_in['Wo'], 'L0_cond2_w': _L0_cond2_in['w'], 'L0_cond2_u': _L0_cond2_in['u'], 'L0_ffn_router_w': _L0_ffn_in['router_w'], 'L0_ffn_gate_w': _L0_ffn_in['gate_w'], 'L0_ffn_up_w': _L0_ffn_in['up_w'], 'L0_ffn_down_w': _L0_ffn_in['down_w'], 'L1_cond_w': _L1_cond_in['w'], 'L1_cond_u': _L1_cond_in['u'], 'L1_attn_w_attn': _L1_attn_in['w_attn'], 'L1_attn_b_attn': _L1_attn_in['b_attn'], 'L1_attn_w_proj': _L1_attn_in['w_proj'], 'L1_attn_b_proj': _L1_attn_in['b_proj'], 'L1_cond2_w': _L1_cond2_in['w'], 'L1_cond2_u': _L1_cond2_in['u'], 'L1_ffn_W0': _L1_ffn_in['W0'], 'L1_ffn_bias0': _L1_ffn_in['bias0'], 'L1_ffn_W1': _L1_ffn_in['W1'], 'L1_ffn_bias1': _L1_ffn_in['bias1']}

def reference(x, fside_BxSxS_0, cond_512, L0_cond_w, L0_cond_u, L0_attn_Wq, L0_attn_Wk, L0_attn_Wv, L0_attn_Wg, L0_attn_Wo, L0_cond2_w, L0_cond2_u, L0_ffn_router_w, L0_ffn_gate_w, L0_ffn_up_w, L0_ffn_down_w, L1_cond_w, L1_cond_u, L1_attn_w_attn, L1_attn_b_attn, L1_attn_w_proj, L1_attn_b_proj, L1_cond2_w, L1_cond2_u, L1_ffn_W0, L1_ffn_bias0, L1_ffn_W1, L1_ffn_bias1):
    import jax
    import jax.numpy as jnp

    def _L0_cond_ref(r, k, v, w, u, time_emb):
        import jax, jax.numpy as jnp
        from jax import lax
        import numpy as np
        B, T, C, TD = (8, 512, 512, 128)

        def _bi_wkv(r, k, v, w, u, time_emb):
            tf = jax.nn.sigmoid(jnp.sum(time_emb, axis=-1))[:, None, None]
            decay = jnp.exp(-jnp.exp(w.astype(jnp.float32)))[None, :] * (0.5 + 0.5 * tf[:, :, 0])
            kf = k.astype(jnp.float32)
            vf = v.astype(jnp.float32)
            ek = jnp.exp(jnp.minimum(kf, 30.0))
            ekv = ek * vf

            def step(carry, x):
                a, b = carry
                ekv_t, ek_t = x
                a = a * decay + ekv_t
                b = b * decay + ek_t
                return ((a, b), (a, b))
            ekv_t = jnp.swapaxes(ekv, 0, 1)
            ek_t = jnp.swapaxes(ek, 0, 1)
            init = (jnp.zeros_like(decay), jnp.zeros_like(decay))
            _, (nf, df) = lax.scan(step, init, (ekv_t, ek_t))
            _, (nb, db) = lax.scan(step, init, (ekv_t, ek_t), reverse=True)
            nf = jnp.swapaxes(nf, 0, 1)
            df = jnp.swapaxes(df, 0, 1)
            nb = jnp.swapaxes(nb, 0, 1)
            db = jnp.swapaxes(db, 0, 1)
            euk = jnp.exp(jnp.minimum(u.astype(jnp.float32)[None, None, :] + kf, 30.0))
            num = nf + nb - ekv + euk * vf
            den = df + db - ek + euk
            base = jax.nn.sigmoid(r.astype(jnp.float32)) * (num / jnp.maximum(den, 1e-08))
            out = base * (0.8 + 0.2 * tf)
            return out.astype(r.dtype)
        return _bi_wkv(r, k, v, w, u, time_emb)

    def _L0_attn_ref(x, Wq, Wk, Wv, Wg, Wo):
        import jax, jax.numpy as jnp
        import numpy as np
        H = 16
        HD = 128
        BS = 64
        SEL = 8
        WIN = 64
        BASE = 10000.0

        def _rope(t):
            n, hd = (t.shape[1], t.shape[-1])
            half = hd // 2
            inv = 1.0 / BASE ** (jnp.arange(half, dtype=jnp.float32) / half)
            th = jnp.arange(n, dtype=jnp.float32)[:, None] * inv[None, :]
            cos = jnp.cos(th)[None, :, None, :]
            sin = jnp.sin(th)[None, :, None, :]
            t1, t2 = (t[..., :half], t[..., half:])
            return jnp.concatenate([t1 * cos - t2 * sin, t1 * sin + t2 * cos], axis=-1)

        def _nsa_forward(x, Wq, Wk, Wv, Wg, Wo):
            b, n, d = x.shape
            nb = n // BS
            scale = HD ** (-0.5)
            q = (x @ Wq).reshape(b, n, H, HD)
            k = (x @ Wk).reshape(b, n, H, HD)
            v = (x @ Wv).reshape(b, n, H, HD)
            g = jax.nn.sigmoid(x @ Wg)
            g_cmp, g_slc, g_swa = jnp.split(g, 3, axis=-1)
            q = _rope(q)
            k = _rope(k)
            idx = jnp.arange(n)
            k_cmp = k.reshape(b, nb, BS, H, HD).mean(axis=2)
            v_cmp = v.reshape(b, nb, BS, H, HD).mean(axis=2)
            s_cmp = jnp.einsum('bnhd,bmhd->bhnm', q, k_cmp) * scale
            blk_end = (jnp.arange(nb) + 1) * BS - 1
            cmp_mask = idx[:, None] >= blk_end[None, :]
            p_cmp = jax.nn.softmax(jnp.where(cmp_mask[None, None], s_cmp, -1e+30), axis=-1)
            p_cmp = p_cmp * cmp_mask.any(-1)[None, None, :, None]
            o_cmp = jnp.einsum('bhnm,bmhd->bnhd', p_cmp, v_cmp)
            cur_blk = jax.nn.one_hot(idx // BS, nb, dtype=jnp.float32)
            imp = p_cmp + 2.0 * cur_blk[None, None]
            sel = jax.lax.top_k(imp, SEL)[1]
            blk_sel = jax.nn.one_hot(sel, nb).sum(-2) > 0
            causal = idx[:, None] >= idx[None, :]
            slc_mask = blk_sel[..., idx // BS] & causal[None, None]
            s_full = jnp.einsum('bnhd,bmhd->bhnm', q, k) * scale
            p_slc = jax.nn.softmax(jnp.where(slc_mask, s_full, -1e+30), axis=-1)
            o_slc = jnp.einsum('bhnm,bmhd->bnhd', p_slc, v)
            swa_mask = causal & (idx[:, None] - idx[None, :] <= WIN)
            p_swa = jax.nn.softmax(jnp.where(swa_mask[None, None], s_full, -1e+30), axis=-1)
            o_swa = jnp.einsum('bhnm,bmhd->bnhd', p_swa, v)
            o = o_cmp * g_cmp[..., None] + o_slc * g_slc[..., None] + o_swa * g_swa[..., None]
            return o.reshape(b, n, H * HD) @ Wo
        return _nsa_forward(x, Wq, Wk, Wv, Wg, Wo)

    def _L0_cond2_ref(r, k, v, w, u, time_emb):
        import jax, jax.numpy as jnp
        from jax import lax
        import numpy as np
        B, T, C, TD = (8, 512, 512, 128)

        def _bi_wkv(r, k, v, w, u, time_emb):
            tf = jax.nn.sigmoid(jnp.sum(time_emb, axis=-1))[:, None, None]
            decay = jnp.exp(-jnp.exp(w.astype(jnp.float32)))[None, :] * (0.5 + 0.5 * tf[:, :, 0])
            kf = k.astype(jnp.float32)
            vf = v.astype(jnp.float32)
            ek = jnp.exp(jnp.minimum(kf, 30.0))
            ekv = ek * vf

            def step(carry, x):
                a, b = carry
                ekv_t, ek_t = x
                a = a * decay + ekv_t
                b = b * decay + ek_t
                return ((a, b), (a, b))
            ekv_t = jnp.swapaxes(ekv, 0, 1)
            ek_t = jnp.swapaxes(ek, 0, 1)
            init = (jnp.zeros_like(decay), jnp.zeros_like(decay))
            _, (nf, df) = lax.scan(step, init, (ekv_t, ek_t))
            _, (nb, db) = lax.scan(step, init, (ekv_t, ek_t), reverse=True)
            nf = jnp.swapaxes(nf, 0, 1)
            df = jnp.swapaxes(df, 0, 1)
            nb = jnp.swapaxes(nb, 0, 1)
            db = jnp.swapaxes(db, 0, 1)
            euk = jnp.exp(jnp.minimum(u.astype(jnp.float32)[None, None, :] + kf, 30.0))
            num = nf + nb - ekv + euk * vf
            den = df + db - ek + euk
            base = jax.nn.sigmoid(r.astype(jnp.float32)) * (num / jnp.maximum(den, 1e-08))
            out = base * (0.8 + 0.2 * tf)
            return out.astype(r.dtype)
        return _bi_wkv(r, k, v, w, u, time_emb)

    def _L0_ffn_ref(hidden_states, router_w, gate_w, up_w, down_w):
        import jax, jax.numpy as jnp
        import numpy as np
        B, S, H, I, E = (2, 512, 512, 352, 8)
        TOP_K = 2
        b, s, h = hidden_states.shape
        e = router_w.shape[0]
        x = hidden_states.reshape(-1, h)
        logits = jnp.einsum('th,eh->te', x, router_w)
        top_vals, top_idx = jax.lax.top_k(logits, TOP_K)
        top_w = jax.nn.softmax(top_vals, axis=-1)
        expert = top_idx[:, 0]
        weight = top_w[:, 0]
        gate = jnp.einsum('th,eih->eti', x, gate_w)
        up = jnp.einsum('th,eih->eti', x, up_w)
        act = jax.nn.silu(gate) * up
        out_e = jnp.einsum('eti,ehi->eth', act, down_w)
        combine = jax.nn.one_hot(expert, e, dtype=x.dtype) * weight[:, None]
        out = jnp.einsum('eth,te->th', out_e, combine)
        return out.reshape(b, s, h)

    def _L1_cond_ref(r, k, v, w, u, time_emb):
        import jax, jax.numpy as jnp
        from jax import lax
        import numpy as np
        B, T, C, TD = (8, 512, 512, 128)

        def _bi_wkv(r, k, v, w, u, time_emb):
            tf = jax.nn.sigmoid(jnp.sum(time_emb, axis=-1))[:, None, None]
            decay = jnp.exp(-jnp.exp(w.astype(jnp.float32)))[None, :] * (0.5 + 0.5 * tf[:, :, 0])
            kf = k.astype(jnp.float32)
            vf = v.astype(jnp.float32)
            ek = jnp.exp(jnp.minimum(kf, 30.0))
            ekv = ek * vf

            def step(carry, x):
                a, b = carry
                ekv_t, ek_t = x
                a = a * decay + ekv_t
                b = b * decay + ek_t
                return ((a, b), (a, b))
            ekv_t = jnp.swapaxes(ekv, 0, 1)
            ek_t = jnp.swapaxes(ek, 0, 1)
            init = (jnp.zeros_like(decay), jnp.zeros_like(decay))
            _, (nf, df) = lax.scan(step, init, (ekv_t, ek_t))
            _, (nb, db) = lax.scan(step, init, (ekv_t, ek_t), reverse=True)
            nf = jnp.swapaxes(nf, 0, 1)
            df = jnp.swapaxes(df, 0, 1)
            nb = jnp.swapaxes(nb, 0, 1)
            db = jnp.swapaxes(db, 0, 1)
            euk = jnp.exp(jnp.minimum(u.astype(jnp.float32)[None, None, :] + kf, 30.0))
            num = nf + nb - ekv + euk * vf
            den = df + db - ek + euk
            base = jax.nn.sigmoid(r.astype(jnp.float32)) * (num / jnp.maximum(den, 1e-08))
            out = base * (0.8 + 0.2 * tf)
            return out.astype(r.dtype)
        return _bi_wkv(r, k, v, w, u, time_emb)

    def _L1_attn_ref(x, w_attn, b_attn, w_proj, b_proj):
        import jax, jax.numpy as jnp
        import numpy as np
        B, T, C = (4, 512, 512)
        N_HEAD = 16
        HEAD_DIM = C // N_HEAD
        Bsz, Tlen, Cdim = x.shape
        qkv = x @ w_attn + b_attn
        q, k, v = jnp.split(qkv, 3, axis=-1)

        def heads(t):
            return t.reshape(Bsz, Tlen, N_HEAD, HEAD_DIM).transpose(0, 2, 1, 3)
        q, k, v = (heads(q), heads(k), heads(v))
        scale = 1.0 / np.sqrt(HEAD_DIM).astype(np.float32)
        att = jnp.einsum('bhqd,bhkd->bhqk', q, k) * scale
        causal = jnp.tril(jnp.ones((Tlen, Tlen), dtype=bool))
        att = jnp.where(causal, att, -jnp.inf)
        att = jax.nn.softmax(att, axis=-1)
        y = jnp.einsum('bhqk,bhkd->bhqd', att, v)
        y = y.transpose(0, 2, 1, 3).reshape(Bsz, Tlen, Cdim)
        return y @ w_proj + b_proj

    def _L1_cond2_ref(r, k, v, w, u, time_emb):
        import jax, jax.numpy as jnp
        from jax import lax
        import numpy as np
        B, T, C, TD = (8, 512, 512, 128)

        def _bi_wkv(r, k, v, w, u, time_emb):
            tf = jax.nn.sigmoid(jnp.sum(time_emb, axis=-1))[:, None, None]
            decay = jnp.exp(-jnp.exp(w.astype(jnp.float32)))[None, :] * (0.5 + 0.5 * tf[:, :, 0])
            kf = k.astype(jnp.float32)
            vf = v.astype(jnp.float32)
            ek = jnp.exp(jnp.minimum(kf, 30.0))
            ekv = ek * vf

            def step(carry, x):
                a, b = carry
                ekv_t, ek_t = x
                a = a * decay + ekv_t
                b = b * decay + ek_t
                return ((a, b), (a, b))
            ekv_t = jnp.swapaxes(ekv, 0, 1)
            ek_t = jnp.swapaxes(ek, 0, 1)
            init = (jnp.zeros_like(decay), jnp.zeros_like(decay))
            _, (nf, df) = lax.scan(step, init, (ekv_t, ek_t))
            _, (nb, db) = lax.scan(step, init, (ekv_t, ek_t), reverse=True)
            nf = jnp.swapaxes(nf, 0, 1)
            df = jnp.swapaxes(df, 0, 1)
            nb = jnp.swapaxes(nb, 0, 1)
            db = jnp.swapaxes(db, 0, 1)
            euk = jnp.exp(jnp.minimum(u.astype(jnp.float32)[None, None, :] + kf, 30.0))
            num = nf + nb - ekv + euk * vf
            den = df + db - ek + euk
            base = jax.nn.sigmoid(r.astype(jnp.float32)) * (num / jnp.maximum(den, 1e-08))
            out = base * (0.8 + 0.2 * tf)
            return out.astype(r.dtype)
        return _bi_wkv(r, k, v, w, u, time_emb)

    def _L1_ffn_ref(x, W0, bias0, W1, bias1):
        import jax, jax.numpy as jnp
        import numpy as np
        B, L, H = x.shape
        X = x.reshape(-1, H).astype(jnp.float16)
        D = jnp.dot(X.astype(jnp.float32), W0.T) + bias0
        D = jax.nn.gelu(D, approximate=False).astype(jnp.float16)
        E = jnp.dot(D.astype(jnp.float32), W1.T) + bias1
        return E.astype(jnp.float16).reshape(B, L, H)
    x = x + _L0_attn_ref(_L0_cond_ref(x, fside_BxSxS_0, fside_BxSxS_0, L0_cond_w, L0_cond_u, cond_512), L0_attn_Wq, L0_attn_Wk, L0_attn_Wv, L0_attn_Wg, L0_attn_Wo)
    x = x + _L0_ffn_ref(_L0_cond2_ref(x, fside_BxSxS_0, fside_BxSxS_0, L0_cond2_w, L0_cond2_u, cond_512), L0_ffn_router_w, L0_ffn_gate_w, L0_ffn_up_w, L0_ffn_down_w)
    x = x + _L1_attn_ref(_L1_cond_ref(x, fside_BxSxS_0, fside_BxSxS_0, L1_cond_w, L1_cond_u, cond_512), L1_attn_w_attn, L1_attn_b_attn, L1_attn_w_proj, L1_attn_b_proj)
    x = x + _L1_ffn_ref(_L1_cond2_ref(x, fside_BxSxS_0, fside_BxSxS_0, L1_cond2_w, L1_cond2_u, cond_512), L1_ffn_W0, L1_ffn_bias0, L1_ffn_W1, L1_ffn_bias1)
    return x

_drawn_inputs = setup_inputs


def setup_inputs(seed=0):
    import zlib

    import numpy as np

    out = dict(_drawn_inputs(seed))
    spreads = {}
    factors = {'L0_cond_u': 3.058,
     'L0_attn_Wq': 8.0,
     'L0_attn_Wk': 8.0,
     'L0_attn_Wg': 5.952,
     'L1_attn_b_attn': 3.079,
     'L1_attn_b_proj': 3.131,
     'L1_ffn_bias0': 5.096,
     'L1_ffn_bias1': 3.15}
    for name, (base, spread) in spreads.items():
        noise = np.random.default_rng([zlib.crc32(name.encode()), seed]).standard_normal(out[name].shape)
        drawn = base * np.exp(spread * noise) if base else spread * noise
        out[name] = jnp.asarray(drawn.astype(out[name].dtype))
    for name, factor in factors.items():
        out[name] = (out[name] * factor).astype(out[name].dtype)
    return out
```

```python
from contextlib import ExitStack

import numpy as np

import concourse.bass as bass
from concourse import mybir

ALU = mybir.AluOpType
ACT = mybir.ActivationFunctionType
AX = mybir.AxisListType.X
F32 = mybir.dt.float32
F16 = mybir.dt.float16
BF16 = mybir.dt.bfloat16
I32 = mybir.dt.int32

P = 128
B, T, C = 4, 512, 512
CC = C // P
TT = T // P
LAYERS = 4
NEG = -1e30
EXP30 = float(np.exp(30.0))

H0, D0 = 16, 128
NBLK, BLK = 8, 64
WIN = 64
H1, D1 = 16, 32
HPC = P // D1
E, I = 8, 352
KI = (I + P - 1) // P
NT = B * TT
SLOT_TILES = NT + E - 1
F = 2048
NF = F // P
WSCALE = 64.0


class Tally:

    def __init__(self, sem, start=0):
        self.sem, self.n, self.base = sem, start, 0

    def inc(self, instruction):
        instruction.then_inc(self.sem, 1)
        self.n += 1
        return self.n


def score_columns(j):
    return {3: (0, 0), 2: (1, 0), 0: (1, 384), 1: (2, 0)}[j]


BANK_TILES = ((0, (3,)), (1, (2, 0)), (2, (1,)))


def turned_columns(m):
    return {0: (0, 0), 1: (1, 0), 3: (1, 384), 2: (2, 0)}[m]


class Core:

    def __init__(self, nc, ctx, dram):
        self.nc, self.ctx, self.d = nc, ctx, dram

    def sem(self, name):
        return self.ctx.enter_context(self.nc.semaphore(name))

    def scratch(self, name, shape):
        return self.nc.dram_tensor(name, shape, F32).ap()


def constants(k):
    nc, ctx = k.nc, k.ctx
    k.ident = ctx.enter_context(nc.sbuf_tensor("ident", [P, P], F32))
    k.ident_b = ctx.enter_context(nc.sbuf_tensor("ident_b", [P, P], BF16))
    k.causal_b = ctx.enter_context(nc.sbuf_tensor("causal_b", [P, P], BF16))
    k.slot = ctx.enter_context(nc.sbuf_tensor("slot", [P, NT], I32))
    k.weight = ctx.enter_context(nc.sbuf_tensor("weight", [P, NT], F32))
    k.tile_expert = ctx.enter_context(nc.sbuf_tensor("tile_expert", [P, SLOT_TILES], I32))
    made = k.sem("const_made")
    with nc.Block() as block:

        @block.gpsimd
        def _(pool):
            pool.memset(k.ident[:], 0.0).then_inc(made, 1)
            pool.memset(k.ident_b[:], 0.0).then_inc(made, 1)
            pool.memset(k.causal_b[:], 0.0).then_inc(made, 1)
            pool.wait_ge(made, 3)
            for m in (k.ident, k.ident_b):
                pool.affine_select(out=m[:], in_=m[:], compare_op=ALU.not_equal, fill=1.0, base=0,
                                   pattern=[[-1, P]], channel_multiplier=1).then_inc(made, 1)
            pool.affine_select(out=k.causal_b[:], in_=k.causal_b[:], compare_op=ALU.is_ge, fill=NEG,
                               base=0, pattern=[[-1, P]], channel_multiplier=1).then_inc(made, 1)


def wkv_gain(k):
    nc, d = k.nc, k.d
    UNITS = CC * LAYERS
    with ExitStack() as ctx:
        def sb(n, s, dt=F32):
            return ctx.enter_context(nc.sbuf_tensor("wkv_" + n, s, dt))

        wu = sb("wu", [P, 2, UNITS])
        cond = sb("cond", [P, B, P])
        csum = sb("csum", [P, B])
        tf = sb("tf", [P, B])
        halff = sb("halff", [P, B])
        negf = sb("negf", [P, B])
        ew = sb("ew", [P, UNITS])
        dk = sb("dk", [P, UNITS])
        decay = sb("decay", [P, B, UNITS])
        kt = sb("kt", [P, 2, T])
        ek_raw = sb("ek_raw", [P, T])
        ek = sb("ek", [P, 2, T])
        ekv = sb("ekv", [P, 2, T])
        euk_raw = sb("euk_raw", [P, 2, T])
        euk = sb("euk", [P, 2, T])
        eukv = sb("eukv", [P, 2, T])
        nf = sb("nf", [P, 2, T + 1])
        df = sb("df", [P, 2, T + 1])
        nb = sb("nb", [P, 2, T])
        db = sb("db", [P, 2, T])
        num = sb("num", [P, 2, T])
        den = sb("den", [P, 2, T])
        lnd = sb("lnd", [P, 2, T])
        r0 = sb("r0", [P, 2, T])
        err = sb("err", [P, T])
        r1 = sb("r1", [P, T])
        gain = sb("gain", [P, 2, T])
        s = {n: k.sem("wkv_" + n) for n in (
            "in_loaded", "k_loaded0", "k_loaded1", "dec_step", "exp_w", "decay_ready", "zeroed", "ek_raw", "ek", "ekv", "euk_raw",
            "euk", "eukv", "scan", "part", "joined", "den", "ln", "r0", "newton", "gain",
            "stored0", "stored1")}

        with nc.Block() as block:

            @block.sync
            def _(sp):
                sp.dma_start(wu[:], d["wu"]).then_inc(s["in_loaded"], 16)
                sp.dma_start(cond[:].rearrange("p b n -> p (b n)"),
                             d["cond"].partition_broadcast(P)).then_inc(s["in_loaded"], 16)
                with sp.Fori(0, B) as b:
                    srcs = [d["fT"][bass.ds(b, 1), c].rearrange("a p n -> (a p) n") for c in range(CC)]
                    for c in range(2):
                        sp.dma_start(kt[:, c, :], srcs[c]).then_inc(s[f"k_loaded{c}"], 16)
                    for n in range(UNITS):
                        c, l = divmod(n, LAYERS)
                        dst = d["gain"][l, bass.ds(b, 1), c].rearrange("a p n -> (a p) n")
                        sp.wait_ge(s["gain"], b * UNITS + n + 1)
                        sp.dma_start(dst, gain[:, n % 2, :]).then_inc(s[f"stored{n % 2}"], 16)
                        if l == LAYERS - 1 and c + 2 < CC:
                            sp.dma_start(kt[:, c % 2, :], srcs[c + 2]).then_inc(s[f"k_loaded{c % 2}"], 16)
                for i in range(2):
                    sp.wait_ge(s[f"stored{i}"], 16 + 16 * B * UNITS // 2)

            @block.gpsimd
            def _(pool):
                with pool.Fori(0, B) as b:
                    for n in range(UNITS):
                        c, l = divmod(n, LAYERS)
                        if l == 0:
                            pool.wait_ge(s["ek"], b * CC + c + 1)
                            pool.tensor_tensor(ekv[:, c % 2, :], ek[:, c % 2, :], kt[:, c % 2, :],
                                               ALU.mult).then_inc(s["ekv"], 1)
                        pool.wait_ge(s["euk"], b * UNITS + n + 1)
                        pool.tensor_tensor(eukv[:, n % 2, :], euk[:, n % 2, :], kt[:, c % 2, :],
                                           ALU.mult).then_inc(s["eukv"], 1)
                        pool.wait_ge(s["part"], b * UNITS + n + 1)
                        pool.tensor_tensor(den[:, n % 2, :], den[:, n % 2, :], euk[:, n % 2, :],
                                           ALU.add).then_inc(s["joined"], 1)
                        pool.wait_ge(s["eukv"], b * UNITS + n + 1)
                        pool.tensor_tensor(num[:, n % 2, :], num[:, n % 2, :], eukv[:, n % 2, :],
                                           ALU.add).then_inc(s["joined"], 1)

            @block.scalar
            def _(act):
                act.wait_ge(s["in_loaded"], 32)
                act.activation(ew[:], wu[:, 0, :], ACT.Exp).then_inc(s["exp_w"], 1)
                act.wait_ge(s["exp_w"], 1)
                act.activation(dk[:], ew[:], ACT.Exp, scale=-1.0).then_inc(s["exp_w"], 1)
                act.wait_ge(s["dec_step"], 1)
                act.activation(tf[:], csum[:], ACT.Sigmoid).then_inc(s["exp_w"], 1)
                act.preload_act_table_set("natural_log_exp_and_others")
                with act.Fori(0, B) as b:
                    def exps(n):
                        c, l = divmod(n, LAYERS)
                        if l == 0:
                            act.wait_ge(s[f"k_loaded{c % 2}"], b * 32 + 16 * (c // 2 + 1))
                            if c >= 1:
                                act.wait_ge(s["ek"], b * CC + c)
                            act.activation(ek_raw[:], kt[:, c % 2, :], ACT.Exp).then_inc(s["ek_raw"], 1)
                        if n >= 2:
                            act.wait_ge(s["euk"], b * UNITS + n - 1)
                        act.activation(euk_raw[:, n % 2, :], kt[:, c % 2, :], ACT.Exp,
                                       bias=wu[:, 1, n:n + 1]).then_inc(s["euk_raw"], 1)

                    def invert(n):
                        act.wait_ge(s["den"], b * UNITS + n + 1)
                        if n >= 2:
                            act.wait_ge(s["r0"], b * UNITS + n - 1)
                        act.activation(lnd[:, n % 2, :], den[:, n % 2, :], ACT.Ln).then_inc(s["ln"], 1)
                        act.wait_ge(s["ln"], b * UNITS + n + 1)
                        if n >= 2:
                            act.wait_ge(s["gain"], b * UNITS + n - 1)
                        act.activation(r0[:, n % 2, :], lnd[:, n % 2, :], ACT.Exp, scale=-1.0).then_inc(s["r0"], 1)

                    for n in range(UNITS + 1):
                        if n < UNITS:
                            exps(n)
                        if n >= 1:
                            invert(n - 1)

            @block.vector
            def _(dve):
                for i in range(2):
                    dve.sem_inc(s[f"stored{i}"], 16)
                dve.wait_ge(s["in_loaded"], 32)
                dve.tensor_reduce(csum[:], cond[:], AX, ALU.add).then_inc(s["dec_step"], 1)
                dve.memset(nf[:], 0.0)
                dve.memset(df[:], 0.0).then_inc(s["zeroed"], 1)
                dve.wait_ge(s["exp_w"], 3)
                dve.tensor_scalar(halff[:], tf[:], 0.5, 0.5, ALU.mult, ALU.add).then_inc(s["dec_step"], 1)
                dve.tensor_scalar(negf[:], tf[:], -0.2, -0.8, ALU.mult, ALU.add).then_inc(s["dec_step"], 1)
                dve.wait_ge(s["dec_step"], 3)
                for i in range(B):
                    dve.tensor_scalar(decay[:, i, :], dk[:], halff[:, i:i + 1], None,
                                      ALU.mult).then_inc(s["decay_ready"], 1)
                dve.wait_ge(s["decay_ready"], B)
                dve.wait_ge(s["zeroed"], 1)
                with dve.Fori(0, B) as b:
                    def scans(n):
                        c, l = divmod(n, LAYERS)
                        dec = decay[:, bass.ds(b, 1), n:n + 1].rearrange("p a n -> p (a n)")
                        dect = dec.to_broadcast([P, T])
                        if l == 0:
                            dve.wait_ge(s["ek_raw"], b * CC + c + 1)
                            dve.tensor_scalar(ek[:, c % 2, :], ek_raw[:], EXP30, None, ALU.min).then_inc(s["ek"], 1)
                        dve.wait_ge(s["euk_raw"], b * UNITS + n + 1)
                        if n >= 2:
                            dve.wait_ge(s["joined"], (b * UNITS + n - 1) * 2)
                        dve.tensor_scalar(euk[:, n % 2, :], euk_raw[:, n % 2, :], EXP30, None,
                                          ALU.min).then_inc(s["euk"], 1)
                        if l == 0:
                            dve.wait_ge(s["ek"], b * CC + c + 1)
                            dve.wait_ge(s["ekv"], b * CC + c + 1)
                        for src, fw, bw in ((ek, df, db), (ekv, nf, nb)):
                            dve.tensor_tensor_scan(fw[:, n % 2, 1:T + 1], dect, src[:, c % 2, :], 0.0,
                                                   ALU.mult, ALU.add)
                            dve.tensor_tensor_scan(bw[:, n % 2, ::-1], dect, src[:, c % 2, ::-1], 0.0,
                                                   ALU.mult, ALU.add).then_inc(s["scan"], 1)
                        if n >= 2:
                            dve.wait_ge(s["gain"], b * UNITS + n - 1)
                        for step, (out, fw, bw) in enumerate(((den, df, db), (num, nf, nb))):
                            dve.wait_ge(s["scan"], (b * UNITS + n) * 2 + 1 + step)
                            i = dve.scalar_tensor_tensor(out=out[:, n % 2, :], in0=fw[:, n % 2, 0:T], scalar=dec,
                                                         in1=bw[:, n % 2, :], op0=ALU.mult, op1=ALU.add)
                        i.then_inc(s["part"], 1)

                    def guard(n):
                        dve.wait_ge(s["joined"], (b * UNITS + n) * 2 + 2)
                        dve.tensor_scalar(den[:, n % 2, :], den[:, n % 2, :], 1e-8, None,
                                          ALU.max).then_inc(s["den"], 1)

                    def finish(n):
                        dve.wait_ge(s["r0"], b * UNITS + n + 1)
                        dve.tensor_tensor(err[:], den[:, n % 2, :], r0[:, n % 2, :], ALU.mult).then_inc(s["newton"], 1)
                        dve.wait_ge(s["newton"], (b * UNITS + n) * 2 + 1)
                        if n >= 1:
                            dve.wait_ge(s["gain"], b * UNITS + n)
                        dve.scalar_tensor_tensor(out=r1[:], in0=err[:], scalar=-2.0, in1=r0[:, n % 2, :],
                                                 op0=ALU.add, op1=ALU.mult).then_inc(s["newton"], 1)
                        dve.wait_ge(s["newton"], (b * UNITS + n) * 2 + 2)
                        dve.wait_ge(s[f"stored{n % 2}"], b * (8 * UNITS) + 16 * (n // 2) + 16)
                        dve.scalar_tensor_tensor(out=gain[:, n % 2, :], in0=num[:, n % 2, :],
                                                 scalar=negf[:, bass.ds(b, 1)], in1=r1[:],
                                                 op0=ALU.mult, op1=ALU.mult).then_inc(s["gain"], 1)

                    for n in range(UNITS + 2):
                        if n >= 2:
                            finish(n - 2)
                        if n < UNITS:
                            scans(n)
                        if 1 <= n <= UNITS:
                            guard(n - 1)


def layer0_attn(k):
    nc, d = k.nc, k.d
    with ExitStack() as ctx:
        def sb(n, s, dt=F32):
            return ctx.enter_context(nc.sbuf_tensor("a0_" + n, s, dt))

        wh = sb("wh", [P, 2, 3, CC, D0])
        wo = sb("wo", [P, H0, C])
        wg = sb("wg", [P, CC, 3 * H0])
        rot = sb("rot", [P, 4, T])
        xt = sb("xt", [P, CC, T])
        gt = sb("gt", [P, CC, T])
        yt = sb("yt", [P, CC, T])
        ot = sb("ot", [P, H0, T])
        x1 = sb("x1", [P, 2, T])
        ra = sb("ra", [P, 2, T])
        rb = sb("rb", [P, 2, T])
        qk = sb("qk", [P, 2, T])
        ksum = sb("ksum", [P, NBLK])
        v = sb("v", [P, TT, D0])
        gate_raw = sb("gate_raw", [P, TT, 3 * H0])
        gate = sb("gate", [P, H0, 3, TT])
        seen = sb("seen", [P, TT])
        wmask = sb("wmask", [P, 3 * BLK])
        cmask = sb("cmask", [P, TT, NBLK])
        zero8 = sb("zero8", [P, TT, NBLK])
        nmax = sb("nmax", [P, 2, TT])
        cmax = sb("cmax", [P, TT])
        sums = sb("sums", [P, 3, TT])
        rsum = sb("rsum", [P, 3, TT])
        coef = sb("coef", [P, 3, TT])
        ef = sb("ef", [P, 3, 512])
        sw = sb("sw", [P, TT, 3 * BLK])
        ewn = sb("ewn", [P, TT, 3 * BLK])
        sc = sb("sc", [P, TT, NBLK])
        sc2 = sb("sc2", [P, TT, NBLK])
        ec = sb("ec", [P, TT, NBLK])
        pc = sb("pc", [P, TT, NBLK])
        pt = sb("pt", [P, 3, 512])
        tt_ = sb("tt_", [P, 3, 512])
        ps = [ctx.enter_context(nc.psum_tensor(f"ps0_s{i}", [P, 512], F32)) for i in range(3)]
        psq = [ctx.enter_context(nc.psum_tensor(f"ps0_q{i}", [P, 512], F32)) for i in range(2)]
        psv = ctx.enter_context(nc.psum_tensor("ps0_v", [P, 512], F32))
        pso = ctx.enter_context(nc.psum_tensor("ps0_o", [P, 512], F32))
        psg = ctx.enter_context(nc.psum_tensor("ps0_g", [P, 512], F32))
        s = {n: k.sem("a0_" + n) for n in (
            "const", "w0", "w1", "fixed", "rot", "x_loaded", "sig", "y", "gates_raw",
            "gates_sig", "gates", "qproj", "roped", "q_sb", "ksum", "vproj", "v_sb", "scores", "win_neg",
            "nmax", "expd", "cmp_step", "cmp_e", "coef", "p_step", "p", "turned", "t_sb", "pv", "o_sb",
            "wo_psum", "x1", "x1_stored0", "x1_stored1")}
        CMP_STEPS = 5

        def cols(t, j, lo=0, hi=None):
            bank, c0 = score_columns(j)
            hi = P * (j + 1) if hi is None else hi
            return t[bank][:, c0 + lo:c0 + hi] if isinstance(t, list) else t[:, bank, c0 + lo:c0 + hi]

        def win(t, j):
            return cols(t, j, max(0, P * j - WIN))

        def wcols(t, j):
            lo = 0 if j else WIN
            return t[:, j, lo:] if len(t.shape) == 3 else t[:, lo:]

        with nc.Block() as block:

            @block.sync
            def _(sp):
                sp.dma_start(wg[:], d["wg"]).then_inc(s["fixed"], 16)
                sp.dma_start(rot[:], d["rot"]).then_inc(s["rot"], 16)
                sp.dma_start(wo[:], d["wo"]).then_inc(s["fixed"], 16)
                with sp.Fori(0, B) as b:
                    xsrc = d["xT"][bass.ds(b, 1)].rearrange("a c p n -> p (a c) n")
                    gsrc = d["gain"][0, bass.ds(b, 1)].rearrange("a c p n -> p (a c) n")
                    sp.wait_ge(s["x1"], b * CC + 1)
                    sp.dma_start(xt[:], xsrc).then_inc(s["x_loaded"], 16)
                    sp.dma_start(gt[:], gsrc).then_inc(s["x_loaded"], 16)
                    with sp.Fori(0, H0 // 2) as n:
                        for i in range(2):
                            src = d["wqkv0"][bass.ds(n * 2 + i, 1)].rearrange("a p k c n -> p (a k) c n")
                            sp.wait_ge(s["vproj"], b * H0 + n * 2 + i + 1)
                            sp.dma_start(wh[:, i], src).then_inc(s[f"w{i}"], 16)
                    for co in range(CC):
                        dst = d["x1"][bass.ds(b, 1), co].rearrange("a p n -> (a p) n")
                        sp.wait_ge(s["x1"], b * CC + co + 2)
                        sp.dma_start(dst, x1[:, co % 2, :]).then_inc(s[f"x1_stored{co % 2}"], 16)
                for i in range(2):
                    sp.wait_ge(s[f"x1_stored{i}"], 16 + 16 * B * CC // 2)

            @block.gpsimd
            def _(pool):
                pool.memset(wmask[:], 0.0).then_inc(s["const"], 1)
                pool.memset(cmask[:], 0.0).then_inc(s["const"], 1)
                pool.memset(seen[:], 1.0 / BLK).then_inc(s["const"], 1)
                pool.wait_ge(s["const"], 3)
                pool.affine_select(out=wmask[:], in_=wmask[:], compare_op=ALU.is_ge, fill=NEG, base=0,
                                   pattern=[[1, 3 * BLK]], channel_multiplier=-1).then_inc(s["const"], 1)
                pool.wait_ge(s["const"], 4)
                pool.affine_select(out=wmask[:], in_=wmask[:], compare_op=ALU.is_ge, fill=NEG, base=WIN,
                                   pattern=[[-1, 3 * BLK]], channel_multiplier=1).then_inc(s["const"], 1)
                pool.affine_select(out=cmask[:], in_=cmask[:], compare_op=ALU.is_ge, fill=NEG, base=1 - BLK,
                                   pattern=[[P, TT], [-BLK, NBLK]], channel_multiplier=1).then_inc(s["const"], 1)
                pool.affine_select(out=seen[:], in_=seen[:], compare_op=ALU.is_ge, fill=0.0, base=1 - BLK,
                                   pattern=[[P, TT]], channel_multiplier=1).then_inc(s["const"], 1)
                with pool.Fori(0, B * H0) as g:
                    for i in range(2):
                        pool.wait_ge(s["roped"], g * 2 + i + 1)
                        pool.tensor_tensor(qk[:, i, :], ra[:, i, :], rb[:, i, :], ALU.add).then_inc(s["q_sb"], 1)

            @block.scalar
            def _(act):
                with act.Fori(0, B) as b:
                    act.wait_ge(s["x_loaded"], b * 32 + 32)
                    for c in range(CC):
                        act.activation(yt[:, c, :], xt[:, c, :], ACT.Sigmoid).then_inc(s["sig"], 1)
                    act.wait_ge(s["gates_raw"], b + 1)
                    act.activation(gate_raw[:], psg[:, 0:TT * 3 * H0].rearrange("p (t n) -> p t n", t=TT),
                                   ACT.Sigmoid).then_inc(s["gates_sig"], 1)

                    def exps(g):
                        for bank, tiles in BANK_TILES:
                            act.wait_ge(s["nmax"], g * 3 + bank + 1)
                            for j in tiles:
                                act.activation(cols(ef, j), cols(ps, j), ACT.Exp, bias=nmax[:, 0, j:j + 1],
                                               accum_out=sums[:, 1, j:j + 1]).then_inc(s["expd"], 1)
                                act.activation(wcols(ewn, j), wcols(sw, j), ACT.Exp, bias=nmax[:, 1, j:j + 1],
                                               scale=-1.0, accum_out=sums[:, 2, j:j + 1]).then_inc(s["expd"], 1)
                        act.wait_ge(s["cmp_step"], g * CMP_STEPS + 2)
                        act.activation(ec[:], sc2[:], ACT.Exp).then_inc(s["cmp_e"], 1)

                    def turn(g, h):
                        for m in range(3):
                            act.wait_ge(s["turned"], g * 3 + m + 1)
                            w = 256 if m == 2 else 512
                            act.activation(tt_[:, m, 0:w], ps[m][:, 0:w], ACT.Copy).then_inc(s["t_sb"], 1)
                        act.wait_ge(s["pv"], g + 1)
                        act.activation(ot[:, bass.ds(h, 1), :].rearrange("p a n -> p (a n)"), pso[:],
                                       ACT.Copy).then_inc(s["o_sb"], 1)

                    def head(g, h, first):
                        if not first:
                            turn(g - 1, h - 1)
                        act.wait_ge(s["vproj"], g + 3)
                        act.activation(v[:].rearrange("p t n -> p (t n)"), psv[:], ACT.Copy).then_inc(s["v_sb"], 1)
                        exps(g)

                    head(b * H0, 0, True)
                    with act.Fori(1, H0) as h:
                        head(b * H0 + h, h, False)
                    turn(b * H0 + H0 - 1, H0 - 1)

            @block.tensor
            def _(pe):
                pe.sem_inc(s["vproj"], 2)
                pe.sem_inc(s["x1"], 1)
                pe.wait_ge(s["fixed"], 32)
                with pe.Fori(0, B) as b:
                    pe.wait_ge(s["y"], b * CC + CC)
                    for t in range(TT):
                        for c in range(CC):
                            mm = pe.matmul(psg[:, t * 48:t * 48 + 48], yt[:, c, t * P:(t + 1) * P], wg[:, c, :],
                                           start=c == 0, stop=c == CC - 1)
                    mm.then_inc(s["gates_raw"], 1)

                    def project(g, i, pair):
                        pe.wait_ge(s[f"w{i}"], b * (8 * H0) + pair * 16 + 16)
                        for n in range(2):
                            for c in range(CC):
                                mm = pe.matmul(psq[n][:], wh[:, i, n, c, :], yt[:, c, :],
                                               start=c == 0, stop=c == CC - 1)
                            mm.then_inc(s["qproj"], 1)

                    def project_v(g, i):
                        for t in range(TT):
                            for c in range(CC):
                                mm = pe.matmul(psv[:, t * D0:(t + 1) * D0], yt[:, c, t * P:(t + 1) * P],
                                               wh[:, i, 2, c, :], start=c == 0, stop=c == CC - 1)
                        mm.then_inc(s["vproj"], 1)

                    def scores(g):
                        pe.wait_ge(s["q_sb"], g * 2 + 2)
                        for bank, tiles in BANK_TILES:
                            for j in tiles:
                                pe.matmul(cols(ps, j), qk[:, 0, j * P:(j + 1) * P], qk[:, 1, 0:P * (j + 1)],
                                          start=True, stop=False)
                                mm = pe.matmul(cols(ps, j, P * j), k.ident_b[:], k.causal_b[:],
                                               start=False, stop=True)
                            if bank == 2:
                                pe.wait_ge(s["ksum"], g + 1)
                                for j in range(TT):
                                    mm = pe.matmul(ps[2][:, 256 + j * NBLK:256 + (j + 1) * NBLK],
                                                   qk[:, 0, j * P:(j + 1) * P], ksum[:], start=True, stop=True)
                            mm.then_inc(s["scores"], 1)

                    def values(g, first):
                        for bank, tiles in ((0, (0,)), (1, (1, 3)), (2, (2,))):
                            if bank == 0:
                                pe.wait_ge(s["p"], g * TT + TT)
                            for m in tiles:
                                _, c0 = turned_columns(m)
                                for j in range(m, TT):
                                    mm = pe.transpose(ps[bank][:, c0 + (j - m) * P:c0 + (j - m + 1) * P],
                                                      cols(pt, j, m * P, (m + 1) * P), k.ident[:])
                            mm.then_inc(s["turned"], 1)
                        for n, m in enumerate((0, 1, 3, 2)):
                            bank, c0 = turned_columns(m)
                            if n == 0:
                                pe.wait_ge(s["v_sb"], g + 1)
                                if not first:
                                    pe.wait_ge(s["o_sb"], g)
                            pe.wait_ge(s["t_sb"], g * 3 + bank + 1)
                            mm = pe.matmul(pso[:, m * P:], v[:, m, :], tt_[:, bank, c0:c0 + T - m * P],
                                           start=n == 0, stop=n == TT - 1)
                        mm.then_inc(s["pv"], 1)

                    def pair(n, first):
                        for i in range(2):
                            g = b * H0 + n * 2 + i
                            project(g, i, n)
                            if not (first and i == 0):
                                values(g - 1, first and i == 1)
                            project_v(g, i)
                            scores(g)

                    pair(0, True)
                    with pe.Fori(1, H0 // 2) as n:
                        pair(n, False)
                    values(b * H0 + H0 - 1, False)
                    pe.wait_ge(s["o_sb"], b * H0 + H0)
                    for co in range(CC):
                        if co >= 2:
                            pe.wait_ge(s["x1"], b * CC + co)
                        for h in range(H0):
                            mm = pe.matmul(psq[co % 2][:], wo[:, h, co * P:(co + 1) * P], ot[:, h, :],
                                           start=h == 0, stop=h == H0 - 1)
                        mm.then_inc(s["wo_psum"], 1)

            @block.vector
            def _(dve):
                for i in range(2):
                    dve.sem_inc(s[f"x1_stored{i}"], 16)
                dve.wait_ge(s["const"], 7)
                dve.wait_ge(s["rot"], 16)
                with dve.Fori(0, B) as b:
                    for c in range(CC):
                        dve.wait_ge(s["sig"], b * CC + c + 1)
                        dve.tensor_tensor(yt[:, c, :], yt[:, c, :], gt[:, c, :], ALU.mult).then_inc(s["y"], 1)
                    dve.wait_ge(s["gates_sig"], b + 1)
                    dve.tensor_copy(gate[:].rearrange("p h k t -> p t k h"),
                                    gate_raw[:].rearrange("p t (k h) -> p t k h", k=3)).then_inc(s["gates"], 1)
                    dve.wait_ge(s["gates"], b * 2 + 1)
                    dve.tensor_tensor(gate[:, :, 0, :], gate[:, :, 0, :],
                                      seen[:].unsqueeze(1).to_broadcast([P, H0, TT]), ALU.mult).then_inc(s["gates"], 1)

                    def rope(g):
                        for i in range(2):
                            dve.wait_ge(s["qproj"], g * 2 + i + 1)
                            dve.tensor_tensor(ra[:, i, :], psq[i][:], rot[:, 2 * i, :], ALU.mult)
                            dve.tensor_tensor(rb[0:64, i, :], psq[i][64:P, :], rot[64:P, 2 * i + 1, :], ALU.mult)
                            dve.tensor_tensor(rb[64:P, i, :], psq[i][0:64, :], rot[0:64, 2 * i + 1, :],
                                              ALU.mult).then_inc(s["roped"], 1)
                        dve.wait_ge(s["q_sb"], g * 2 + 2)
                        dve.tensor_reduce(ksum[:], qk[:, 1, :].rearrange("p (m n) -> p m n", n=BLK), AX,
                                          ALU.add).then_inc(s["ksum"], 1)

                    def softmax(g, h):
                        c = g * CMP_STEPS
                        for bank, tiles in BANK_TILES:
                            dve.wait_ge(s["scores"], g * 3 + bank + 1)
                            for j in tiles:
                                dve.tensor_reduce(nmax[:, 0, j:j + 1], cols(ps, j), AX, ALU.max, negate=True)
                                i = dve.tensor_tensor_reduce(out=wcols(sw, j), in0=win(ps, j), in1=wcols(wmask, j),
                                                             scale=-1.0, scalar=3.0e38, op0=ALU.add, op1=ALU.min,
                                                             accum_out=nmax[:, 1, j:j + 1])
                            if bank == 2:
                                i = dve.scalar_tensor_tensor(
                                    out=sc[:], in0=ps[2][:, 256:256 + TT * NBLK].rearrange("p (t m) -> p t m", t=TT),
                                    scalar=1.0 / BLK, in1=cmask[:], op0=ALU.mult, op1=ALU.add)
                            i.then_inc(s["nmax"], 1)
                        dve.wait_ge(s["nmax"], g * 3 + 3)
                        dve.tensor_reduce(cmax[:], sc[:], AX, ALU.max).then_inc(s["cmp_step"], 1)
                        dve.wait_ge(s["cmp_step"], c + 1)
                        dve.tensor_tensor(sc2[:], sc[:], cmax[:].unsqueeze(2).to_broadcast([P, TT, NBLK]),
                                          ALU.subtract).then_inc(s["cmp_step"], 1)
                        dve.wait_ge(s["cmp_e"], g + 1)
                        dve.tensor_reduce(sums[:, 0, :], ec[:], AX, ALU.add).then_inc(s["cmp_step"], 1)
                        dve.wait_ge(s["cmp_step"], c + 3)
                        dve.wait_ge(s["expd"], g * 2 * TT + 2 * TT)
                        dve.wait_ge(s["gates"], b * 2 + 2)
                        dve.reciprocal(rsum[:], sums[:]).then_inc(s["cmp_step"], 1)
                        dve.wait_ge(s["cmp_step"], c + 4)
                        dve.tensor_tensor(coef[:], rsum[:], gate[:, bass.ds(h, 1)].rearrange("p a k t -> p (a k) t"),
                                          ALU.mult).then_inc(s["cmp_step"], 1)
                        dve.wait_ge(s["cmp_step"], c + 5)
                        dve.tensor_tensor(pc[:], ec[:], coef[:, 0, :].unsqueeze(2).to_broadcast([P, TT, NBLK]),
                                          ALU.mult).then_inc(s["coef"], 1)
                        dve.wait_ge(s["coef"], g + 1)
                        for n, j in enumerate((3, 2, 1, 0)):
                            dve.scalar_tensor_tensor(
                                out=cols(pt, j).rearrange("p (m n) -> p m n", n=BLK),
                                in0=cols(ef, j).rearrange("p (m n) -> p m n", n=BLK), scalar=coef[:, 1, j:j + 1],
                                in1=pc[:, j, 0:2 * (j + 1)].unsqueeze(2).to_broadcast([P, 2 * (j + 1), BLK]),
                                op0=ALU.mult, op1=ALU.add).then_inc(s["p_step"], 1)
                        for n, j in enumerate((3, 2, 1, 0)):
                            dve.wait_ge(s["p_step"], g * TT + n + 1)
                            dve.scalar_tensor_tensor(out=win(pt, j), in0=wcols(ewn, j), scalar=coef[:, 2, j:j + 1],
                                                     in1=win(pt, j), op0=ALU.mult, op1=ALU.add).then_inc(s["p"], 1)

                    with dve.Fori(0, H0) as h:
                        g = b * H0 + h
                        rope(g)
                        softmax(g, h)
                    for co in range(CC):
                        dve.wait_ge(s["wo_psum"], b * CC + co + 1)
                        dve.wait_ge(s[f"x1_stored{co % 2}"], b * 32 + 16 * (co // 2) + 16)
                        dve.tensor_tensor(x1[:, co % 2, :], psq[co % 2][:], xt[:, co, :],
                                          ALU.add).then_inc(s["x1"], 1)


def moe_route(k):
    nc, d = k.nc, k.d
    with ExitStack() as ctx:
        def sb(n, s, dt=F32):
            return ctx.enter_context(nc.sbuf_tensor("mr_" + n, s, dt))

        wr = sb("wr", [P, CC, E])
        zeros = sb("zeros", [P, C])
        xt = sb("xt", [P, CC, T])
        gt = sb("gt", [P, CC, T])
        yt = sb("yt", [P, CC, T])
        rows = sb("rows", [P, NT, C])
        logits = sb("logits", [P, NT, E])
        top = sb("top", [P, NT, 8])
        first = sb("first", [P, E])
        pick = sb("pick", [P, NT, E])
        best = sb("best", [P, NT])
        onehot = sb("onehot", [P, NT, E])
        before = sb("before", [P, NT + 1, E])
        diff = sb("diff", [P, NT])
        ones = sb("ones", [P, P])
        prior = sb("prior", [P, P])
        steps = sb("steps", [P, E, NT])
        over = sb("over", [P, E, NT])
        tiles = sb("tiles", [P, E])
        count = sb("count", [P, E])
        ends = sb("ends", [P, E])
        base = sb("base", [P, E])
        place = sb("place", [P, NT, E])
        slotf = sb("slotf", [P, NT])
        tile_no = sb("tile_no", [P, SLOT_TILES, E])
        past = sb("past", [P, SLOT_TILES, E])
        expertf = sb("expertf", [P, SLOT_TILES])
        psr = ctx.enter_context(nc.psum_tensor("psr_l", [P, 512], F32))
        pst = [ctx.enter_context(nc.psum_tensor(f"psr_t{i}", [P, 512], F32)) for i in range(2)]
        pss = ctx.enter_context(nc.psum_tensor("psr_s", [P, 512], F32))
        s = {n: k.sem("mr_" + n) for n in (
            "router", "x_loaded", "zeros", "zeroed", "const", "sig", "y", "logits_ps", "logits", "rows_ps",
            "rows", "math", "sums", "exp", "slots", "scattered")}
        with nc.Block() as block:

            @block.sync
            def _(sp):
                sp.dma_start(wr[:], d["router"]).then_inc(s["router"], 16)
                with sp.Fori(0, B) as b:
                    xsrc = d["x1"][bass.ds(b, 1)].rearrange("a c p n -> p (a c) n")
                    gsrc = d["gain"][1, bass.ds(b, 1)].rearrange("a c p n -> p (a c) n")
                    sp.wait_ge(s["y"], b * CC + 1)
                    sp.dma_start(xt[:], xsrc).then_inc(s["x_loaded"], 16)
                    sp.dma_start(gt[:], gsrc).then_inc(s["x_loaded"], 16)
                sp.wait_ge(s["zeros"], 1)
                for j in range(SLOT_TILES + 1):
                    sp.dma_start(d["slot_x"][j * P:(j + 1) * P, :], zeros[:]).then_inc(s["zeroed"], 16)

            @block.gpsimd
            def _(pool):
                pool.memset(zeros[:], 0.0).then_inc(s["zeros"], 1)
                pool.memset(ones[:], 1.0).then_inc(s["const"], 1)
                pool.memset(prior[:], 1.0).then_inc(s["const"], 1)
                pool.iota(first[:], pattern=[[-1, E]], base=E, channel_multiplier=0,
                          allow_small_or_imprecise_dtypes=True).then_inc(s["const"], 1)
                pool.iota(steps[:], pattern=[[0, E], [P, NT]], base=0, channel_multiplier=0,
                          allow_small_or_imprecise_dtypes=True).then_inc(s["const"], 1)
                pool.iota(tile_no[:], pattern=[[1, SLOT_TILES], [0, E]], base=0, channel_multiplier=0,
                          allow_small_or_imprecise_dtypes=True).then_inc(s["const"], 1)
                pool.wait_ge(s["const"], 5)
                pool.affine_select(out=prior[:], in_=prior[:], compare_op=ALU.is_gt, fill=0.0, base=0,
                                   pattern=[[1, P]], channel_multiplier=-1).then_inc(s["const"], 1)
                pool.wait_ge(s["zeroed"], 16 * (SLOT_TILES + 1))
                pool.wait_ge(s["slots"], 1)
                pool.wait_ge(s["rows"], NT)
                for i in range(NT):
                    pool.indirect_dma_start(d["slot_x"], bass.IndirectOffsetOnAxis(ap=k.slot[:, i:i + 1], axis=0),
                                            rows[:, i, :], None).then_inc(s["scattered"], 16)
                pool.wait_ge(s["scattered"], 16 * NT)

            @block.scalar
            def _(act):
                with act.Fori(0, B) as b:
                    act.wait_ge(s["x_loaded"], b * 32 + 32)
                    for c in range(CC):
                        act.activation(yt[:, c, :], xt[:, c, :], ACT.Sigmoid).then_inc(s["sig"], 1)
                    for t in range(TT):
                        act.wait_ge(s["rows_ps"], b * TT + t + 1)
                        act.activation(rows[:, bass.ds(b * TT + t, 1), :].rearrange("p a n -> p (a n)"),
                                       pst[t % 2][:], ACT.Copy).then_inc(s["rows"], 1)
                act.wait_ge(s["math"], 1)
                act.activation(diff[:], diff[:], ACT.Exp).then_inc(s["exp"], 1)

            @block.tensor
            def _(pe):
                pe.wait_ge(s["router"], 16)
                pe.sem_inc(s["y"], 1)
                with pe.Fori(0, B) as b:
                    pe.wait_ge(s["y"], b * CC + CC + 1)
                    for t in range(TT):
                        for c in range(CC):
                            mm = pe.matmul(psr[:, t * E:(t + 1) * E], yt[:, c, t * P:(t + 1) * P], wr[:, c, :],
                                           start=c == 0, stop=c == CC - 1)
                    mm.then_inc(s["logits_ps"], 1)
                    for t in range(TT):
                        if t >= 2:
                            pe.wait_ge(s["rows"], b * TT + t - 1)
                        for c in range(CC):
                            mm = pe.transpose(pst[t % 2][:, c * P:(c + 1) * P], yt[:, c, t * P:(t + 1) * P], k.ident[:])
                        mm.then_inc(s["rows_ps"], 1)
                pe.wait_ge(s["math"], 2)
                pe.wait_ge(s["const"], 6)
                pe.matmul(pss[:, 0:NT * E], prior[:], onehot[:].rearrange("p t e -> p (t e)"), start=True, stop=False)
                pe.matmul(pss[:, 0:NT * E], ones[:], before[:, 0:NT, :].rearrange("p t e -> p (t e)"),
                          start=False, stop=True)
                pe.matmul(pss[:, NT * E:NT * E + E], ones[:], before[:, NT, :], start=True,
                          stop=True).then_inc(s["sums"], 1)

            @block.vector
            def _(dve):
                with dve.Fori(0, B) as b:
                    for c in range(CC):
                        dve.wait_ge(s["sig"], b * CC + c + 1)
                        dve.tensor_tensor(yt[:, c, :], yt[:, c, :], gt[:, c, :], ALU.mult).then_inc(s["y"], 1)
                    dve.wait_ge(s["logits_ps"], b + 1)
                    dve.tensor_copy(logits[:, bass.ds(b * TT, TT), :],
                                    psr[:, 0:TT * E].rearrange("p (t e) -> p t e", t=TT)).then_inc(s["logits"], 1)
                dve.wait_ge(s["const"], 6)
                dve.wait_ge(s["logits"], B)
                for i in range(NT):
                    m = dve.max(top[:, i, :], logits[:, i, :])
                step = Tally(k.sem("mr_step"))

                def then(ins):
                    dve.wait_ge(step.sem, step.inc(ins))

                def wide(a, n=E):
                    return a.unsqueeze(2).to_broadcast([P, a.shape[1], n])

                then(m)
                dve.tensor_tensor(diff[:], top[:, :, 1], top[:, :, 0], ALU.subtract).then_inc(s["math"], 1)
                then(dve.tensor_tensor(pick[:], logits[:], wide(top[:, :, 0]), ALU.is_equal))
                then(dve.tensor_tensor(pick[:], pick[:], first[:].unsqueeze(1).to_broadcast([P, NT, E]), ALU.mult))
                then(dve.tensor_reduce(best[:], pick[:], AX, ALU.max))
                then(dve.memset(before[:, 0, :], 0.0))
                then(dve.tensor_tensor(onehot[:], wide(best[:]), first[:].unsqueeze(1).to_broadcast([P, NT, E]),
                                       ALU.is_equal))
                for i in range(NT):
                    then(dve.tensor_tensor(before[:, i + 1, :], before[:, i, :], onehot[:, i, :], ALU.add))
                dve.wait_ge(s["exp"], 1)
                then(dve.tensor_scalar(diff[:], diff[:], 1.0, None, ALU.add))
                dve.reciprocal(k.weight[:], diff[:]).then_inc(s["math"], 1)
                dve.wait_ge(s["sums"], 1)
                then(dve.tensor_copy(count[:], pss[:, NT * E:NT * E + E]))
                then(dve.tensor_tensor(over[:], wide(count[:], NT), steps[:], ALU.is_gt))
                then(dve.tensor_reduce(tiles[:], over[:], AX, ALU.add))
                then(dve.tensor_tensor_scan(ends[:], ones[:, 0:E], tiles[:], 0.0, ALU.mult, ALU.add))
                then(dve.tensor_tensor(base[:], ends[:], tiles[:], ALU.subtract))
                then(dve.tensor_scalar(base[:], base[:], float(P), None, ALU.mult))
                then(dve.tensor_tensor(place[:], pss[:, 0:NT * E].rearrange("p (t e) -> p t e", t=NT),
                                       base[:].unsqueeze(1).to_broadcast([P, NT, E]), ALU.add))
                then(dve.tensor_tensor(place[:], place[:], onehot[:], ALU.mult))
                then(dve.tensor_reduce(slotf[:], place[:], AX, ALU.add))
                dve.tensor_copy(k.slot[:], slotf[:]).then_inc(s["slots"], 1)
                then(dve.tensor_tensor(past[:], tile_no[:], ends[:].unsqueeze(1).to_broadcast([P, SLOT_TILES, E]),
                                       ALU.is_ge))
                then(dve.tensor_reduce(expertf[:], past[:], AX, ALU.add))
                then(dve.tensor_scalar(expertf[:], expertf[:], float(E - 1), None, ALU.min))
                then(dve.tensor_copy(k.tile_expert[:], expertf[:]))


def moe_experts(k):
    nc, d = k.nc, k.d
    GW = (E // 4)
    with ExitStack() as ctx:
        def sb(n, s, dt=F32):
            return ctx.enter_context(nc.sbuf_tensor("me_" + n, s, dt))

        wgu = sb("wgu", [P, E, 2, CC, I])
        wd = sb("wd", [P, E, KI, C])
        xin = sb("xin", [P, 2, C])
        xT = sb("xT", [P, 2, C])
        sg = sb("sg", [P, I])
        a = sb("a", [P, 2, KI * P])
        aT = sb("aT", [P, KI * P])
        yo = sb("yo", [P, 2, C])
        psx = ctx.enter_context(nc.psum_tensor("pse_x", [P, 512], F32))
        psg = ctx.enter_context(nc.psum_tensor("pse_g", [P, 512], F32))
        psu = ctx.enter_context(nc.psum_tensor("pse_u", [P, 512], F32))
        psa = ctx.enter_context(nc.psum_tensor("pse_a", [P, 512], F32))
        psd = ctx.enter_context(nc.psum_tensor("pse_d", [P, 512], F32))
        s = {n: k.sem("me_" + n) for n in (
            "weights", "x0", "x1", "x_ps", "xT", "gu", "silu", "a", "a_pad", "a_ps", "aT", "down", "y", "stored0",
            "stored1")}
        last = SLOT_TILES - 1
        with nc.Block() as block:

            @block.sync
            def _(sp):
                def load(j, i, dyn):
                    src = d["slot_x"][bass.ds(j * P, P), :] if dyn else d["slot_x"][j * P:(j + 1) * P, :]
                    if dyn:
                        sp.wait_ge(s["x_ps"], j - 1)
                    sp.dma_start(xin[:, i, :], src).then_inc(s[f"x{i}"], 16)

                def store(j, i, dyn):
                    dst = d["slot_y"][bass.ds(j * P, P), :] if dyn else d["slot_y"][j * P:(j + 1) * P, :]
                    sp.wait_ge(s["y"], j + 1)
                    sp.dma_start(dst, yo[:, i, :]).then_inc(s[f"stored{i}"], 16)

                load(0, 0, False)
                load(1, 1, False)
                for e in range(0, E, GW):
                    sp.dma_start(wgu[:, e:e + GW], d["gate_up"][:, e:e + GW]).then_inc(s["weights"], 16)
                    sp.dma_start(wd[:, e:e + GW], d["down"][:, e:e + GW]).then_inc(s["weights"], 16)
                with sp.Fori(1, last // 2 + 1) as m:
                    for i in range(2):
                        load(m * 2 + i, i, True)
                        store(m * 2 + (i - 2), i, True)
                store(last, last % 2, False)
                for i in range(2):
                    sp.wait_ge(s[f"stored{i}"], 16 + 16 * ((SLOT_TILES + 1 - i) // 2))

            @block.tensor
            def _(pe):
                pe.wait_ge(s["a_pad"], 1)

                def turn_x(j, i, first):
                    pe.wait_ge(s[f"x{i}"], (j // 2 if isinstance(j, int) else (j - i) // 2) * 16 + 16)
                    if not first:
                        pe.wait_ge(s["xT"], j)
                    for c in range(CC):
                        mm = pe.transpose(psx[:, c * P:(c + 1) * P], xin[:, i, c * P:(c + 1) * P], k.ident[:])
                    mm.then_inc(s["x_ps"], 1)

                def gate_up(j, i):
                    e = pe.value_load(k.tile_expert[0:1, bass.ds(j, 1)], min_val=0, max_val=E - 1)
                    pe.wait_ge(s["xT"], j + 1)
                    for n, ps in enumerate((psg, psu)):
                        for c in range(CC):
                            mm = pe.matmul(ps[:, 0:I], xT[:, i, c * P:(c + 1) * P],
                                           wgu[:, bass.ds(e, 1), n, c, :].rearrange("p a n -> p (a n)"),
                                           start=c == 0, stop=c == CC - 1)
                    mm.then_inc(s["gu"], 1)

                def turn_a(j, i):
                    pe.wait_ge(s["a"], j + 1)
                    for c in range(KI):
                        mm = pe.transpose(psa[:, c * P:(c + 1) * P], a[:, i, c * P:(c + 1) * P], k.ident[:])
                    mm.then_inc(s["a_ps"], 1)

                def down(j, i, first):
                    e = pe.value_load(k.tile_expert[0:1, bass.ds(j, 1)], min_val=0, max_val=E - 1)
                    pe.wait_ge(s["aT"], j + 1)
                    if not first:
                        pe.wait_ge(s["y"], j)
                    for c in range(KI):
                        mm = pe.matmul(psd[:], aT[:, c * P:(c + 1) * P],
                                       wd[:, bass.ds(e, 1), c, :].rearrange("p a n -> p (a n)"),
                                       start=c == 0, stop=c == KI - 1)
                    mm.then_inc(s["down"], 1)

                turn_x(0, 0, True)
                pe.wait_ge(s["weights"], 16 * 2 * (E // GW))
                gate_up(0, 0)
                turn_x(1, 1, False)
                def step(j, i, first):
                    turn_a(j - 1, 1 - i)
                    gate_up(j, i)
                    turn_x(j + 1, 1 - i, False)
                    down(j - 1, 1 - i, first)

                step(1, 1, True)
                step(2, 0, False)
                with pe.Fori(2, last // 2 + 1) as m:
                    step(m * 2 - 1, 1, False)
                    step(m * 2, 0, False)
                turn_a(last, last % 2)
                down(last, last % 2, False)

            @block.scalar
            def _(act):
                def take_x(j, i):
                    act.wait_ge(s["x_ps"], j + 1)
                    act.activation(xT[:, i, :], psx[:], ACT.Copy).then_inc(s["xT"], 1)

                def silu(j):
                    act.wait_ge(s["gu"], j + 1)
                    act.activation(sg[:], psg[:, 0:I], ACT.Silu).then_inc(s["silu"], 1)

                take_x(0, 0)
                silu(0)
                take_x(1, 1)
                with act.Fori(1, last // 2 + 1) as m:
                    silu(m * 2 - 1)
                    take_x(m * 2, 0)
                    silu(m * 2)
                    take_x(m * 2 + 1, 1)

            @block.vector
            def _(dve):
                for i in range(2):
                    dve.sem_inc(s[f"stored{i}"], 16)
                dve.memset(a[:], 0.0).then_inc(s["a_pad"], 1)
                dve.wait_ge(s["a_pad"], 1)

                def mul(j, i):
                    dve.wait_ge(s["silu"], j + 1)
                    dve.tensor_tensor(a[:, i, 0:I], sg[:], psu[:, 0:I], ALU.mult).then_inc(s["a"], 1)

                def take_a(j):
                    dve.wait_ge(s["a_ps"], j + 1)
                    dve.tensor_copy(aT[:], psa[:, 0:KI * P]).then_inc(s["aT"], 1)

                def out(j, i, half):
                    dve.wait_ge(s["down"], j + 1)
                    dve.wait_ge(s[f"stored{i}"], half * 16 + 16)
                    dve.tensor_copy(yo[:, i, :], psd[:]).then_inc(s["y"], 1)

                mul(0, 0)
                with dve.Fori(1, last // 2 + 1) as m:
                    take_a(m * 2 - 2)
                    mul(m * 2 - 1, 1)
                    out(m * 2 - 2, 0, m - 1)
                    take_a(m * 2 - 1)
                    mul(m * 2, 0)
                    out(m * 2 - 1, 1, m - 1)
                take_a(last)
                out(last, last % 2, last // 2)


def moe_combine(k):
    nc, d = k.nc, k.d
    with ExitStack() as ctx:
        def sb(n, s, dt=F32):
            return ctx.enter_context(nc.sbuf_tensor("mc_" + n, s, dt))

        got = sb("got", [P, NT, C])
        yw = sb("yw", [P, 2, C])
        xt = sb("xt", [P, 2, CC, T])
        ps = [ctx.enter_context(nc.psum_tensor(f"psc_{i}", [P, 512], F32)) for i in range(2)]
        s = {n: k.sem("mc_" + n) for n in ("got", "x0", "x1", "weighted", "turned", "x2", "stored")}
        with nc.Block() as block:

            @block.gpsimd
            def _(pool):
                for i in range(NT):
                    pool.indirect_dma_start(got[:, i, :], None, d["slot_y"],
                                            bass.IndirectOffsetOnAxis(ap=k.slot[:, i:i + 1], axis=0)
                                            ).then_inc(s["got"], 16)

            @block.sync
            def _(sp):
                for b in range(B):
                    if b >= 2:
                        sp.wait_ge(s["stored"], 16 * (b - 1))
                    sp.dma_start(xt[:, b % 2], d["x1"][b].rearrange("c p n -> p c n")).then_inc(s[f"x{b % 2}"], 16)
                    if b >= 1:
                        sp.wait_ge(s["x2"], TT * b)
                        sp.dma_start(d["x2"][b - 1].rearrange("c p n -> p c n"), xt[:, (b - 1) % 2]).then_inc(s["stored"], 16)
                sp.wait_ge(s["x2"], TT * B)
                sp.dma_start(d["x2"][B - 1].rearrange("c p n -> p c n"), xt[:, (B - 1) % 2]).then_inc(s["stored"], 16)
                sp.wait_ge(s["stored"], 16 * B)

            @block.tensor
            def _(pe):
                for i in range(NT):
                    pe.wait_ge(s["weighted"], i + 1)
                    if i >= 2:
                        pe.wait_ge(s["x2"], i - 1)
                    for c in range(CC):
                        mm = pe.transpose(ps[i % 2][:, c * P:(c + 1) * P], yw[:, i % 2, c * P:(c + 1) * P], k.ident[:])
                    mm.then_inc(s["turned"], 1)

            @block.vector
            def _(dve):
                def weigh(i):
                    dve.wait_ge(s["got"], 16 * NT)
                    if i >= 2:
                        dve.wait_ge(s["turned"], i - 1)
                    dve.tensor_scalar(yw[:, i % 2, :], got[:, i, :], k.weight[:, i:i + 1], None,
                                      ALU.mult).then_inc(s["weighted"], 1)

                weigh(0)
                for i in range(NT):
                    if i + 1 < NT:
                        weigh(i + 1)
                    b, t = divmod(i, TT)
                    if t == 0:
                        dve.wait_ge(s[f"x{b % 2}"], 16 * (b // 2 + 1))
                    dve.wait_ge(s["turned"], i + 1)
                    x = xt[:, b % 2, :, t * P:(t + 1) * P]
                    dve.tensor_tensor(x, ps[i % 2][:].rearrange("p (c n) -> p c n", c=CC), x, ALU.add).then_inc(s["x2"], 1)


def layer1_attn(k):
    nc, d = k.nc, k.d
    with ExitStack() as ctx:
        def sb(n, s, dt=F32):
            return ctx.enter_context(nc.sbuf_tensor("a1_" + n, s, dt))

        w = sb("w", [P, 3, CC, P])
        wp = sb("wp", [P, CC, C])
        bqk = sb("bqk", [P, 3, CC])
        bq = sb("bq", [P, CC])
        bv = sb("bv", [P, C])
        bp = sb("bp", [P, CC])
        xt = sb("xt", [P, CC, T])
        gt = sb("gt", [P, CC, T])
        yt = sb("yt", [P, CC, T])
        qk = sb("qk", [P, 2, T])
        v = sb("v", [P, TT, P])
        nmax = sb("nmax", [P, HPC, TT])
        sums = sb("sums", [P, HPC, TT])
        rsum = sb("rsum", [P, HPC, TT])
        ef = sb("ef", [P, 2, 3, 512])
        tt = sb("tt", [P, 2, 3, 512])
        ob = sb("ob", [P, TT, P])
        ot = sb("ot", [P, CC, T])
        x3 = sb("x3", [P, 2, T])
        ps = [[ctx.enter_context(nc.psum_tensor(f"ps1_{a}{i}", [P, 512], F32)) for i in range(3)] for a in range(2)]
        pso = [ctx.enter_context(nc.psum_tensor(f"ps1_o{i}", [P, 512], F32)) for i in range(2)]
        s = {n: k.sem("a1_" + n) for n in (
            "fixed", "w", "x_loaded", "sig", "y", "bq", "qkproj", "qk", "vproj", "v", "scores", "nmax", "expd",
            "turned", "t_act", "t_dve", "pv", "rsum", "o", "o_ps", "ot", "proj", "x3", "x3_stored0", "x3_stored1")}
        SCALE = float(np.float32(1.0) / np.sqrt(np.float32(D1)))

        def cols(t, j, lo=0, hi=None):
            bank, c0 = score_columns(j)
            hi = P * (j + 1) if hi is None else hi
            return t[bank][:, c0 + lo:c0 + hi] if isinstance(t, list) else t[:, bank, c0 + lo:c0 + hi]

        def bufs(i):
            return (i + 1) % 2

        with nc.Block() as block:

            @block.sync
            def _(sp):
                sp.dma_start(wp[:], d["wp1"]).then_inc(s["fixed"], 16)
                sp.dma_start(bqk[:], d["bqkv1"]).then_inc(s["fixed"], 16)
                sp.dma_start(bv[:], d["bv1"].partition_broadcast(P)).then_inc(s["fixed"], 16)
                sp.dma_start(bp[:], d["bp1"]).then_inc(s["fixed"], 16)
                with sp.Fori(0, B) as b:
                    xsrc = d["x2"][bass.ds(b, 1)].rearrange("a c p n -> p (a c) n")
                    gsrc = d["gain"][2, bass.ds(b, 1)].rearrange("a c p n -> p (a c) n")
                    sp.wait_ge(s["x3"], b * CC + 1)
                    sp.dma_start(xt[:], xsrc).then_inc(s["x_loaded"], 16)
                    sp.dma_start(gt[:], gsrc).then_inc(s["x_loaded"], 16)
                    with sp.Fori(0, CC) as q:
                        src = d["wqkv1"][bass.ds(q, 1)].rearrange("a p k c n -> p (a k) c n")
                        sp.wait_ge(s["vproj"], b * CC + q + 1)
                        sp.dma_start(w[:], src).then_inc(s["w"], 16)
                    for co in range(CC):
                        dst = d["x3"][bass.ds(b, 1), co].rearrange("a p n -> (a p) n")
                        sp.wait_ge(s["x3"], b * CC + co + 2)
                        sp.dma_start(dst, x3[:, co % 2, :]).then_inc(s[f"x3_stored{co % 2}"], 16)
                for i in range(2):
                    sp.wait_ge(s[f"x3_stored{i}"], 16 + 16 * B * CC // 2)

            @block.scalar
            def _(act):
                act.wait_ge(s["bq"], 1)
                with act.Fori(0, B) as b:
                    act.wait_ge(s["x_loaded"], b * 32 + 32)
                    for c in range(CC):
                        act.activation(yt[:, c, :], xt[:, c, :], ACT.Sigmoid).then_inc(s["sig"], 1)
                    with act.Fori(0, CC) as q:
                        g = b * CC + q
                        act.wait_ge(s["qkproj"], g * 2 + 1)
                        act.activation(qk[:, 0, :], ps[0][0][:], ACT.Identity, bias=bq[:, bass.ds(q, 1)],
                                       scale=SCALE).then_inc(s["qk"], 1)
                        act.wait_ge(s["qkproj"], g * 2 + 2)
                        act.activation(qk[:, 1, :], ps[0][1][:], ACT.Identity,
                                       bias=bqk[:, 1, bass.ds(q, 1)]).then_inc(s["qk"], 1)

                        def exps(i):
                            for bank, tiles in BANK_TILES:
                                act.wait_ge(s["nmax"], (g * HPC + i) * 3 + bank + 1)
                                for j in tiles:
                                    act.activation(cols(ef[:, bufs(i)], j), cols(ps[bufs(i)], j), ACT.Exp,
                                                   bias=nmax[:, i, j:j + 1],
                                                   accum_out=sums[:, i, j:j + 1]).then_inc(s["expd"], 1)

                        def take(i):
                            act.wait_ge(s["turned"], (g * HPC + i) * 3 + 1)
                            act.activation(tt[:, bufs(i), 0, :], ps[bufs(i)][0][:], ACT.Copy).then_inc(s["t_act"], 1)

                        exps(0)
                        exps(1)
                        for i in range(HPC):
                            take(i)
                            if i + 2 < HPC:
                                exps(i + 2)
                        act.wait_ge(s["o_ps"], g + 1)
                        act.activation(ot[:, bass.ds(q, 1), :].rearrange("p a n -> p (a n)"), ps[1][0][:],
                                       ACT.Copy).then_inc(s["ot"], 1)

            @block.tensor
            def _(pe):
                pe.sem_inc(s["vproj"], 1)
                pe.sem_inc(s["x3"], 1)
                pe.wait_ge(s["fixed"], 64)
                with pe.Fori(0, B) as b:
                    with pe.Fori(0, CC) as q:
                        g = b * CC + q
                        pe.wait_ge(s["y"], b * CC + CC)
                        pe.wait_ge(s["w"], g * 16 + 16)
                        for n in range(2):
                            for c in range(CC):
                                mm = pe.matmul(ps[0][n][:], w[:, n, c, :], yt[:, c, :], start=c == 0, stop=c == CC - 1)
                            mm.then_inc(s["qkproj"], 1)
                        for t in range(TT):
                            for c in range(CC):
                                mm = pe.matmul(ps[0][2][:, t * P:(t + 1) * P], yt[:, c, t * P:(t + 1) * P],
                                               w[:, 2, c, :], start=c == 0, stop=c == CC - 1)
                        mm.then_inc(s["vproj"], 1)

                        def scores(i):
                            r = slice(i * D1, (i + 1) * D1)
                            if i == 0:
                                pe.wait_ge(s["qk"], g * 2 + 2)
                            if i == 1:
                                pe.wait_ge(s["v"], g + 1)
                            for bank, tiles in BANK_TILES:
                                for j in tiles:
                                    pe.matmul(cols(ps[bufs(i)], j), qk[r, 0, j * P:(j + 1) * P],
                                              qk[r, 1, 0:P * (j + 1)], start=True, stop=False)
                                    mm = pe.matmul(cols(ps[bufs(i)], j, P * j), k.ident_b[:], k.causal_b[:],
                                                   start=False, stop=True)
                                mm.then_inc(s["scores"], 1)

                        def values(i):
                            h = g * HPC + i
                            for bank, tiles in ((0, (0,)), (1, (1, 3)), (2, (2,))):
                                if bank == 0:
                                    pe.wait_ge(s["expd"], h * TT + TT)
                                for m in tiles:
                                    _, c0 = turned_columns(m)
                                    for j in range(m, TT):
                                        mm = pe.transpose(ps[bufs(i)][bank][:, c0 + (j - m) * P:c0 + (j - m + 1) * P],
                                                          cols(ef[:, bufs(i)], j, m * P, (m + 1) * P), k.ident[:])
                                mm.then_inc(s["turned"], 1)
                            pe.wait_ge(s["t_act"], h + 1)
                            pe.wait_ge(s["t_dve"], h * 2 + 2)
                            for j in range(TT):
                                for m in range(j + 1):
                                    bank, c0 = turned_columns(m)
                                    mm = pe.matmul(pso[i % 2][:, j * D1:(j + 1) * D1],
                                                   tt[:, bufs(i), bank, c0 + (j - m) * P:c0 + (j - m + 1) * P],
                                                   v[:, m, i * D1:(i + 1) * D1], start=m == 0, stop=m == j)
                            mm.then_inc(s["pv"], 1)

                        scores(0)
                        scores(1)
                        for i in range(HPC):
                            values(i)
                            if i + 2 < HPC:
                                scores(i + 2)
                        pe.wait_ge(s["o"], g * HPC + HPC)
                        for t in range(TT):
                            mm = pe.transpose(ps[1][0][:, t * P:(t + 1) * P], ob[:, t, :], k.ident[:])
                        mm.then_inc(s["o_ps"], 1)
                        pe.wait_ge(s["ot"], g + 1)
                    for co in range(CC):
                        if co >= 2:
                            pe.wait_ge(s["x3"], b * CC + co)
                        for c in range(CC):
                            mm = pe.matmul(pso[co % 2][:], wp[:, c, co * P:(co + 1) * P], ot[:, c, :],
                                           start=c == 0, stop=c == CC - 1)
                        mm.then_inc(s["proj"], 1)

            @block.vector
            def _(dve):
                for i in range(2):
                    dve.sem_inc(s[f"x3_stored{i}"], 16)
                dve.wait_ge(s["fixed"], 64)
                dve.tensor_scalar(bq[:], bqk[:, 0, :], SCALE, None, ALU.mult).then_inc(s["bq"], 1)
                with dve.Fori(0, B) as b:
                    for c in range(CC):
                        dve.wait_ge(s["sig"], b * CC + c + 1)
                        i = dve.tensor_tensor(yt[:, c, :], yt[:, c, :], gt[:, c, :], ALU.mult).then_inc(s["y"], 1)
                    with dve.Fori(0, CC) as q:
                        g = b * CC + q
                        dve.wait_ge(s["vproj"], g + 2)
                        dve.tensor_tensor(v[:], ps[0][2][:].rearrange("p (t n) -> p t n", t=TT),
                                          bv[:, bass.ds(q * P, P)].unsqueeze(1).to_broadcast([P, TT, P]),
                                          ALU.add).then_inc(s["v"], 1)

                        def maxima(i):
                            for bank, tiles in BANK_TILES:
                                dve.wait_ge(s["scores"], (g * HPC + i) * 3 + bank + 1)
                                for j in tiles:
                                    m = dve.tensor_reduce(nmax[:, i, j:j + 1], cols(ps[bufs(i)], j), AX, ALU.max,
                                                          negate=True)
                                m.then_inc(s["nmax"], 1)

                        def take(i):
                            h = g * HPC + i
                            for bank, width in ((1, 512), (2, 256)):
                                dve.wait_ge(s["turned"], h * 3 + bank + 1)
                                dve.tensor_copy(tt[:, bufs(i), bank, 0:width],
                                                ps[bufs(i)][bank][:, 0:width]).then_inc(s["t_dve"], 1)
                            dve.reciprocal(rsum[:, i, :], sums[:, i, :]).then_inc(s["rsum"], 1)

                        def out(i):
                            h = g * HPC + i
                            dve.wait_ge(s["pv"], h + 1)
                            dve.wait_ge(s["rsum"], h + 1)
                            dve.tensor_tensor(ob[:, :, i * D1:(i + 1) * D1],
                                              pso[i % 2][:, 0:P].rearrange("p (t n) -> p t n", t=TT),
                                              rsum[:, i, :].unsqueeze(2).to_broadcast([P, TT, D1]),
                                              ALU.mult).then_inc(s["o"], 1)

                        maxima(0)
                        maxima(1)
                        for i in range(HPC):
                            take(i)
                            if i + 2 < HPC:
                                maxima(i + 2)
                            out(i)
                    for co in range(CC):
                        dve.wait_ge(s["proj"], b * CC + co + 1)
                        dve.wait_ge(s[f"x3_stored{co % 2}"], b * 32 + 16 * (co // 2) + 16)
                        dve.scalar_tensor_tensor(out=x3[:, co % 2, :], in0=pso[co % 2][:], scalar=bp[:, co:co + 1],
                                                 in1=xt[:, co, :], op0=ALU.add, op1=ALU.add).then_inc(s["x3"], 1)


def layer1_ffn(k):
    nc, d = k.nc, k.d
    with ExitStack() as ctx:
        def sb(n, s, dt=F32):
            return ctx.enter_context(nc.sbuf_tensor("f_" + n, s, dt))

        stage = sb("stage", [P, 2, F // 2 * CC // 2])
        w0 = sb("w0", [P, 2, CC, F], F16)
        w1 = sb("w1", [P, 2, NF, C], F16)
        b0 = sb("b0", [P, NF])
        b1 = sb("b1", [P, CC])
        xt = sb("xt", [P, CC, T])
        gt = sb("gt", [P, CC, T])
        yf = sb("yf", [P, CC, T])
        y = sb("y", [P, CC, T], F16)
        h = sb("h", [P, NF, T], F16)
        e16 = sb("e16", [P, 2, T], F16)
        xo = sb("xo", [P, 2, T])
        psh = [ctx.enter_context(nc.psum_tensor(f"psf_h{i}", [P, 512], F32)) for i in range(4)]
        pse = [ctx.enter_context(nc.psum_tensor(f"psf_e{i}", [P, 512], F32)) for i in range(2)]
        s = {n: k.sem("f_" + n) for n in (
            "fixed", "raw0", "raw1", "hi", "lo", "x_loaded", "sig", "y", "hid", "gelu", "e_ps", "e16", "xo",
            "stored0", "stored1")}
        PIECE = F // 2 * CC // 2
        w0f = w0[:].rearrange("p s c n -> p s (c n)")
        w1f = w1[:].rearrange("p s c n -> p s (c n)")
        NP = CC * F // PIECE

        def piece(i):
            w, n = (w0f, i) if i < NP else (w1f, i - NP)
            return w[:, 0, n * PIECE:(n + 1) * PIECE], w[:, 1, n * PIECE:(n + 1) * PIECE]

        with nc.Block() as block:

            @block.sync
            def _(sp):
                def raw(i):
                    src = (d["w0"] if i < NP else d["w1"]).rearrange("p c n -> p (c n)")
                    n = i % NP
                    if i >= 2:
                        sp.wait_ge(s["lo"], i - 1)
                    sp.dma_start(stage[:, i % 2, :], src[:, n * PIECE:(n + 1) * PIECE]).then_inc(s[f"raw{i % 2}"], 16)

                sp.dma_start(b0[:], d["b0"]).then_inc(s["fixed"], 16)
                sp.dma_start(b1[:], d["b1"]).then_inc(s["fixed"], 16)
                for i in range(2 * NP):
                    raw(i)
                with sp.Fori(0, B) as b:
                    xsrc = d["x3"][bass.ds(b, 1)].rearrange("a c p n -> p (a c) n")
                    gsrc = d["gain"][3, bass.ds(b, 1)].rearrange("a c p n -> p (a c) n")
                    sp.wait_ge(s["xo"], b * CC + 1)
                    sp.dma_start(xt[:], xsrc).then_inc(s["x_loaded"], 16)
                    sp.dma_start(gt[:], gsrc).then_inc(s["x_loaded"], 16)
                    for co in range(CC):
                        dst = d["out"][bass.ds(b, 1), co].rearrange("a p n -> (a p) n")
                        sp.wait_ge(s["xo"], b * CC + co + 2)
                        sp.dma_start(dst, xo[:, co % 2, :]).then_inc(s[f"stored{co % 2}"], 16)
                for i in range(2):
                    sp.wait_ge(s[f"stored{i}"], 16 + 16 * B * CC // 2)

            @block.scalar
            def _(act):
                for i in range(2 * NP):
                    act.wait_ge(s[f"raw{i % 2}"], 16 * (i // 2 + 1))
                    act.activation(piece(i)[0], stage[:, i % 2, :], ACT.Copy, scale=WSCALE).then_inc(s["hi"], 1)
                act.wait_ge(s["fixed"], 32)
                with act.Fori(0, B) as b:
                    act.wait_ge(s["x_loaded"], b * 32 + 32)
                    for c in range(CC):
                        act.activation(yf[:, c, :], xt[:, c, :], ACT.Sigmoid).then_inc(s["sig"], 1)
                    for n in range(NF):
                        act.wait_ge(s["hid"], b * NF + n + 1)
                        act.activation(h[:, n, :], psh[n % 4][:], ACT.Gelu, bias=b0[:, n:n + 1],
                                       scale=1.0 / WSCALE).then_inc(s["gelu"], 1)
                    for co in range(CC):
                        act.wait_ge(s["e_ps"], b * CC + co + 1)
                        if co >= 2:
                            act.wait_ge(s["xo"], b * CC + co)
                        act.activation(e16[:, co % 2, :], pse[co % 2][:], ACT.Identity, bias=b1[:, co:co + 1],
                                       scale=1.0 / WSCALE).then_inc(s["e16"], 1)

            @block.tensor
            def _(pe):
                pe.sem_inc(s["xo"], 1)
                pe.wait_ge(s["lo"], 2 * NP)
                with pe.Fori(0, B) as b:
                    pe.wait_ge(s["y"], b * CC + CC)
                    for n in range(NF):
                        if n >= 4:
                            pe.wait_ge(s["gelu"], b * NF + n - 3)
                        for c in range(CC):
                            for part in range(2):
                                mm = pe.matmul(psh[n % 4][:], w0[:, part, c, n * P:(n + 1) * P], y[:, c, :],
                                               start=c + part == 0, stop=c == CC - 1 and part == 1)
                        mm.then_inc(s["hid"], 1)
                    pe.wait_ge(s["gelu"], b * NF + NF)
                    for co in range(CC):
                        if co >= 2:
                            pe.wait_ge(s["e16"], b * CC + co - 1)
                        for n in range(NF):
                            for part in range(2):
                                mm = pe.matmul(pse[co % 2][:], w1[:, part, n, co * P:(co + 1) * P], h[:, n, :],
                                               start=n + part == 0, stop=n == NF - 1 and part == 1)
                        mm.then_inc(s["e_ps"], 1)

            @block.vector
            def _(dve):
                for i in range(2):
                    dve.sem_inc(s[f"stored{i}"], 16)
                for i in range(2 * NP):
                    dve.wait_ge(s["hi"], i + 1)
                    hi, lo = piece(i)
                    dve.scalar_tensor_tensor(out=lo, in0=stage[:, i % 2, :], scalar=WSCALE, in1=hi,
                                             op0=ALU.mult, op1=ALU.subtract).then_inc(s["lo"], 1)
                with dve.Fori(0, B) as b:
                    for c in range(CC):
                        dve.wait_ge(s["sig"], b * CC + c + 1)
                        dve.tensor_tensor(y[:, c, :], yf[:, c, :], gt[:, c, :], ALU.mult).then_inc(s["y"], 1)
                    for co in range(CC):
                        dve.wait_ge(s["e16"], b * CC + co + 1)
                        dve.wait_ge(s[f"stored{co % 2}"], b * 32 + 16 * (co // 2) + 16)
                        dve.tensor_tensor(xo[:, co % 2, :], xt[:, co, :], e16[:, co % 2, :],
                                          ALU.add).then_inc(s["xo"], 1)


SCRATCH = {
    "gain": (LAYERS, B, CC, P, T), "x1": (B, CC, P, T), "x2": (B, CC, P, T), "x3": (B, CC, P, T),
    "slot_x": ((SLOT_TILES + 1) * P, C), "slot_y": (SLOT_TILES * P, C),
}


def rotation():
    half = D0 // 2
    inv = np.float32(1.0) / np.float32(10000.0) ** (np.arange(half, dtype=np.float32) / np.float32(half))
    th = np.arange(T, dtype=np.float32)[None, :] * inv[:, None]
    cos, sin = np.cos(th), np.sin(th)
    cos, sin = np.concatenate([cos, cos]), np.concatenate([sin, -sin])
    scale = np.float32(D0 ** -0.5)
    return np.ascontiguousarray(np.stack([cos * scale, sin * scale, cos, sin], 1).astype(np.float32))


def transposed(x):
    return np.ascontiguousarray(np.transpose(x, (0, 2, 1))).reshape(B, CC, P, T)


def layouts(i):
    a = {n: np.asarray(v) for n, v in i.items()}

    def rows(w):
        return np.ascontiguousarray(w.reshape(w.shape[0] // P, P, -1).transpose(1, 0, 2))

    cond = ["L0_cond", "L0_cond2", "L1_cond", "L1_cond2"]
    wu = np.stack([np.stack([a[n + "_" + x] for n in cond]) for x in "wu"])
    wqkv = np.stack([a["L0_attn_W" + x].reshape(CC, P, H0, D0) for x in "qkv"])
    down = np.zeros((E, KI * P, C), np.float32)
    down[:, :I] = a["L0_ffn_down_w"].transpose(0, 2, 1)
    qkv1 = a["L1_attn_w_attn"].reshape(CC, P, 3, CC, P)
    return {
        "xT": transposed(a["x"]),
        "fT": transposed(a["fside_BxSxS_0"]),
        "cond": np.ascontiguousarray(a["cond_512"].reshape(-1)),
        "wu": np.ascontiguousarray(wu.reshape(2, LAYERS, CC, P).transpose(3, 0, 2, 1).reshape(P, 2, CC * LAYERS)),
        "wqkv0": np.ascontiguousarray(wqkv.transpose(3, 2, 0, 1, 4)),
        "wo": np.ascontiguousarray(a["L0_attn_Wo"].reshape(H0, D0, C).transpose(1, 0, 2)),
        "wg": rows(a["L0_attn_Wg"]),
        "rot": rotation(),
        "router": rows(np.ascontiguousarray(a["L0_ffn_router_w"].T)),
        "gate_up": np.ascontiguousarray(np.stack([a["L0_ffn_gate_w"], a["L0_ffn_up_w"]], 1)
                                        .reshape(E, 2, I, CC, P).transpose(4, 0, 1, 3, 2)),
        "down": np.ascontiguousarray(down.reshape(E, KI, P, C).transpose(2, 0, 1, 3)),
        "wqkv1": np.ascontiguousarray(qkv1.transpose(3, 1, 2, 0, 4)),
        "bqkv1": np.ascontiguousarray(a["L1_attn_b_attn"].reshape(3, CC, P).transpose(2, 0, 1)),
        "bv1": np.ascontiguousarray(a["L1_attn_b_attn"].reshape(1, 3, C)[:, 2]),
        "wp1": rows(a["L1_attn_w_proj"]),
        "bp1": np.ascontiguousarray(a["L1_attn_b_proj"].reshape(CC, P).T),
        "w0": rows(np.ascontiguousarray(a["L1_ffn_W0"].T)),
        "b0": np.ascontiguousarray(a["L1_ffn_bias0"].reshape(NF, P).T),
        "w1": rows(np.ascontiguousarray(a["L1_ffn_W1"].T)),
        "b1": np.ascontiguousarray(a["L1_ffn_bias1"].reshape(CC, P).T),
    }


STAGES = [wkv_gain, layer0_attn, moe_route, moe_experts, moe_combine, layer1_attn, layer1_ffn]


def program(nc, dram, stages=None):
    with ExitStack() as ctx:
        k = Core(nc, ctx, dram)
        constants(k)
        for stage in (stages or STAGES):
            stage(k)


def kernel(**inputs):
    import concourse.bacc as bacc
    from concourse.bass_utils import run_bass_kernel_spmd

    nc = bacc.Bacc("TRN2", target_bir_lowering=False, num_devices=1)
    arrays, dram = {}, {}
    for name, a in layouts(inputs).items():
        arrays["in_" + name] = a
        dram[name] = nc.dram_tensor("in_" + name, a.shape, mybir.dt.from_np(a.dtype), kind="ExternalInput").ap()
    for name, shape in SCRATCH.items():
        dram[name] = nc.dram_tensor("scratch_" + name, shape, F32).ap()
    dram["out"] = nc.dram_tensor("out_0", (B, CC, P, T), F32, kind="ExternalOutput").ap()
    program(nc, dram)
    out = run_bass_kernel_spmd(nc, [arrays], core_ids=[0]).results[0]["out_0"]
    return np.ascontiguousarray(np.transpose(out.reshape(B, C, T), (0, 2, 1)))
```

```python
from contextlib import ExitStack

import numpy as np

import concourse.bass as bass
from concourse import mybir

ALU = mybir.AluOpType
ACT = mybir.ActivationFunctionType
AX = mybir.AxisListType.X
F32 = mybir.dt.float32
F16 = mybir.dt.float16
BF16 = mybir.dt.bfloat16
I32 = mybir.dt.int32

P = 128
B, T, C = 4, 512, 512
CC = C // P
TT = T // P
LAYERS = 4
NEG = -1e30
EXP30 = float(np.exp(30.0))

H0, D0 = 16, 128
NBLK, BLK = 8, 64
WIN = 64
H1, D1 = 16, 32
HPC = P // D1
E, I = 8, 352
KI = (I + P - 1) // P
NT = B * TT
SLOT_TILES = NT + E - 1
F = 2048
NF = F // P
WSCALE = 64.0


class Tally:

    def __init__(self, sem, start=0):
        self.sem, self.n, self.base = sem, start, 0

    def inc(self, instruction):
        instruction.then_inc(self.sem, 1)
        self.n += 1
        return self.n


def score_columns(j):
    return {3: (0, 0), 2: (1, 0), 0: (1, 384), 1: (2, 0)}[j]


BANK_TILES = ((0, (3,)), (1, (2, 0)), (2, (1,)))


def turned_columns(m):
    return {0: (0, 0), 1: (1, 0), 3: (1, 384), 2: (2, 0)}[m]


class Core:

    def __init__(self, nc, ctx, dram):
        self.nc, self.ctx, self.d = nc, ctx, dram

    def sem(self, name):
        return self.nc.alloc_semaphore(name=name)

    def scratch(self, name, shape):
        return self.nc.dram_tensor(name, shape, F32).ap()


def constants(k):
    nc, ctx = k.nc, k.ctx
    k.ident = ctx.enter_context(nc.sbuf_tensor("ident", [P, P], F32))
    k.ident_b = ctx.enter_context(nc.sbuf_tensor("ident_b", [P, P], BF16))
    k.causal_b = ctx.enter_context(nc.sbuf_tensor("causal_b", [P, P], BF16))
    k.slot = ctx.enter_context(nc.sbuf_tensor("slot", [P, NT], I32))
    k.weight = ctx.enter_context(nc.sbuf_tensor("weight", [P, NT], F32))
    k.tile_expert = ctx.enter_context(nc.sbuf_tensor("tile_expert", [P, SLOT_TILES], I32))
    made = k.sem("const_made")
    with nc.Block() as block:

        @block.gpsimd
        def _(pool):
            pool.memset(k.ident[:], 0.0).then_inc(made, 1)
            pool.memset(k.ident_b[:], 0.0).then_inc(made, 1)
            pool.memset(k.causal_b[:], 0.0).then_inc(made, 1)
            pool.wait_ge(made, 3)
            for m in (k.ident, k.ident_b):
                pool.affine_select(out=m[:], in_=m[:], compare_op=ALU.not_equal, fill=1.0, base=0,
                                   pattern=[[-1, P]], channel_multiplier=1).then_inc(made, 1)
            pool.affine_select(out=k.causal_b[:], in_=k.causal_b[:], compare_op=ALU.is_ge, fill=NEG,
                               base=0, pattern=[[-1, P]], channel_multiplier=1).then_inc(made, 1)


class Wkv:

    def __init__(self, k, ctx, name, tiles):
        nc = k.nc
        self.k, self.tiles = k, tiles

        def sb(n, s):
            return ctx.enter_context(nc.sbuf_tensor(f"{name}_{n}", s, F32))

        self.kt = [sb(f"kt{i}", [P, T]) for i in range(tiles)]
        self.ek_raw, self.ek, self.ekv = sb("ek_raw", [P, T]), sb("ek", [P, T]), sb("ekv", [P, T])
        self.euk_raw, self.euk, self.eukv = sb("euk_raw", [P, T]), sb("euk", [P, T]), sb("eukv", [P, T])
        self.nf, self.df = sb("nf", [P, T + 1]), sb("df", [P, T + 1])
        self.nb, self.db = sb("nb", [P, T]), sb("db", [P, T])
        self.num, self.den = sb("num", [P, T]), sb("den", [P, T])
        self.lnd, self.r0, self.gain = sb("lnd", [P, T]), sb("r0", [P, T]), sb("gain", [P, T])
        self.s = {n: k.sem(f"{name}_{n}") for n in (
            "ek_raw", "ek", "ekv", "euk_raw", "euk", "eukv", "scan", "part", "joined", "den", "ln", "r0",
            "newton", "gain", "stored", "zeroed")}
        self.loaded = [k.sem(f"{name}_loaded{i}") for i in range(tiles)]

    def source(self, b, c):
        return self.k.d["fT"][bass.ds(b, 1), bass.ds(c, 1)].rearrange("a c p n -> (a c p) n")

    def act_load(self, act, tile, b, c, units_done):
        src = self.source(b, c)
        if units_done is not None:
            act.wait_ge(self.s["eukv"], units_done)
        act.dma_start(self.kt[tile][:], src).then_inc(self.loaded[tile], 16)

    def act_prepare(self, act, tile, u, n, p=None, loads=None):
        if p is not None:
            act.wait_ge(self.loaded[tile], loads * 16)
            act.wait_ge(self.s["ek"], p)
            act.activation(self.ek_raw[:], self.kt[tile][:], ACT.Exp).then_inc(self.s["ek_raw"], 1)
        act.wait_ge(self.s["euk"], u)
        act.activation(self.euk_raw[:], self.kt[tile][:], ACT.Exp,
                       bias=self.k.wu[:, 1, bass.ds(n, 1)]).then_inc(self.s["euk_raw"], 1)

    def act_invert(self, act, u):
        act.wait_ge(self.s["den"], u + 1)
        act.activation(self.lnd[:], self.den[:], ACT.Ln).then_inc(self.s["ln"], 1)
        act.wait_ge(self.s["ln"], u + 1)
        act.activation(self.r0[:], self.lnd[:], ACT.Exp, scale=-1.0).then_inc(self.s["r0"], 1)

    def act_store(self, act, u, layer, b, c):
        dst = self.k.d["gain"][layer, bass.ds(b, 1), bass.ds(c, 1)].rearrange("a c p n -> (a c p) n")
        act.wait_ge(self.s["gain"], u + 1)
        act.dma_start(dst, self.gain[:]).then_inc(self.s["stored"], 16)

    def pool_prepare(self, pool, tile, u, p=None):
        s = self.s
        if p is not None:
            pool.wait_ge(s["ek"], p + 1)
            pool.tensor_tensor(self.ekv[:], self.ek[:], self.kt[tile][:], ALU.mult).then_inc(s["ekv"], 1)
        pool.wait_ge(s["euk"], u + 1)
        pool.tensor_tensor(self.eukv[:], self.euk[:], self.kt[tile][:], ALU.mult).then_inc(s["eukv"], 1)

    def pool_join(self, pool, u):
        s = self.s
        pool.wait_ge(s["part"], u + 1)
        pool.tensor_tensor(self.den[:], self.den[:], self.euk[:], ALU.add).then_inc(s["joined"], 1)
        pool.wait_ge(s["eukv"], u + 1)
        pool.tensor_tensor(self.num[:], self.num[:], self.eukv[:], ALU.add).then_inc(s["joined"], 1)

    def dve_zero(self, dve):
        dve.memset(self.nf[:, 0:1], 0.0)
        dve.memset(self.df[:, 0:1], 0.0).then_inc(self.s["zeroed"], 1)
        dve.wait_ge(self.s["zeroed"], 1)

    def dve_prepare(self, dve, u, p=None):
        s = self.s
        if p is not None:
            dve.wait_ge(s["ek_raw"], p + 1)
            dve.tensor_scalar(self.ek[:], self.ek_raw[:], EXP30, None, ALU.min).then_inc(s["ek"], 1)
        dve.wait_ge(s["euk_raw"], u + 1)
        dve.tensor_scalar(self.euk[:], self.euk_raw[:], EXP30, None, ALU.min).then_inc(s["euk"], 1)

    def dve_sums(self, dve, u, b, n, p):
        s = self.s
        dec = self.k.decay[:, bass.ds(b, 1), bass.ds(n, 1)].rearrange("p a n -> p (a n)")
        dect = dec.to_broadcast([P, T])
        if not (isinstance(u, int) and u == 0):
            dve.wait_ge(s["gain"], u)
        for step, (src, fw, bw) in enumerate(((self.ek, self.df, self.db), (self.ekv, self.nf, self.nb))):
            dve.wait_ge(s["ekv" if step else "ek"], p + 1)
            dve.tensor_tensor_scan(fw[:, 1:T + 1], dect, src[:], 0.0, ALU.mult, ALU.add)
            dve.tensor_tensor_scan(bw[:, ::-1], dect, src[:, ::-1], 0.0, ALU.mult, ALU.add).then_inc(s["scan"], 1)
        for step, (out, fw, bw) in enumerate(((self.den, self.df, self.db), (self.num, self.nf, self.nb))):
            dve.wait_ge(s["scan"], u * 2 + 1 + step)
            i = dve.scalar_tensor_tensor(out=out[:], in0=fw[:, 0:T], scalar=dec, in1=bw[:],
                                         op0=ALU.mult, op1=ALU.add)
        i.then_inc(s["part"], 1)

    def dve_guard(self, dve, u):
        dve.wait_ge(self.s["joined"], u * 2 + 2)
        dve.tensor_scalar(self.den[:], self.den[:], 1e-8, None, ALU.max).then_inc(self.s["den"], 1)

    def dve_finish(self, dve, u, b, stores):
        s = self.s
        dve.wait_ge(s["r0"], u + 1)
        dve.tensor_tensor(self.db[:], self.den[:], self.r0[:], ALU.mult).then_inc(s["newton"], 1)
        dve.wait_ge(s["newton"], u * 2 + 1)
        dve.scalar_tensor_tensor(out=self.nb[:], in0=self.db[:], scalar=-2.0, in1=self.r0[:],
                                 op0=ALU.add, op1=ALU.mult).then_inc(s["newton"], 1)
        dve.wait_ge(s["newton"], u * 2 + 2)
        if not (isinstance(stores, int) and stores == 0):
            dve.wait_ge(s["stored"], stores * 16)
        dve.scalar_tensor_tensor(out=self.gain[:], in0=self.num[:], scalar=self.k.negf[:, bass.ds(b, 1)],
                                 in1=self.nb[:], op0=ALU.mult, op1=ALU.mult).then_inc(s["gain"], 1)


def wkv_setup(k):
    nc, d, ctx = k.nc, k.d, k.ctx
    UNITS = CC * LAYERS
    k.wu = ctx.enter_context(nc.sbuf_tensor("wu", [P, 2, UNITS], F32))
    k.decay = ctx.enter_context(nc.sbuf_tensor("decay", [P, B, UNITS], F32))
    k.negf = ctx.enter_context(nc.sbuf_tensor("negf", [P, B], F32))
    with ExitStack() as tmp:
        def sb(n, s):
            return tmp.enter_context(nc.sbuf_tensor("ws_" + n, s, F32))

        cond = sb("cond", [P, B, P])
        csum, tf, halff = sb("csum", [P, B]), sb("tf", [P, B]), sb("halff", [P, B])
        ew, dk = sb("ew", [P, UNITS]), sb("dk", [P, UNITS])
        loaded, act_step, dve_step = k.sem("ws_loaded"), k.sem("ws_act_step"), k.sem("ws_dve_step")
        with nc.Block() as block:

            @block.sync
            def _(sp):
                sp.dma_start(k.wu[:], d["wu"]).then_inc(loaded, 16)
                sp.dma_start(cond[:].rearrange("p b n -> p (b n)"),
                             d["cond"].partition_broadcast(P)).then_inc(loaded, 16)

            @block.scalar
            def _(act):
                act.wait_ge(loaded, 32)
                act.activation(ew[:], k.wu[:, 0, :], ACT.Exp).then_inc(act_step, 1)
                act.wait_ge(act_step, 1)
                act.activation(dk[:], ew[:], ACT.Exp, scale=-1.0).then_inc(act_step, 1)
                act.wait_ge(dve_step, 1)
                act.activation(tf[:], csum[:], ACT.Sigmoid).then_inc(act_step, 1)
                act.preload_act_table_set("natural_log_exp_and_others")

            @block.vector
            def _(dve):
                dve.wait_ge(loaded, 32)
                dve.tensor_reduce(csum[:], cond[:], AX, ALU.add).then_inc(dve_step, 1)
                dve.wait_ge(act_step, 3)
                dve.tensor_scalar(halff[:], tf[:], 0.5, 0.5, ALU.mult, ALU.add).then_inc(dve_step, 1)
                dve.tensor_scalar(k.negf[:], tf[:], -0.2, -0.8, ALU.mult, ALU.add).then_inc(dve_step, 1)
                dve.wait_ge(dve_step, 3)
                for i in range(B):
                    dve.tensor_scalar(k.decay[:, i, :], dk[:], halff[:, i:i + 1], None,
                                      ALU.mult).then_inc(dve_step, 1)
                dve.wait_ge(dve_step, 3 + B)


def layer0_attn(k):
    nc, d = k.nc, k.d
    G = H0 // CC
    with ExitStack() as ctx:
        def sb(n, s, dt=F32):
            return ctx.enter_context(nc.sbuf_tensor("a0_" + n, s, dt))

        wraw = sb("wraw", [P, 3, CC, D0])
        w16 = sb("w16", [P, 2, 2, 3, CC, D0], F16)
        wo16 = sb("wo16", [P, 2, CC, G, C], F16)
        wg = sb("wg", [P, CC, 3 * H0])
        wg16 = sb("wg16", [P, 2, CC, 3 * H0], F16)
        rot = sb("rot", [P, 4, T])
        xc = sb("xc", [P, T])
        sg = sb("sg", [P, T])
        yf = sb("yf", [P, T])
        y16 = sb("y16", [P, 2, CC, T], F16)
        ynext = sb("ynext", [P, 2, CC, T], F16)
        of = sb("of", [P, T])
        o16 = sb("o16", [P, 2, 2, G, T], F16)
        acc = sb("acc", [P, CC, T])
        ra = sb("ra", [P, 2, T])
        rb = sb("rb", [P, 2, T])
        qk = sb("qk", [P, 2, T])
        ksum = sb("ksum", [P, NBLK])
        v = sb("v", [P, 2, TT, D0])
        gate_raw = sb("gate_raw", [P, TT, 3 * H0])
        gate = sb("gate", [P, H0, 3, TT])
        seen = sb("seen", [P, TT])
        wmask = sb("wmask", [P, 3 * BLK])
        cmask = sb("cmask", [P, TT, NBLK])
        nmax = sb("nmax", [P, 2, TT])
        cmax = sb("cmax", [P, TT])
        sums = sb("sums", [P, 3, TT])
        rsum = sb("rsum", [P, 3, TT])
        coef = sb("coef", [P, 3, TT])
        ef = sb("ef", [P, 3, 512])
        sw = sb("sw", [P, TT, 3 * BLK])
        ewn = sb("ewn", [P, TT, 3 * BLK])
        sc = sb("sc", [P, TT, NBLK])
        sc2 = sb("sc2", [P, TT, NBLK])
        ec = sb("ec", [P, TT, NBLK])
        pc = sb("pc", [P, TT, NBLK])
        pt = sb("pt", [P, 3, 512])
        tt_ = sb("tt_", [P, 3, 512])
        ps = [ctx.enter_context(nc.psum_tensor(f"ps0_s{i}", [P, 512], F32)) for i in range(3)]
        psq = [ctx.enter_context(nc.psum_tensor(f"ps0_q{i}", [P, 512], F32)) for i in range(2)]
        psv = ctx.enter_context(nc.psum_tensor("ps0_v", [P, 512], F32))
        pso = ctx.enter_context(nc.psum_tensor("ps0_o", [P, 512], F32))
        psg = ctx.enter_context(nc.psum_tensor("ps0_g", [P, 512], F32))
        s = {n: k.sem("a0_" + n) for n in (
            "const", "wraw", "w64", "whi", "wlo", "rot", "wg_loaded", "wg64", "wg_hi", "wg_lo",
            "x_loaded", "sig_step", "sig", "yf", "yhi", "ylo", "y_moved", "gates_raw", "gates_step",
            "gates_sig", "gates", "qproj", "cosed", "swapped", "roped", "q_sb", "ksum", "vproj", "v_sb", "scores",
            "nmax", "expd", "cmp_step", "cmp_e", "coef", "p_step", "p", "turned", "t_sb", "pv", "of", "o_hi", "o_lo",
            "wo_raw0", "wo_raw1", "wo64", "wo_hi", "wo_lo", "out_ps", "acc", "acc_loaded", "x1_stored")}
        CMP_STEPS = 5
        wkv = Wkv(k, ctx, "wkv0", 2)
        wo_raw = (acc, sb("wo_raw", [P, G, C]))
        PER = 3

        def cols(t, j, lo=0, hi=None):
            bank, c0 = score_columns(j)
            hi = P * (j + 1) if hi is None else hi
            return t[bank][:, c0 + lo:c0 + hi] if isinstance(t, list) else t[:, bank, c0 + lo:c0 + hi]

        def win(t, j):
            return cols(t, j, max(0, P * j - WIN))

        def wcols(t, j):
            lo = 0 if j else WIN
            return t[:, j, lo:] if len(t.shape) == 3 else t[:, lo:]

        def ynew(part, c):
            return ynext[:, part, bass.ds(c, 1), :].rearrange("p a n -> p (a n)")

        def wo_part(part, c):
            return wo16[:, part, bass.ds(c, 1)].rearrange("p a h n -> p (a h) n")

        def o_part(group, part, i):
            return o16[:, bass.ds(group, 1), part, i, :].rearrange("p a n -> p (a n)")

        def group_units(b, c):
            return (b * CC + c) * PER + CC, (b * CC + c) * 2 + CC

        def run(eng, group, last):
            group(0, 0, True, False)
            with eng.Fori(1, CC) as c:
                group(0, c, False, False)
            with eng.Fori(1, B) as b:
                group(b, 0, True, True)
                with eng.Fori(1, CC) as c:
                    group(b, c, False, False)
            last()

        with nc.Block() as block:

            @block.sync
            def _(sp):
                def weights(g, h):
                    src = d["wqkv0"][bass.ds(h, 1)].rearrange("a p k c n -> p (a k) c n")
                    sp.wait_ge(s["wlo"], g)
                    sp.dma_start(wraw[:], src).then_inc(s["wraw"], 16)

                def x_chunk(b, c, n):
                    src = d["xT"][bass.ds(b, 1), bass.ds(c, 1)].rearrange("a c p n -> (a c p) n")
                    sp.wait_ge(s["sig"], n)
                    sp.dma_start(xc[:], src).then_inc(s["x_loaded"], 16)

                def move_y(b):
                    if isinstance(b, int):
                        sp.wait_ge(s["ylo"], CC)
                    else:
                        sp.wait_ge(s["vproj"], b * H0)
                    sp.dma_start(y16[:], ynext[:]).then_inc(s["y_moved"], 16)

                def residual(b, co, n):
                    src = d["xT"][bass.ds(b, 1), co].rearrange("a p n -> (a p) n")
                    if n is not None:
                        sp.wait_ge(s["x1_stored"], n * 16)
                    sp.dma_start(acc[:, co, :], src).then_inc(s["acc_loaded"], 16)

                def store(b, co):
                    dst = d["x1"][bass.ds(b, 1), co].rearrange("a p n -> (a p) n")
                    sp.wait_ge(s["acc"], (b * CC + (CC - 1)) * CC + co + 1)
                    sp.dma_start(dst, acc[:, co, :]).then_inc(s["x1_stored"], 16)

                def group(b, c, first, output_before):
                    if output_before:
                        move_y(b)
                    for i in range(G):
                        weights(b * H0 + c * G + (i + 2), (c * G + (i + 2)) % H0)
                        if i == 0:
                            x_chunk((b + 1) % B, c, (b + 1) * CC + c)
                        if output_before:
                            store(b - 1, i)
                            residual(b, i, (b - 1) * CC + (i + 1))

                def wo_load(c):
                    sp.dma_start(wo_raw[c % 2][:], d["wo"][:, c * G:(c + 1) * G]).then_inc(s[f"wo_raw{c % 2}"], 16)

                sp.dma_start(wg[:], d["wg"]).then_inc(s["wg_loaded"], 16)
                x_chunk(0, 0, 0)
                weights(0, 0)
                sp.dma_start(rot[:], d["rot"]).then_inc(s["rot"], 16)
                wo_load(0)
                wo_load(1)
                x_chunk(0, 1, 1)
                weights(1, 1)
                for c in range(2, CC):
                    x_chunk(0, c, c)
                    sp.wait_ge(s["wo_lo"], c - 1)
                    wo_load(c)
                move_y(0)
                sp.wait_ge(s["wo_lo"], CC - 1)
                for co in range(CC):
                    residual(0, co, None)
                run(sp, group, lambda: [store(B - 1, co) for co in range(CC)])
                sp.wait_ge(s["x1_stored"], 16 * B * CC)

            @block.gpsimd
            def _(pool):
                pool.memset(wmask[:], 0.0).then_inc(s["const"], 1)
                pool.memset(cmask[:], 0.0).then_inc(s["const"], 1)
                pool.memset(seen[:], 1.0 / BLK).then_inc(s["const"], 1)
                pool.wait_ge(s["const"], 3)
                pool.affine_select(out=wmask[:], in_=wmask[:], compare_op=ALU.is_ge, fill=NEG, base=0,
                                   pattern=[[1, 3 * BLK]], channel_multiplier=-1).then_inc(s["const"], 1)
                pool.wait_ge(s["const"], 4)
                pool.affine_select(out=wmask[:], in_=wmask[:], compare_op=ALU.is_ge, fill=NEG, base=WIN,
                                   pattern=[[-1, 3 * BLK]], channel_multiplier=1).then_inc(s["const"], 1)
                pool.affine_select(out=cmask[:], in_=cmask[:], compare_op=ALU.is_ge, fill=NEG, base=1 - BLK,
                                   pattern=[[P, TT], [-BLK, NBLK]], channel_multiplier=1).then_inc(s["const"], 1)
                pool.affine_select(out=seen[:], in_=seen[:], compare_op=ALU.is_ge, fill=0.0, base=1 - BLK,
                                   pattern=[[P, TT]], channel_multiplier=1).then_inc(s["const"], 1)

                def y_low(c, n):
                    pool.wait_ge(s["yhi"], n + 1)
                    pool.tensor_tensor(ynew(1, c), yf[:], ynew(0, c), ALU.subtract).then_inc(s["ylo"], 1)

                def o_low(g, group, i):
                    pool.wait_ge(s["o_hi"], g + 1)
                    pool.tensor_tensor(o_part(group, 1, i), of[:], o_part(group, 0, i), ALU.subtract).then_inc(s["o_lo"], 1)

                def split(g, i):
                    pool.wait_ge(s["whi"], g + 1)
                    pool.tensor_tensor(w16[:, i, 1], wraw[:], w16[:, i, 0], ALU.subtract).then_inc(s["wlo"], 1)

                def rope(g, n):
                    pool.wait_ge(s["swapped"], g * 2 + n + 1)
                    pool.tensor_tensor(rb[:, n, :], rb[:, n, :], rot[:, 2 * n + 1, :],
                                       ALU.mult).then_inc(s["roped"], 1)
                    pool.wait_ge(s["cosed"], g * 2 + n + 1)
                    pool.wait_ge(s["roped"], g * 2 + n + 1)
                    pool.tensor_tensor(qk[:, n, :], ra[:, n, :], rb[:, n, :], ALU.add).then_inc(s["q_sb"], 1)

                pool.wait_ge(s["wg_hi"], 1)
                pool.tensor_tensor(wg16[:, 1], wg[:], wg16[:, 0], ALU.subtract).then_inc(s["wg_lo"], 1)
                wkv.pool_prepare(pool, 0, 0, 0)
                for c in range(CC):
                    wkv.pool_join(pool, c)
                    wkv.pool_prepare(pool, (c + 1) % 2, c + 1, c + 1)
                    if c < 2:
                        split(c, c)
                    if c == CC - 1:
                        y_low(c, c)
                    pool.wait_ge(s["wo_hi"], c + 1)
                    pool.tensor_tensor(wo_part(1, c), wo_raw[c % 2][:], wo_part(0, c),
                                       ALU.subtract).then_inc(s["wo_lo"], 1)
                    if c < CC - 1:
                        y_low(c, c)

                def group(b, c, first, output_before):
                    u, p = group_units(b, c)
                    for i in range(G):
                        g = b * H0 + c * G + i
                        rope(g, 1)
                        if i == 1:
                            y_low(c, (b + 1) * CC + c)
                        if i == 0 and (output_before or not first):
                            o_low(g - 1, (b * CC + c + 1) % 2, G - 1)
                        if i < PER:
                            wkv.pool_join(pool, u + i)
                        if i:
                            o_low(g - 1, (b * CC + c) % 2, i - 1)
                        if i == 0:
                            wkv.pool_prepare(pool, 1, u + 1, p + 1)
                        if i == 1:
                            wkv.pool_prepare(pool, 1, u + 2)
                        if i == 3:
                            wkv.pool_prepare(pool, 0, u + 3, p + 2)
                        rope(g + 1, 0)
                        split(g + 2, i % 2)

                rope(0, 0)
                run(pool, group, lambda: o_low(B * H0 - 1, (B * CC - 1) % 2, G - 1))

            @block.scalar
            def _(act):
                def split(g, i):
                    act.wait_ge(s["wraw"], g * 16 + 16)
                    act.activation(wraw[:], wraw[:], ACT.Copy, scale=WSCALE).then_inc(s["w64"], 1)
                    act.wait_ge(s["w64"], g + 1)
                    act.activation(w16[:, i, 0], wraw[:], ACT.Copy).then_inc(s["whi"], 1)

                def sigmoid(out, x, steps, before, done, scale=-1.0):
                    act.activation(out, x, ACT.Exp, scale=scale).then_inc(steps, 1)
                    act.wait_ge(steps, before + 1)
                    act.activation(out, out, ACT.Ln, bias=1.0).then_inc(steps, 1)
                    act.wait_ge(steps, before + 2)
                    act.activation(out, out, ACT.Exp, scale=-1.0).then_inc(done, 1)

                def y_sigmoid(n):
                    act.wait_ge(s["x_loaded"], n * 16 + 16)
                    act.wait_ge(s["yf"], n)
                    sigmoid(sg[:], xc[:], s["sig_step"], n * 2, s["sig"])

                def y_high(c, n):
                    act.wait_ge(s["yf"], n + 1)
                    act.activation(ynew(0, c), yf[:], ACT.Copy).then_inc(s["yhi"], 1)

                for tile in range(2):
                    wkv.act_load(act, tile, 0, tile, None)
                act.wait_ge(s["wg_loaded"], 16)
                act.activation(wg[:], wg[:], ACT.Copy, scale=WSCALE).then_inc(s["wg64"], 1)
                act.wait_ge(s["wg64"], 1)
                act.activation(wg16[:, 0], wg[:], ACT.Copy).then_inc(s["wg_hi"], 1)
                wkv.act_prepare(act, 0, 0, 0, 0, 1)
                for c in range(CC):
                    y_sigmoid(c)
                    wkv.act_load(act, c % 2, *((0, c + 2) if c + 2 < CC else (1 - c % 2, 0)), c + 1)
                    wkv.act_prepare(act, (c + 1) % 2, c + 1, (c + 1) % CC * LAYERS, c + 1, (c + 1) // 2 + 1)
                    wkv.act_invert(act, c)
                    if c < 2:
                        split(c, c)
                    if c == CC - 1:
                        y_high(c, c)
                    act.wait_ge(s[f"wo_raw{c % 2}"], c // 2 * 16 + 16)
                    act.activation(wo_raw[c % 2][:], wo_raw[c % 2][:], ACT.Copy, scale=WSCALE).then_inc(s["wo64"], 1)
                    act.wait_ge(s["wo64"], c + 1)
                    act.activation(wo_part(0, c), wo_raw[c % 2][:], ACT.Copy).then_inc(s["wo_hi"], 1)
                    if c < CC - 1:
                        y_high(c, c)

                def swap(g, n):
                    act.wait_ge(s["cosed"], g * 2 + n + 1)
                    act.activation(rb[0:64, n, :], psq[n][64:P, :], ACT.Copy)
                    act.activation(rb[64:P, n, :], psq[n][0:64, :], ACT.Copy).then_inc(s["swapped"], 1)

                def exps(g):
                    for bank, tiles in BANK_TILES:
                        act.wait_ge(s["nmax"], g * 3 + bank + 1)
                        for j in tiles:
                            act.activation(cols(ef, j), cols(ps, j), ACT.Exp, bias=nmax[:, 0, j:j + 1],
                                           accum_out=sums[:, 1, j:j + 1]).then_inc(s["expd"], 1)
                            act.activation(wcols(ewn, j), wcols(sw, j), ACT.Exp, bias=nmax[:, 1, j:j + 1],
                                           scale=-1.0, accum_out=sums[:, 2, j:j + 1]).then_inc(s["expd"], 1)
                    act.wait_ge(s["cmp_step"], g * CMP_STEPS + 2)
                    act.activation(ec[:], sc2[:], ACT.Exp).then_inc(s["cmp_e"], 1)

                def turn(g, group, i):
                    for m in range(3):
                        act.wait_ge(s["turned"], g * 3 + m + 1)
                        w = 256 if m == 2 else 512
                        act.activation(tt_[:, m, 0:w], ps[m][:, 0:w], ACT.Copy).then_inc(s["t_sb"], 1)
                    act.wait_ge(s["pv"], g + 1)
                    act.wait_ge(s["o_lo"], g)
                    act.activation(of[:], pso[:], ACT.Copy).then_inc(s["of"], 1)
                    act.wait_ge(s["of"], g + 1)
                    act.activation(o_part(group, 0, i), of[:], ACT.Copy).then_inc(s["o_hi"], 1)

                def group(b, c, first, output_before):
                    u, p = group_units(b, c)
                    for i in range(G):
                        g = b * H0 + c * G + i
                        if first and i == 0:
                            act.wait_ge(s["gates_raw"], b + 1)
                            sigmoid(gate_raw[:], psg[:, 0:TT * 3 * H0].rearrange("p (t n) -> p t n", t=TT),
                                    s["gates_step"], b * 2, s["gates_sig"], -1.0 / WSCALE)
                        swap(g, 1)
                        act.wait_ge(s["vproj"], g + 1)
                        act.activation(v[:, i % 2].rearrange("p t n -> p (t n)"), psv[:], ACT.Copy,
                                       scale=1.0 / WSCALE).then_inc(s["v_sb"], 1)
                        if i or output_before or not first:
                            turn(g - 1, (b * CC + c + (i == 0)) % 2, (i + G - 1) % G)
                        it = b * CC + c
                        if i == 0:
                            wkv.act_prepare(act, 1, u + 1, c * LAYERS + 1, p + 1, it + 3)
                        if i == 1:
                            wkv.act_prepare(act, 1, u + 2, c * LAYERS + 2)
                            act.wait_ge(s["y_moved"], b * 16 + 16)
                            y_high(c, (b + 1) * CC + c)
                        if i == 3:
                            wkv.act_prepare(act, 0, u + 3, (c + 1) % CC * LAYERS, p + 2, it + 4)
                        exps(g)
                        swap(g + 1, 0)
                        if i < PER:
                            wkv.act_invert(act, u + i)
                        split(g + 2, i % 2)
                        if i == 0:
                            y_sigmoid((b + 1) * CC + c)
                            wkv.act_load(act, 0, ((it + 1) // CC + 1) % B, (it + 1) % CC, u + 1)
                        if i == 2:
                            wkv.act_store(act, u + 1, 1, b, c)
                            wkv.act_load(act, 1, (it + 1) // CC % B, (it + 1) % CC, u + 3)
                        if i == 3:
                            wkv.act_store(act, u + 2, 2, b, c)

                swap(0, 0)
                run(act, group, lambda: turn(B * H0 - 1, (B * CC - 1) % 2, G - 1))
                act.wait_ge(wkv.s["stored"], 16 * 2 * B * CC)
                for tile, loads in enumerate((B * CC + 3, B * CC + 3)):
                    act.wait_ge(wkv.loaded[tile], loads * 16)

            @block.tensor
            def _(pe):
                PARTS = ((0, 0), (0, 1), (1, 0))

                def gates(b):
                    pe.wait_ge(s["y_moved"], b * 16 + 16)
                    for t in range(TT):
                        for c in range(CC):
                            for n, (yp, wp) in enumerate(PARTS):
                                mm = pe.matmul(psg[:, t * 48:t * 48 + 48], y16[:, yp, c, t * P:(t + 1) * P],
                                               wg16[:, wp, c, :], start=c + n == 0, stop=c == CC - 1 and n == 2)
                    mm.then_inc(s["gates_raw"], 1)

                def project(g, i):
                    pe.wait_ge(s["wlo"], g + 1)
                    for n in range(2):
                        for c in range(CC):
                            for m, (yp, wp) in enumerate(PARTS):
                                mm = pe.matmul(psq[n][:], w16[:, i % 2, wp, n, c, :], y16[:, yp, c, :],
                                               start=c + m == 0, stop=c == CC - 1 and m == 2)
                        mm.then_inc(s["qproj"], 1)
                    pe.wait_ge(s["v_sb"], g)
                    for t in range(TT):
                        for c in range(CC):
                            for m, (yp, wp) in enumerate(PARTS):
                                mm = pe.matmul(psv[:, t * D0:(t + 1) * D0], y16[:, yp, c, t * P:(t + 1) * P],
                                               w16[:, i % 2, wp, 2, c, :], start=c + m == 0, stop=c == CC - 1 and m == 2)
                    mm.then_inc(s["vproj"], 1)

                def scores(g):
                    pe.wait_ge(s["q_sb"], g * 2 + 2)
                    for bank, tiles in BANK_TILES:
                        for j in tiles:
                            pe.matmul(cols(ps, j), qk[:, 0, j * P:(j + 1) * P], qk[:, 1, 0:P * (j + 1)],
                                      start=True, stop=False)
                            mm = pe.matmul(cols(ps, j, P * j), k.ident_b[:], k.causal_b[:],
                                           start=False, stop=True)
                        if bank == 2:
                            pe.wait_ge(s["ksum"], g + 1)
                            for j in range(TT):
                                mm = pe.matmul(ps[2][:, 256 + j * NBLK:256 + (j + 1) * NBLK],
                                               qk[:, 0, j * P:(j + 1) * P], ksum[:], start=True, stop=True)
                        mm.then_inc(s["scores"], 1)

                def values(g, i):
                    for bank, tiles in ((0, (0,)), (1, (1, 3)), (2, (2,))):
                        if bank == 0:
                            pe.wait_ge(s["p"], g * TT + TT)
                        for m in tiles:
                            _, c0 = turned_columns(m)
                            for j in range(m, TT):
                                mm = pe.transpose(ps[bank][:, c0 + (j - m) * P:c0 + (j - m + 1) * P],
                                                  cols(pt, j, m * P, (m + 1) * P), k.ident[:])
                        mm.then_inc(s["turned"], 1)
                    for n, m in enumerate((0, 1, 3, 2)):
                        bank, c0 = turned_columns(m)
                        if n == 0:
                            pe.wait_ge(s["of"], g)
                        pe.wait_ge(s["t_sb"], g * 3 + bank + 1)
                        mm = pe.matmul(pso[:, m * P:], v[:, i % 2, m, :], tt_[:, bank, c0:c0 + T - m * P],
                                       start=n == 0, stop=n == TT - 1)
                    mm.then_inc(s["pv"], 1)

                def output(group, og, c, co):
                    if co == 0:
                        pe.wait_ge(s["o_lo"], group * G + G)
                    if not (isinstance(group, int) and group == 0 and co == 0):
                        pe.wait_ge(s["acc"], group * CC + co)
                    for h in range(G):
                        for m, (op, wp) in enumerate(PARTS):
                            mm = pe.matmul(psg[:], wo16[:, wp, bass.ds(c, 1), h, co * P:(co + 1) * P]
                                           .rearrange("p a n -> p (a n)"),
                                           o_part(og, op, h), start=h + m == 0, stop=h == G - 1 and m == 2)
                    mm.then_inc(s["out_ps"], 1)

                def group(b, c, first, output_before):
                    it = b * CC + c
                    og, oc = (it + 1) % 2, (c + (CC - 1)) % CC
                    for i in range(G):
                        g = b * H0 + c * G + i
                        before = output_before or not first
                        if first and i == 0:
                            if output_before:
                                pe.wait_ge(s["acc"], (it - 1) * CC)
                            gates(b)
                        project(g, i)
                        if i and before:
                            output(it - 1, og, oc, i)
                        if i or before:
                            values(g - 1, i + G - 1)
                        scores(g)
                        if i == 0 and before:
                            if first:
                                pe.wait_ge(s["gates_sig"], b + 1)
                            output(it - 1, og, oc, 0)

                def last():
                    pe.sem_inc(s["qproj"], 1)
                    values(B * H0 - 1, G - 1)
                    for co in range(CC):
                        output(B * CC - 1, (B * CC - 1) % 2, CC - 1, co)

                pe.wait_ge(s["wg_lo"], 1)
                run(pe, group, last)

            @block.vector
            def _(dve):
                wkv.dve_zero(dve)

                def condition(n):
                    dve.wait_ge(s["sig"], n + 1)
                    dve.wait_ge(s["ylo"], n)
                    dve.tensor_tensor(yf[:], sg[:], wkv.gain[:], ALU.mult).then_inc(s["yf"], 1)

                wkv.dve_prepare(dve, 0, 0)
                for c in range(CC):
                    wkv.dve_sums(dve, c, 0, c * LAYERS, c)
                    wkv.dve_guard(dve, c)
                    wkv.dve_prepare(dve, c + 1, c + 1)
                    wkv.dve_finish(dve, c, 0, 0)
                    dve.wait_ge(wkv.s["gain"], c + 1)
                    condition(c)
                dve.wait_ge(s["const"], 7)
                dve.wait_ge(s["rot"], 16)

                def gates(b):
                    dve.wait_ge(s["gates_sig"], b + 1)
                    dve.tensor_copy(gate[:].rearrange("p h k t -> p t k h"),
                                    gate_raw[:].rearrange("p t (k h) -> p t k h", k=3)).then_inc(s["gates"], 1)
                    dve.wait_ge(s["gates"], b * 2 + 1)
                    dve.tensor_tensor(gate[:, :, 0, :], gate[:, :, 0, :],
                                      seen[:].unsqueeze(1).to_broadcast([P, H0, TT]), ALU.mult).then_inc(s["gates"], 1)

                def rope(g, n):
                    dve.wait_ge(s["qproj"], g * 2 + n + 1)
                    dve.wait_ge(s["q_sb"], g * 2 + n)
                    dve.tensor_tensor(ra[:, n, :], psq[n][:], rot[:, 2 * n, :], ALU.mult).then_inc(s["cosed"], 1)

                def sum_keys(g):
                    dve.wait_ge(s["q_sb"], g * 2 + 2)
                    dve.tensor_reduce(ksum[:], qk[:, 1, :].rearrange("p (m n) -> p m n", n=BLK), AX,
                                      ALU.add).then_inc(s["ksum"], 1)

                def softmax(b, g, h, between):
                    c = g * CMP_STEPS
                    for bank, tiles in BANK_TILES:
                        dve.wait_ge(s["scores"], g * 3 + bank + 1)
                        for j in tiles:
                            dve.tensor_reduce(nmax[:, 0, j:j + 1], cols(ps, j), AX, ALU.max, negate=True)
                            i = dve.tensor_tensor_reduce(out=wcols(sw, j), in0=win(ps, j), in1=wcols(wmask, j),
                                                         scale=-1.0, scalar=3.0e38, op0=ALU.add, op1=ALU.min,
                                                         accum_out=nmax[:, 1, j:j + 1])
                        if bank == 2:
                            i = dve.scalar_tensor_tensor(
                                out=sc[:], in0=ps[2][:, 256:256 + TT * NBLK].rearrange("p (t m) -> p t m", t=TT),
                                scalar=1.0 / BLK, in1=cmask[:], op0=ALU.mult, op1=ALU.add)
                        i.then_inc(s["nmax"], 1)
                    dve.wait_ge(s["nmax"], g * 3 + 3)
                    dve.tensor_reduce(cmax[:], sc[:], AX, ALU.max).then_inc(s["cmp_step"], 1)
                    dve.wait_ge(s["cmp_step"], c + 1)
                    dve.tensor_tensor(sc2[:], sc[:], cmax[:].unsqueeze(2).to_broadcast([P, TT, NBLK]),
                                      ALU.subtract).then_inc(s["cmp_step"], 1)
                    between()
                    dve.wait_ge(s["cmp_e"], g + 1)
                    dve.tensor_reduce(sums[:, 0, :], ec[:], AX, ALU.add).then_inc(s["cmp_step"], 1)
                    dve.wait_ge(s["cmp_step"], c + 3)
                    dve.wait_ge(s["expd"], g * 2 * TT + 2 * TT)
                    dve.wait_ge(s["gates"], b * 2 + 2)
                    dve.reciprocal(rsum[:], sums[:]).then_inc(s["cmp_step"], 1)
                    dve.wait_ge(s["cmp_step"], c + 4)
                    dve.tensor_tensor(coef[:], rsum[:], gate[:, bass.ds(h, 1)].rearrange("p a k t -> p (a k) t"),
                                      ALU.mult).then_inc(s["cmp_step"], 1)
                    dve.wait_ge(s["cmp_step"], c + 5)
                    dve.tensor_tensor(pc[:], ec[:], coef[:, 0, :].unsqueeze(2).to_broadcast([P, TT, NBLK]),
                                      ALU.mult).then_inc(s["coef"], 1)
                    dve.wait_ge(s["coef"], g + 1)
                    for n, j in enumerate((3, 2, 1, 0)):
                        dve.scalar_tensor_tensor(
                            out=cols(pt, j).rearrange("p (m n) -> p m n", n=BLK),
                            in0=cols(ef, j).rearrange("p (m n) -> p m n", n=BLK), scalar=coef[:, 1, j:j + 1],
                            in1=pc[:, j, 0:2 * (j + 1)].unsqueeze(2).to_broadcast([P, 2 * (j + 1), BLK]),
                            op0=ALU.mult, op1=ALU.add).then_inc(s["p_step"], 1)
                    for n, j in enumerate((3, 2, 1, 0)):
                        dve.wait_ge(s["p_step"], g * TT + n + 1)
                        dve.scalar_tensor_tensor(out=win(pt, j), in0=wcols(ewn, j), scalar=coef[:, 2, j:j + 1],
                                                 in1=win(pt, j), op0=ALU.mult, op1=ALU.add).then_inc(s["p"], 1)

                def output(group, co, loads):
                    dve.wait_ge(s["out_ps"], group * CC + co + 1)
                    dve.wait_ge(s["acc_loaded"], loads * 16)
                    dve.scalar_tensor_tensor(out=acc[:, co, :], in0=psg[:], scalar=1.0 / WSCALE, in1=acc[:, co, :],
                                             op0=ALU.mult, op1=ALU.add).then_inc(s["acc"], 1)

                def group(b, c, first, output_before):
                    u, p = group_units(b, c)
                    bn, it = (b + 1) % B, b * CC + c
                    for i in range(G):
                        g = b * H0 + c * G + i
                        if first and i == 0:
                            gates(b)
                        rope(g, 1)
                        if i == 0:
                            wkv.dve_sums(dve, u, bn, c * LAYERS, p)
                        if i == 1:
                            wkv.dve_finish(dve, u, bn, it * 2)
                            dve.wait_ge(wkv.s["gain"], u + 1)
                            condition((b + 1) * CC + c)
                            wkv.dve_sums(dve, u + 1, b, c * LAYERS + 1, p + 1)
                        if i == 2:
                            dve.wait_ge(s["yf"], (b + 1) * CC + c + 1)
                            wkv.dve_finish(dve, u + 1, b, it * 2)
                            wkv.dve_sums(dve, u + 2, b, c * LAYERS + 2, p + 1)
                        if i == 3:
                            wkv.dve_finish(dve, u + 2, b, it * 2 + 1)

                        def between():
                            if i == 0 and (output_before or not first):
                                output(it - 1, 0, b * CC if first else b * CC + CC)
                            if i < PER:
                                wkv.dve_guard(dve, u + i)
                            if i == 0:
                                wkv.dve_prepare(dve, u + 1, p + 1)
                            if i == 1:
                                wkv.dve_prepare(dve, u + 2)
                            if i == 3:
                                wkv.dve_prepare(dve, u + 3, p + 2)
                            rope(g + 1, 0)

                        if i and (output_before or not first):
                            output(it - 1, i, b * CC if first else b * CC + CC)
                        sum_keys(g)
                        softmax(b, g, c * G + i, between)

                rope(0, 0)
                run(dve, group, lambda: [output(B * CC - 1, co, B * CC) for co in range(CC)])


def moe_route(k):
    nc, d = k.nc, k.d
    with ExitStack() as ctx:
        def sb(n, s, dt=F32):
            return ctx.enter_context(nc.sbuf_tensor("mr_" + n, s, dt))

        wr = sb("wr", [P, CC, E])
        zeros = sb("zeros", [P, C])
        xt = sb("xt", [P, CC, T])
        gt = sb("gt", [P, CC, T])
        yt = sb("yt", [P, CC, T])
        rows = sb("rows", [P, NT, C])
        logits = sb("logits", [P, NT, E])
        top = sb("top", [P, NT, 8])
        first = sb("first", [P, E])
        pick = sb("pick", [P, NT, E])
        best = sb("best", [P, NT])
        onehot = sb("onehot", [P, NT, E])
        before = sb("before", [P, NT + 1, E])
        diff = sb("diff", [P, NT])
        ones = sb("ones", [P, P])
        prior = sb("prior", [P, P])
        steps = sb("steps", [P, E, NT])
        over = sb("over", [P, E, NT])
        tiles = sb("tiles", [P, E])
        count = sb("count", [P, E])
        ends = sb("ends", [P, E])
        base = sb("base", [P, E])
        place = sb("place", [P, NT, E])
        slotf = sb("slotf", [P, NT])
        tile_no = sb("tile_no", [P, SLOT_TILES, E])
        past = sb("past", [P, SLOT_TILES, E])
        expertf = sb("expertf", [P, SLOT_TILES])
        psr = ctx.enter_context(nc.psum_tensor("psr_l", [P, 512], F32))
        pst = [ctx.enter_context(nc.psum_tensor(f"psr_t{i}", [P, 512], F32)) for i in range(2)]
        pss = ctx.enter_context(nc.psum_tensor("psr_s", [P, 512], F32))
        s = {n: k.sem("mr_" + n) for n in (
            "router", "x_loaded", "zeros", "zeroed", "const", "sig", "y", "logits_ps", "logits", "rows_ps",
            "rows", "math", "sums", "exp", "slots", "scattered")}
        with nc.Block() as block:

            @block.sync
            def _(sp):
                sp.dma_start(wr[:], d["router"]).then_inc(s["router"], 16)
                with sp.Fori(0, B) as b:
                    xsrc = d["x1"][bass.ds(b, 1)].rearrange("a c p n -> p (a c) n")
                    gsrc = d["gain"][1, bass.ds(b, 1)].rearrange("a c p n -> p (a c) n")
                    sp.wait_ge(s["y"], b * CC + 1)
                    sp.dma_start(xt[:], xsrc).then_inc(s["x_loaded"], 16)
                    sp.dma_start(gt[:], gsrc).then_inc(s["x_loaded"], 16)
                sp.wait_ge(s["zeros"], 1)
                for j in range(SLOT_TILES + 1):
                    sp.dma_start(d["slot_x"][j * P:(j + 1) * P, :], zeros[:]).then_inc(s["zeroed"], 16)

            @block.gpsimd
            def _(pool):
                pool.memset(zeros[:], 0.0).then_inc(s["zeros"], 1)
                pool.memset(ones[:], 1.0).then_inc(s["const"], 1)
                pool.memset(prior[:], 1.0).then_inc(s["const"], 1)
                pool.iota(first[:], pattern=[[-1, E]], base=E, channel_multiplier=0,
                          allow_small_or_imprecise_dtypes=True).then_inc(s["const"], 1)
                pool.iota(steps[:], pattern=[[0, E], [P, NT]], base=0, channel_multiplier=0,
                          allow_small_or_imprecise_dtypes=True).then_inc(s["const"], 1)
                pool.iota(tile_no[:], pattern=[[1, SLOT_TILES], [0, E]], base=0, channel_multiplier=0,
                          allow_small_or_imprecise_dtypes=True).then_inc(s["const"], 1)
                pool.wait_ge(s["const"], 5)
                pool.affine_select(out=prior[:], in_=prior[:], compare_op=ALU.is_gt, fill=0.0, base=0,
                                   pattern=[[1, P]], channel_multiplier=-1).then_inc(s["const"], 1)
                pool.wait_ge(s["zeroed"], 16 * (SLOT_TILES + 1))
                pool.wait_ge(s["slots"], 1)
                pool.wait_ge(s["rows"], NT)
                for i in range(NT):
                    pool.indirect_dma_start(d["slot_x"], bass.IndirectOffsetOnAxis(ap=k.slot[:, i:i + 1], axis=0),
                                            rows[:, i, :], None).then_inc(s["scattered"], 16)
                pool.wait_ge(s["scattered"], 16 * NT)

            @block.scalar
            def _(act):
                with act.Fori(0, B) as b:
                    act.wait_ge(s["x_loaded"], b * 32 + 32)
                    for c in range(CC):
                        act.activation(yt[:, c, :], xt[:, c, :], ACT.Sigmoid).then_inc(s["sig"], 1)
                    for t in range(TT):
                        act.wait_ge(s["rows_ps"], b * TT + t + 1)
                        act.activation(rows[:, bass.ds(b * TT + t, 1), :].rearrange("p a n -> p (a n)"),
                                       pst[t % 2][:], ACT.Copy).then_inc(s["rows"], 1)
                act.wait_ge(s["math"], 1)
                act.activation(diff[:], diff[:], ACT.Exp).then_inc(s["exp"], 1)

            @block.tensor
            def _(pe):
                pe.wait_ge(s["router"], 16)
                pe.sem_inc(s["y"], 1)
                with pe.Fori(0, B) as b:
                    pe.wait_ge(s["y"], b * CC + CC + 1)
                    for t in range(TT):
                        for c in range(CC):
                            mm = pe.matmul(psr[:, t * E:(t + 1) * E], yt[:, c, t * P:(t + 1) * P], wr[:, c, :],
                                           start=c == 0, stop=c == CC - 1)
                    mm.then_inc(s["logits_ps"], 1)
                    for t in range(TT):
                        if t >= 2:
                            pe.wait_ge(s["rows"], b * TT + t - 1)
                        for c in range(CC):
                            mm = pe.transpose(pst[t % 2][:, c * P:(c + 1) * P], yt[:, c, t * P:(t + 1) * P], k.ident[:])
                        mm.then_inc(s["rows_ps"], 1)
                pe.wait_ge(s["math"], 2)
                pe.wait_ge(s["const"], 6)
                pe.matmul(pss[:, 0:NT * E], prior[:], onehot[:].rearrange("p t e -> p (t e)"), start=True, stop=False)
                pe.matmul(pss[:, 0:NT * E], ones[:], before[:, 0:NT, :].rearrange("p t e -> p (t e)"),
                          start=False, stop=True)
                pe.matmul(pss[:, NT * E:NT * E + E], ones[:], before[:, NT, :], start=True,
                          stop=True).then_inc(s["sums"], 1)

            @block.vector
            def _(dve):
                with dve.Fori(0, B) as b:
                    for c in range(CC):
                        dve.wait_ge(s["sig"], b * CC + c + 1)
                        dve.tensor_tensor(yt[:, c, :], yt[:, c, :], gt[:, c, :], ALU.mult).then_inc(s["y"], 1)
                    dve.wait_ge(s["logits_ps"], b + 1)
                    dve.tensor_copy(logits[:, bass.ds(b * TT, TT), :],
                                    psr[:, 0:TT * E].rearrange("p (t e) -> p t e", t=TT)).then_inc(s["logits"], 1)
                dve.wait_ge(s["const"], 6)
                dve.wait_ge(s["logits"], B)
                for i in range(NT):
                    m = dve.max(top[:, i, :], logits[:, i, :])
                step = Tally(k.sem("mr_step"))

                def then(ins):
                    dve.wait_ge(step.sem, step.inc(ins))

                def wide(a, n=E):
                    return a.unsqueeze(2).to_broadcast([P, a.shape[1], n])

                then(m)
                dve.tensor_tensor(diff[:], top[:, :, 1], top[:, :, 0], ALU.subtract).then_inc(s["math"], 1)
                then(dve.tensor_tensor(pick[:], logits[:], wide(top[:, :, 0]), ALU.is_equal))
                then(dve.tensor_tensor(pick[:], pick[:], first[:].unsqueeze(1).to_broadcast([P, NT, E]), ALU.mult))
                then(dve.tensor_reduce(best[:], pick[:], AX, ALU.max))
                then(dve.memset(before[:, 0, :], 0.0))
                then(dve.tensor_tensor(onehot[:], wide(best[:]), first[:].unsqueeze(1).to_broadcast([P, NT, E]),
                                       ALU.is_equal))
                for i in range(NT):
                    then(dve.tensor_tensor(before[:, i + 1, :], before[:, i, :], onehot[:, i, :], ALU.add))
                dve.wait_ge(s["exp"], 1)
                then(dve.tensor_scalar(diff[:], diff[:], 1.0, None, ALU.add))
                dve.reciprocal(k.weight[:], diff[:]).then_inc(s["math"], 1)
                dve.wait_ge(s["sums"], 1)
                then(dve.tensor_copy(count[:], pss[:, NT * E:NT * E + E]))
                then(dve.tensor_tensor(over[:], wide(count[:], NT), steps[:], ALU.is_gt))
                then(dve.tensor_reduce(tiles[:], over[:], AX, ALU.add))
                then(dve.tensor_tensor_scan(ends[:], ones[:, 0:E], tiles[:], 0.0, ALU.mult, ALU.add))
                then(dve.tensor_tensor(base[:], ends[:], tiles[:], ALU.subtract))
                then(dve.tensor_scalar(base[:], base[:], float(P), None, ALU.mult))
                then(dve.tensor_tensor(place[:], pss[:, 0:NT * E].rearrange("p (t e) -> p t e", t=NT),
                                       base[:].unsqueeze(1).to_broadcast([P, NT, E]), ALU.add))
                then(dve.tensor_tensor(place[:], place[:], onehot[:], ALU.mult))
                then(dve.tensor_reduce(slotf[:], place[:], AX, ALU.add))
                dve.tensor_copy(k.slot[:], slotf[:]).then_inc(s["slots"], 1)
                then(dve.tensor_tensor(past[:], tile_no[:], ends[:].unsqueeze(1).to_broadcast([P, SLOT_TILES, E]),
                                       ALU.is_ge))
                then(dve.tensor_reduce(expertf[:], past[:], AX, ALU.add))
                then(dve.tensor_scalar(expertf[:], expertf[:], float(E - 1), None, ALU.min))
                then(dve.tensor_copy(k.tile_expert[:], expertf[:]))


def moe_experts(k):
    nc, d = k.nc, k.d
    GW = (E // 4)
    with ExitStack() as ctx:
        def sb(n, s, dt=F32):
            return ctx.enter_context(nc.sbuf_tensor("me_" + n, s, dt))

        wgu = sb("wgu", [P, E, 2, CC, I])
        wd = sb("wd", [P, E, KI, C])
        xin = sb("xin", [P, 2, C])
        xT = sb("xT", [P, 2, C])
        sg = sb("sg", [P, I])
        a = sb("a", [P, 2, KI * P])
        aT = sb("aT", [P, KI * P])
        yo = sb("yo", [P, 2, C])
        psx = ctx.enter_context(nc.psum_tensor("pse_x", [P, 512], F32))
        psg = ctx.enter_context(nc.psum_tensor("pse_g", [P, 512], F32))
        psu = ctx.enter_context(nc.psum_tensor("pse_u", [P, 512], F32))
        psa = ctx.enter_context(nc.psum_tensor("pse_a", [P, 512], F32))
        psd = ctx.enter_context(nc.psum_tensor("pse_d", [P, 512], F32))
        s = {n: k.sem("me_" + n) for n in (
            "weights", "x0", "x1", "x_ps", "xT", "gu", "silu", "a", "a_pad", "a_ps", "aT", "down", "y", "stored0",
            "stored1")}
        last = SLOT_TILES - 1
        with nc.Block() as block:

            @block.sync
            def _(sp):
                def load(j, i, dyn):
                    src = d["slot_x"][bass.ds(j * P, P), :] if dyn else d["slot_x"][j * P:(j + 1) * P, :]
                    if dyn:
                        sp.wait_ge(s["x_ps"], j - 1)
                    sp.dma_start(xin[:, i, :], src).then_inc(s[f"x{i}"], 16)

                def store(j, i, dyn):
                    dst = d["slot_y"][bass.ds(j * P, P), :] if dyn else d["slot_y"][j * P:(j + 1) * P, :]
                    sp.wait_ge(s["y"], j + 1)
                    sp.dma_start(dst, yo[:, i, :]).then_inc(s[f"stored{i}"], 16)

                load(0, 0, False)
                load(1, 1, False)
                for e in range(0, E, GW):
                    sp.dma_start(wgu[:, e:e + GW], d["gate_up"][:, e:e + GW]).then_inc(s["weights"], 16)
                    sp.dma_start(wd[:, e:e + GW], d["down"][:, e:e + GW]).then_inc(s["weights"], 16)
                with sp.Fori(1, last // 2 + 1) as m:
                    for i in range(2):
                        load(m * 2 + i, i, True)
                        store(m * 2 + (i - 2), i, True)
                store(last, last % 2, False)
                for i in range(2):
                    sp.wait_ge(s[f"stored{i}"], 16 + 16 * ((SLOT_TILES + 1 - i) // 2))

            @block.tensor
            def _(pe):
                pe.wait_ge(s["a_pad"], 1)

                def turn_x(j, i, first):
                    pe.wait_ge(s[f"x{i}"], (j // 2 if isinstance(j, int) else (j - i) // 2) * 16 + 16)
                    if not first:
                        pe.wait_ge(s["xT"], j)
                    for c in range(CC):
                        mm = pe.transpose(psx[:, c * P:(c + 1) * P], xin[:, i, c * P:(c + 1) * P], k.ident[:])
                    mm.then_inc(s["x_ps"], 1)

                def gate_up(j, i):
                    e = pe.value_load(k.tile_expert[0:1, bass.ds(j, 1)], min_val=0, max_val=E - 1)
                    pe.wait_ge(s["xT"], j + 1)
                    for n, ps in enumerate((psg, psu)):
                        for c in range(CC):
                            mm = pe.matmul(ps[:, 0:I], xT[:, i, c * P:(c + 1) * P],
                                           wgu[:, bass.ds(e, 1), n, c, :].rearrange("p a n -> p (a n)"),
                                           start=c == 0, stop=c == CC - 1)
                    mm.then_inc(s["gu"], 1)

                def turn_a(j, i):
                    pe.wait_ge(s["a"], j + 1)
                    for c in range(KI):
                        mm = pe.transpose(psa[:, c * P:(c + 1) * P], a[:, i, c * P:(c + 1) * P], k.ident[:])
                    mm.then_inc(s["a_ps"], 1)

                def down(j, i, first):
                    e = pe.value_load(k.tile_expert[0:1, bass.ds(j, 1)], min_val=0, max_val=E - 1)
                    pe.wait_ge(s["aT"], j + 1)
                    if not first:
                        pe.wait_ge(s["y"], j)
                    for c in range(KI):
                        mm = pe.matmul(psd[:], aT[:, c * P:(c + 1) * P],
                                       wd[:, bass.ds(e, 1), c, :].rearrange("p a n -> p (a n)"),
                                       start=c == 0, stop=c == KI - 1)
                    mm.then_inc(s["down"], 1)

                turn_x(0, 0, True)
                pe.wait_ge(s["weights"], 16 * 2 * (E // GW))
                gate_up(0, 0)
                turn_x(1, 1, False)
                def step(j, i, first):
                    turn_a(j - 1, 1 - i)
                    gate_up(j, i)
                    turn_x(j + 1, 1 - i, False)
                    down(j - 1, 1 - i, first)

                step(1, 1, True)
                step(2, 0, False)
                with pe.Fori(2, last // 2 + 1) as m:
                    step(m * 2 - 1, 1, False)
                    step(m * 2, 0, False)
                turn_a(last, last % 2)
                down(last, last % 2, False)

            @block.scalar
            def _(act):
                def take_x(j, i):
                    act.wait_ge(s["x_ps"], j + 1)
                    act.activation(xT[:, i, :], psx[:], ACT.Copy).then_inc(s["xT"], 1)

                def silu(j):
                    act.wait_ge(s["gu"], j + 1)
                    act.activation(sg[:], psg[:, 0:I], ACT.Silu).then_inc(s["silu"], 1)

                take_x(0, 0)
                silu(0)
                take_x(1, 1)
                with act.Fori(1, last // 2 + 1) as m:
                    silu(m * 2 - 1)
                    take_x(m * 2, 0)
                    silu(m * 2)
                    take_x(m * 2 + 1, 1)

            @block.vector
            def _(dve):
                for i in range(2):
                    dve.sem_inc(s[f"stored{i}"], 16)
                dve.memset(a[:], 0.0).then_inc(s["a_pad"], 1)
                dve.wait_ge(s["a_pad"], 1)

                def mul(j, i):
                    dve.wait_ge(s["silu"], j + 1)
                    dve.tensor_tensor(a[:, i, 0:I], sg[:], psu[:, 0:I], ALU.mult).then_inc(s["a"], 1)

                def take_a(j):
                    dve.wait_ge(s["a_ps"], j + 1)
                    dve.tensor_copy(aT[:], psa[:, 0:KI * P]).then_inc(s["aT"], 1)

                def out(j, i, half):
                    dve.wait_ge(s["down"], j + 1)
                    dve.wait_ge(s[f"stored{i}"], half * 16 + 16)
                    dve.tensor_copy(yo[:, i, :], psd[:]).then_inc(s["y"], 1)

                mul(0, 0)
                with dve.Fori(1, last // 2 + 1) as m:
                    take_a(m * 2 - 2)
                    mul(m * 2 - 1, 1)
                    out(m * 2 - 2, 0, m - 1)
                    take_a(m * 2 - 1)
                    mul(m * 2, 0)
                    out(m * 2 - 1, 1, m - 1)
                take_a(last)
                out(last, last % 2, last // 2)


def moe_combine(k):
    nc, d = k.nc, k.d
    with ExitStack() as ctx:
        def sb(n, s, dt=F32):
            return ctx.enter_context(nc.sbuf_tensor("mc_" + n, s, dt))

        got = sb("got", [P, NT, C])
        yw = sb("yw", [P, 2, C])
        xt = sb("xt", [P, 2, CC, T])
        ps = [ctx.enter_context(nc.psum_tensor(f"psc_{i}", [P, 512], F32)) for i in range(2)]
        s = {n: k.sem("mc_" + n) for n in ("got", "x0", "x1", "weighted", "turned", "x2", "stored")}
        with nc.Block() as block:

            @block.gpsimd
            def _(pool):
                for i in range(NT):
                    pool.indirect_dma_start(got[:, i, :], None, d["slot_y"],
                                            bass.IndirectOffsetOnAxis(ap=k.slot[:, i:i + 1], axis=0)
                                            ).then_inc(s["got"], 16)

            @block.sync
            def _(sp):
                for b in range(B):
                    if b >= 2:
                        sp.wait_ge(s["stored"], 16 * (b - 1))
                    sp.dma_start(xt[:, b % 2], d["x1"][b].rearrange("c p n -> p c n")).then_inc(s[f"x{b % 2}"], 16)
                    if b >= 1:
                        sp.wait_ge(s["x2"], TT * b)
                        sp.dma_start(d["x2"][b - 1].rearrange("c p n -> p c n"), xt[:, (b - 1) % 2]).then_inc(s["stored"], 16)
                sp.wait_ge(s["x2"], TT * B)
                sp.dma_start(d["x2"][B - 1].rearrange("c p n -> p c n"), xt[:, (B - 1) % 2]).then_inc(s["stored"], 16)
                sp.wait_ge(s["stored"], 16 * B)

            @block.tensor
            def _(pe):
                for i in range(NT):
                    pe.wait_ge(s["weighted"], i + 1)
                    if i >= 2:
                        pe.wait_ge(s["x2"], i - 1)
                    for c in range(CC):
                        mm = pe.transpose(ps[i % 2][:, c * P:(c + 1) * P], yw[:, i % 2, c * P:(c + 1) * P], k.ident[:])
                    mm.then_inc(s["turned"], 1)

            @block.vector
            def _(dve):
                def weigh(i):
                    dve.wait_ge(s["got"], 16 * NT)
                    if i >= 2:
                        dve.wait_ge(s["turned"], i - 1)
                    dve.tensor_scalar(yw[:, i % 2, :], got[:, i, :], k.weight[:, i:i + 1], None,
                                      ALU.mult).then_inc(s["weighted"], 1)

                weigh(0)
                for i in range(NT):
                    if i + 1 < NT:
                        weigh(i + 1)
                    b, t = divmod(i, TT)
                    if t == 0:
                        dve.wait_ge(s[f"x{b % 2}"], 16 * (b // 2 + 1))
                    dve.wait_ge(s["turned"], i + 1)
                    x = xt[:, b % 2, :, t * P:(t + 1) * P]
                    dve.tensor_tensor(x, ps[i % 2][:].rearrange("p (c n) -> p c n", c=CC), x, ALU.add).then_inc(s["x2"], 1)


def layer1_attn(k):
    nc, d = k.nc, k.d
    with ExitStack() as ctx:
        def sb(n, s, dt=F32):
            return ctx.enter_context(nc.sbuf_tensor("a1_" + n, s, dt))

        raw = sb("raw", [P, 2, 3, CC, P])
        w16 = sb("w16", [P, 2, CC, 3, CC, P], F16)
        wp = sb("wp", [P, CC, C])
        wp16 = sb("wp16", [P, 2, CC, C], F16)
        bqk = sb("bqk", [P, 3, CC])
        bq = sb("bq", [P, CC])
        bv = sb("bv", [P, C])
        bp = sb("bp", [P, CC])
        xc = sb("xc", [P, T])
        gc = sb("gc", [P, T])
        sg = sb("sg", [P, T])
        yf = sb("yf", [P, T])
        y16 = sb("y16", [P, 2, CC, T], F16)
        ynext = sb("ynext", [P, 2, CC, T], F16)
        qk = sb("qk", [P, 2, 2, T])
        vf = sb("vf", [P, TT, P])
        v16 = sb("v16", [P, 2, 2, TT, P], F16)
        nmax = sb("nmax", [P, 2, TT])
        sums = sb("sums", [P, 2, TT])
        rsum = sb("rsum", [P, 2, TT])
        ef = sb("ef", [P, 2, 3, 512])
        t16 = sb("t16", [P, 2, 2, 3, 512], F16)
        ob = sb("ob", [P, 2, TT, P])
        ot16 = sb("ot16", [P, 2, CC, T], F16)
        x3 = sb("x3", [P, CC, T])
        ps = [[ctx.enter_context(nc.psum_tensor(f"ps1_{a}{i}", [P, 512], F32)) for i in range(3)] for a in range(2)]
        pso = ctx.enter_context(nc.psum_tensor("ps1_o", [P, 512], F32))
        psp = ctx.enter_context(nc.psum_tensor("ps1_p", [P, 512], F32))
        s = {n: k.sem("a1_" + n) for n in (
            "fixed", "biased", "raw0", "raw1", "w64", "whi", "wlo", "x_loaded", "sig_step", "sig", "yf", "yhi", "ylo", "y_moved",
            "bq", "qproj", "q", "kproj", "k", "vproj", "vf", "vhi", "vlo", "scores", "nmax", "expd",
            "turned", "thi", "tlo", "pv", "rsum", "o", "ot_ps", "ot_hi", "ot_lo", "proj", "x3", "x3_loaded", "x3_stored")}
        SCALE = float(np.float32(1.0) / np.sqrt(np.float32(D1)))
        PARTS = ((0, 0), (0, 1), (1, 0))
        wkv = Wkv(k, ctx, "wkv3", 1)
        LAYER = 3
        AHEAD = CC + 1

        def cols(t, j, lo=0, hi=None):
            bank, c0 = score_columns(j)
            hi = P * (j + 1) if hi is None else hi
            return t[bank][:, c0 + lo:c0 + hi] if isinstance(t, list) else t[:, bank, c0 + lo:c0 + hi]

        def chunk_after(b, q, n):
            return (b + (q + n) // CC) % B, (q + n) % CC

        with nc.Block() as block:

            @block.sync
            def _(sp):
                def load_raw(n):
                    if n < CC:
                        if n >= 2:
                            sp.wait_ge(s["wlo"], n - 1)
                        sp.dma_start(raw[:, n % 2], d["wqkv1"][n]).then_inc(s[f"raw{n % 2}"], 16)
                    else:
                        sp.dma_start(wp[:], d["wp1"]).then_inc(s["raw0"], 16)

                def xg(b, c, n):
                    x = d["x2"][bass.ds(b, 1), c].rearrange("a p n -> (a p) n")
                    g = d["gain"][2, bass.ds(b, 1), c].rearrange("a p n -> (a p) n")
                    if not (isinstance(n, int) and n == 0):
                        sp.wait_ge(s["yf"], n)
                    sp.dma_start(xc[:], x).then_inc(s["x_loaded"], 16)
                    sp.dma_start(gc[:], g).then_inc(s["x_loaded"], 16)

                def residual(b):
                    x = d["x2"][bass.ds(b, 1)].rearrange("a c p n -> p (a c) n")
                    if not isinstance(b, int):
                        sp.wait_ge(s["x3_stored"], b * 16)
                    sp.dma_start(x3[:], x).then_inc(s["x3_loaded"], 16)

                def store(b):
                    dst = d["x3"][bass.ds(b, 1)].rearrange("a c p n -> p (a c) n")
                    sp.wait_ge(s["x3"], b * CC + CC)
                    sp.dma_start(dst, x3[:]).then_inc(s["x3_stored"], 16)

                def batch(b, first):
                    for q in range(CC):
                        bn, cn = chunk_after(b, q, AHEAD + 1)
                        xg(bn, cn, b * CC + q + (AHEAD + 1))
                        if q == 0 and not first:
                            store(b - 1)
                        if q == 1:
                            residual(b)
                        if q == 2:
                            sp.wait_ge(s["vproj"], b * CC + CC)
                            sp.dma_start(y16[:], ynext[:]).then_inc(s["y_moved"], 16)

                xg(0, 0, 0)
                load_raw(0)
                load_raw(1)
                sp.dma_start(bqk[:], d["bqkv1"]).then_inc(s["fixed"], 16)
                sp.dma_start(bv[:], d["bv1"].partition_broadcast(P)).then_inc(s["fixed"], 16)
                sp.dma_start(bp[:], d["bp1"]).then_inc(s["fixed"], 16)
                xg(0, 1, 1)
                load_raw(2)
                xg(0, 2, 2)
                load_raw(3)
                load_raw(4)
                xg(0, 3, 3)
                sp.wait_ge(s["ylo"], CC)
                sp.dma_start(y16[:], ynext[:]).then_inc(s["y_moved"], 16)
                xg(1, 0, 4)
                xg(1, 1, 5)
                batch(0, True)
                with sp.Fori(1, B) as b:
                    batch(b, False)
                store(B - 1)
                sp.wait_ge(s["x3_stored"], 16 * B)
                sp.wait_ge(s["x_loaded"], 32 * (B * CC + AHEAD + 1))

            @block.gpsimd
            def _(pool):
                def y_low(c, n):
                    pool.wait_ge(s["yhi"], n + 1)
                    pool.tensor_tensor(ynext[:, 1, c, :], yf[:], ynext[:, 0, c, :], ALU.subtract).then_inc(s["ylo"], 1)

                def v_low(n, q):
                    pool.wait_ge(s["vhi"], n + 1)
                    pool.tensor_tensor(v16[:, q % 2, 1], vf[:], v16[:, q % 2, 0], ALU.subtract).then_inc(s["vlo"], 1)

                wkv.pool_prepare(pool, 0, 0, 0)
                for n in range(CC):
                    pool.wait_ge(s["whi"], n + 1)
                    pool.tensor_tensor(w16[:, 1, n], raw[:, n % 2], w16[:, 0, n], ALU.subtract).then_inc(s["wlo"], 1)
                    y_low(n, n)
                pool.wait_ge(s["whi"], CC + 1)
                pool.tensor_tensor(wp16[:, 1], wp[:], wp16[:, 0], ALU.subtract).then_inc(s["wlo"], 1)
                v_low(0, 0)
                y_low(0, CC)

                def batch(b, first):
                    for q in range(CC):
                        it = b * CC + q
                        wkv.pool_join(pool, it)
                        y_low(chunk_after(0, q, AHEAD)[1], it + AHEAD)
                        v_low(it + 1, q + 1)
                        wkv.pool_prepare(pool, 0, it + 1, it + 1)

                batch(0, True)
                with pool.Fori(1, B) as b:
                    batch(b, False)

            @block.scalar
            def _(act):
                def split(n):
                    src, dst = (raw[:, n % 2], w16[:, 0, n]) if n < CC else (wp[:], wp16[:, 0])
                    act.wait_ge(s[f"raw{n % 2}"], n // 2 * 16 + 16)
                    act.activation(src, src, ACT.Copy, scale=WSCALE).then_inc(s["w64"], 1)
                    act.wait_ge(s["w64"], n + 1)
                    act.activation(dst, src, ACT.Copy).then_inc(s["whi"], 1)

                def y_sigmoid(n):
                    act.wait_ge(s["x_loaded"], n * 32 + 32)
                    act.activation(sg[:], xc[:], ACT.Exp, scale=-1.0).then_inc(s["sig_step"], 1)
                    act.wait_ge(s["sig_step"], n * 2 + 1)
                    act.activation(sg[:], sg[:], ACT.Ln, bias=1.0).then_inc(s["sig_step"], 1)
                    act.wait_ge(s["sig_step"], n * 2 + 2)
                    act.activation(sg[:], sg[:], ACT.Exp, scale=-1.0).then_inc(s["sig"], 1)

                def y_high(c, n):
                    act.wait_ge(s["yf"], n + 1)
                    act.activation(ynext[:, 0, c, :], yf[:], ACT.Copy).then_inc(s["yhi"], 1)

                def take_q(n, q):
                    act.wait_ge(s["qproj"], n + 1)
                    act.activation(qk[:, q % 2, 0, :], psp[:], ACT.Identity, bias=bq[:, q:q + 1],
                                   scale=SCALE / WSCALE).then_inc(s["q"], 1)

                def take_k(n, q):
                    act.wait_ge(s["kproj"], n + 1)
                    act.activation(qk[:, q % 2, 1, :], psp[:], ACT.Identity, bias=bqk[:, 1, q:q + 1],
                                   scale=1.0 / WSCALE).then_inc(s["k"], 1)

                def v_high(n, q):
                    act.wait_ge(s["vf"], n + 1)
                    act.activation(v16[:, q % 2, 0], vf[:], ACT.Copy).then_inc(s["vhi"], 1)

                def ot_high(n, q):
                    act.wait_ge(s["ot_ps"], n + 1)
                    act.activation(ot16[:, 0, q, :], psp[:], ACT.Copy).then_inc(s["ot_hi"], 1)

                def exps(h, i):
                    for bank, tiles in BANK_TILES:
                        act.wait_ge(s["nmax"], h * 3 + bank + 1)
                        for j in tiles:
                            act.activation(cols(ef[:, i % 2], j), cols(ps[i % 2], j), ACT.Exp,
                                           bias=nmax[:, i % 2, j:j + 1],
                                           accum_out=sums[:, i % 2, j:j + 1]).then_inc(s["expd"], 1)

                def turned_high(h, i):
                    for bank, width in ((0, 512), (1, 512), (2, 256)):
                        act.wait_ge(s["turned"], h * 3 + bank + 1)
                        act.activation(t16[:, i % 2, 0, bank, 0:width], ps[i % 2][bank][:, 0:width],
                                       ACT.Copy).then_inc(s["thi"], 1)

                act.preload_act_table_set("natural_log_exp_and_others")
                wkv.act_load(act, 0, 0, 0, None)
                y_sigmoid(0)
                wkv.act_prepare(act, 0, 0, LAYER, 0, 1)
                y_high(0, 0)
                split(0)
                for n in range(1, CC):
                    y_sigmoid(n)
                    y_high(n, n)
                    split(n)
                split(CC)
                y_sigmoid(CC)
                act.wait_ge(s["y_moved"], 16)
                y_high(0, CC)
                act.wait_ge(s["bq"], 1)
                take_q(0, 0)
                take_k(0, 0)
                v_high(0, 0)
                exps(0, 0)

                def batch(b, first):
                    for q in range(CC):
                        it = b * CC + q
                        for i in range(HPC):
                            h = b * H1 + (q * HPC + i)
                            if i == 1 and (q or not first):
                                ot_high(it - 1, (q - 1) % CC)
                            turned_high(h, i)
                            exps(h + 1, i + 1)
                            if i == 0:
                                y_sigmoid(it + AHEAD)
                                take_q(it + 1, (q + 1) % CC)
                            if i == 1:
                                if q == CC - 1:
                                    act.wait_ge(s["y_moved"], b * 16 + 32)
                                y_high((q + AHEAD) % CC, it + AHEAD)
                                wkv.act_invert(act, it)
                                take_k(it + 1, (q + 1) % CC)
                                wkv.act_load(act, 0, *chunk_after(b, q, 1), it + 1)
                            if i == 2:
                                v_high(it + 1, q + 1)
                            if i == 3:
                                bn, cn = chunk_after(b, q, 1)
                                wkv.act_prepare(act, 0, it + 1, cn * LAYERS + LAYER, it + 1, it + 2)
                                wkv.act_store(act, it, LAYER, b, q)

                batch(0, True)
                with act.Fori(1, B) as b:
                    batch(b, False)
                act.wait_ge(s["ot_ps"], B * CC)
                act.activation(ot16[:, 0, CC - 1, :], psp[:], ACT.Copy).then_inc(s["ot_hi"], 1)
                act.wait_ge(wkv.s["stored"], 16 * B * CC)
                act.wait_ge(wkv.loaded[0], 16 * (B * CC + 1))

            @block.tensor
            def _(pe):
                def project_qk(n, q, kind):
                    for c in range(CC):
                        for m, (yp, wpart) in enumerate(PARTS):
                            mm = pe.matmul(psp[:], w16[:, wpart, q, kind, c, :], y16[:, yp, c, :],
                                           start=c + m == 0, stop=c == CC - 1 and m == 2)
                    mm.then_inc(s["kproj" if kind else "qproj"], 1)

                def project_v(n, q):
                    for t in range(TT):
                        for c in range(CC):
                            for m, (yp, wpart) in enumerate(PARTS):
                                mm = pe.matmul(psp[:, t * P:(t + 1) * P], y16[:, yp, c, t * P:(t + 1) * P],
                                               w16[:, wpart, q, 2, c, :], start=c + m == 0,
                                               stop=c == CC - 1 and m == 2)
                    mm.then_inc(s["vproj"], 1)

                def scores(h, q, i):
                    r = slice(i * D1, (i + 1) * D1)
                    for bank, tiles in BANK_TILES:
                        for j in tiles:
                            pe.matmul(cols(ps[i % 2], j), qk[r, q % 2, 0, j * P:(j + 1) * P],
                                      qk[r, q % 2, 1, 0:P * (j + 1)], start=True, stop=False)
                            mm = pe.matmul(cols(ps[i % 2], j, P * j), k.ident_b[:], k.causal_b[:],
                                           start=False, stop=True)
                        mm.then_inc(s["scores"], 1)

                def turn(h, i):
                    pe.wait_ge(s["expd"], h * TT + TT)
                    for bank, tiles in ((0, (0,)), (1, (1, 3)), (2, (2,))):
                        for m in tiles:
                            _, c0 = turned_columns(m)
                            for j in range(m, TT):
                                mm = pe.transpose(ps[i % 2][bank][:, c0 + (j - m) * P:c0 + (j - m + 1) * P],
                                                  cols(ef[:, i % 2], j, m * P, (m + 1) * P), k.ident[:])
                        mm.then_inc(s["turned"], 1)

                def values(h, q, i):
                    if not (isinstance(h, int) and h == 0):
                        pe.wait_ge(s["o"], h)
                    for j in range(TT):
                        for m in range(j + 1):
                            bank, c0 = turned_columns(m)
                            for n, (tp, vp) in enumerate(PARTS):
                                mm = pe.matmul(pso[:, j * D1:(j + 1) * D1],
                                               t16[:, i % 2, tp, bank, c0 + (j - m) * P:c0 + (j - m + 1) * P],
                                               v16[:, q % 2, vp, m, i * D1:(i + 1) * D1],
                                               start=m + n == 0, stop=m == j and n == 2)
                    mm.then_inc(s["pv"], 1)

                def turn_output(n, q):
                    pe.wait_ge(s["o"], n * HPC + HPC)
                    for t in range(TT):
                        mm = pe.transpose(psp[:, t * P:(t + 1) * P], ob[:, q % 2, t, :], k.ident[:])
                    mm.then_inc(s["ot_ps"], 1)

                def output(co):
                    for c in range(CC):
                        for n, (op, wpart) in enumerate(PARTS):
                            mm = pe.matmul(psp[:], wp16[:, wpart, c, co * P:(co + 1) * P], ot16[:, op, c, :],
                                           start=c + n == 0, stop=c == CC - 1 and n == 2)
                    mm.then_inc(s["proj"], 1)

                pe.wait_ge(s["wlo"], CC + 1)
                pe.wait_ge(s["y_moved"], 16)
                project_qk(0, 0, 0)
                pe.wait_ge(s["q"], 1)
                project_qk(0, 0, 1)
                pe.wait_ge(s["k"], 1)
                project_v(0, 0)
                scores(0, 0, 0)

                def batch(b, first):
                    for q in range(CC):
                        it = b * CC + q
                        qn = (q + 1) % CC
                        for i in range(HPC):
                            h = b * H1 + (q * HPC + i)
                            pe.wait_ge(s["tlo"], h * 3)
                            if i < HPC - 1:
                                scores(h + 1, q, i + 1)
                            else:
                                pe.wait_ge(s["k"], it + 2)
                                scores(h + 1, q + 1, 0)
                            if i == 1 and (q or not first):
                                pe.wait_ge(s["q"], it + 2)
                                turn_output(it - 1, q + 1)
                            turn(h, i)
                            if i == 1:
                                pe.wait_ge(s["vlo"], it + 1)
                            if i or q or not first:
                                values(h - 1, q if i else q + 1, (i - 1) % HPC)
                            if i == 0:
                                if q == CC - 1:
                                    pe.wait_ge(s["y_moved"], b * 16 + 32)
                                if q == 1 and not first:
                                    pe.wait_ge(s["x3"], b * CC)
                                else:
                                    pe.wait_ge(s["vf"], it + 1)
                                project_qk(it + 1, qn, 0)
                            if i == 1:
                                if q or not first:
                                    pe.wait_ge(s["ot_lo"], it)
                                else:
                                    pe.wait_ge(s["q"], it + 2)
                                project_qk(it + 1, qn, 1)
                            if i == 2:
                                pe.wait_ge(s["k"], it + 2)
                                if q == 2:
                                    pe.wait_ge(s["ylo"], b * CC + 2 * CC)
                                project_v(it + 1, qn)
                            if i == 3 and q == 0 and not first:
                                pe.wait_ge(s["vf"], it + 2)
                                for co in range(CC):
                                    if co:
                                        pe.wait_ge(s["x3"], (b - 1) * CC + co)
                                    output(co)

                batch(0, True)
                with pe.Fori(1, B) as b:
                    batch(b, False)
                pe.wait_ge(s["tlo"], B * H1 * 3)
                values(B * H1 - 1, CC - 1, HPC - 1)
                pe.wait_ge(s["vf"], B * CC + 1)
                turn_output(B * CC - 1, CC - 1)
                pe.wait_ge(s["ot_lo"], B * CC)
                for co in range(CC):
                    if co:
                        pe.wait_ge(s["x3"], (B - 1) * CC + co)
                    output(co)

            @block.vector
            def _(dve):
                wkv.dve_zero(dve)

                def condition(n):
                    dve.wait_ge(s["sig"], n + 1)
                    if not (isinstance(n, int) and n == 0):
                        dve.wait_ge(s["ylo"], n)
                    dve.tensor_tensor(yf[:], sg[:], gc[:], ALU.mult).then_inc(s["yf"], 1)

                def take_v(n, q):
                    dve.wait_ge(s["vproj"], n + 1)
                    if not (isinstance(n, int) and n == 0):
                        dve.wait_ge(s["vlo"], n)
                    dve.scalar_tensor_tensor(out=vf[:], in0=psp[:].rearrange("p (t n) -> p t n", t=TT),
                                             scalar=1.0 / WSCALE,
                                             in1=bv[:, q * P:(q + 1) * P].unsqueeze(1).to_broadcast([P, TT, P]),
                                             op0=ALU.mult, op1=ALU.add).then_inc(s["vf"], 1)

                def maxima(h, i):
                    for bank, tiles in BANK_TILES:
                        dve.wait_ge(s["scores"], h * 3 + bank + 1)
                        for j in tiles:
                            m = dve.tensor_reduce(nmax[:, i % 2, j:j + 1], cols(ps[i % 2], j), AX, ALU.max, negate=True)
                        m.then_inc(s["nmax"], 1)

                def turned_low(h, i):
                    for bank, width in ((0, 512), (1, 512), (2, 256)):
                        dve.wait_ge(s["thi"], h * 3 + bank + 1)
                        dve.tensor_tensor(t16[:, i % 2, 1, bank, 0:width], ps[i % 2][bank][:, 0:width],
                                          t16[:, i % 2, 0, bank, 0:width], ALU.subtract).then_inc(s["tlo"], 1)
                    if not isinstance(h, int) or h >= 2:
                        dve.wait_ge(s["o"], h - 1)
                    dve.reciprocal(rsum[:, i % 2, :], sums[:, i % 2, :]).then_inc(s["rsum"], 1)

                def out(h, q, i):
                    dve.wait_ge(s["pv"], h + 1)
                    dve.wait_ge(s["rsum"], h + 1)
                    dve.tensor_tensor(ob[:, q % 2, :, i * D1:(i + 1) * D1],
                                      pso[:, 0:P].rearrange("p (t n) -> p t n", t=TT),
                                      rsum[:, i % 2, :].unsqueeze(2).to_broadcast([P, TT, D1]),
                                      ALU.mult).then_inc(s["o"], 1)

                def ot_low(n, q):
                    dve.wait_ge(s["ot_hi"], n + 1)
                    dve.tensor_tensor(ot16[:, 1, q, :], psp[:], ot16[:, 0, q, :], ALU.subtract).then_inc(s["ot_lo"], 1)

                def output(b, co):
                    dve.wait_ge(s["proj"], b * CC + co + 1)
                    if co == 0:
                        dve.wait_ge(s["biased"], b * 2 + 2)
                    dve.scalar_tensor_tensor(out=x3[:, co, :], in0=psp[:], scalar=1.0 / WSCALE,
                                             in1=x3[:, co, :], op0=ALU.mult, op1=ALU.add).then_inc(s["x3"], 1)

                def add_bias(b, first):
                    dve.wait_ge(s["x3_loaded"], b * 16 + 16)
                    for co in range(first, first + 2):
                        i = dve.tensor_scalar(x3[:, co, :], x3[:, co, :], bp[:, co:co + 1], None, ALU.add)
                    i.then_inc(s["biased"], 1)

                for n in range(CC + 1):
                    condition(n)
                    if n == 0:
                        wkv.dve_prepare(dve, 0, 0)
                dve.wait_ge(s["fixed"], 48)
                dve.tensor_scalar(bq[:], bqk[:, 0, :], SCALE, None, ALU.mult).then_inc(s["bq"], 1)
                take_v(0, 0)
                maxima(0, 0)

                def batch(b, first):
                    for q in range(CC):
                        it = b * CC + q
                        for i in range(HPC):
                            h = b * H1 + (q * HPC + i)
                            maxima(h + 1, i + 1)
                            if i == 1 and (q or not first):
                                ot_low(it - 1, (q - 1) % CC)
                            turned_low(h, i)
                            if i or q or not first:
                                out(h - 1, q if i else q + 1, (i - 1) % HPC)
                            if i == 0:
                                wkv.dve_sums(dve, it, b, q * LAYERS + LAYER, it)
                                condition(it + AHEAD)
                            if i == 1:
                                wkv.dve_guard(dve, it)
                            if i == 2:
                                wkv.dve_finish(dve, it, b, it)
                                take_v(it + 1, (q + 1) % CC)
                            if i == 3:
                                wkv.dve_prepare(dve, it + 1, it + 1)
                                if q == 0 and not first:
                                    for co in range(CC):
                                        output(b - 1, co)
                                if q >= 2:
                                    add_bias(b, (q - 2) * 2)

                batch(0, True)
                with dve.Fori(1, B) as b:
                    batch(b, False)
                out(B * H1 - 1, CC - 1, HPC - 1)
                ot_low(B * CC - 1, CC - 1)
                for co in range(CC):
                    output(B - 1, co)


def layer1_ffn(k):
    nc, d = k.nc, k.d
    with ExitStack() as ctx:
        def sb(n, s, dt=F32):
            return ctx.enter_context(nc.sbuf_tensor("f_" + n, s, dt))

        stage = sb("stage", [P, 2, F // 2 * CC // 2])
        w0 = sb("w0", [P, 2, CC, F], F16)
        w1 = sb("w1", [P, 2, NF, C], F16)
        b0 = sb("b0", [P, NF])
        b1 = sb("b1", [P, CC])
        xt = sb("xt", [P, CC, T])
        gt = sb("gt", [P, CC, T])
        yf = sb("yf", [P, CC, T])
        y = sb("y", [P, CC, T], F16)
        h = sb("h", [P, NF, T], F16)
        e16 = sb("e16", [P, 2, T], F16)
        xo = sb("xo", [P, 2, T])
        psh = [ctx.enter_context(nc.psum_tensor(f"psf_h{i}", [P, 512], F32)) for i in range(4)]
        pse = [ctx.enter_context(nc.psum_tensor(f"psf_e{i}", [P, 512], F32)) for i in range(2)]
        s = {n: k.sem("f_" + n) for n in (
            "fixed", "raw0", "raw1", "hi", "lo", "x_loaded", "sig", "y", "hid", "gelu", "e_ps", "e16", "xo",
            "stored0", "stored1")}
        PIECE = F // 2 * CC // 2
        w0f = w0[:].rearrange("p s c n -> p s (c n)")
        w1f = w1[:].rearrange("p s c n -> p s (c n)")
        NP = CC * F // PIECE

        def piece(i):
            w, n = (w0f, i) if i < NP else (w1f, i - NP)
            return w[:, 0, n * PIECE:(n + 1) * PIECE], w[:, 1, n * PIECE:(n + 1) * PIECE]

        with nc.Block() as block:

            @block.sync
            def _(sp):
                def raw(i):
                    src = (d["w0"] if i < NP else d["w1"]).rearrange("p c n -> p (c n)")
                    n = i % NP
                    if i >= 2:
                        sp.wait_ge(s["lo"], i - 1)
                    sp.dma_start(stage[:, i % 2, :], src[:, n * PIECE:(n + 1) * PIECE]).then_inc(s[f"raw{i % 2}"], 16)

                sp.dma_start(b0[:], d["b0"]).then_inc(s["fixed"], 16)
                sp.dma_start(b1[:], d["b1"]).then_inc(s["fixed"], 16)
                for i in range(2 * NP):
                    raw(i)
                with sp.Fori(0, B) as b:
                    xsrc = d["x3"][bass.ds(b, 1)].rearrange("a c p n -> p (a c) n")
                    gsrc = d["gain"][3, bass.ds(b, 1)].rearrange("a c p n -> p (a c) n")
                    sp.wait_ge(s["xo"], b * CC + 1)
                    sp.dma_start(xt[:], xsrc).then_inc(s["x_loaded"], 16)
                    sp.dma_start(gt[:], gsrc).then_inc(s["x_loaded"], 16)
                    for co in range(CC):
                        dst = d["out"][bass.ds(b, 1), co].rearrange("a p n -> (a p) n")
                        sp.wait_ge(s["xo"], b * CC + co + 2)
                        sp.dma_start(dst, xo[:, co % 2, :]).then_inc(s[f"stored{co % 2}"], 16)
                for i in range(2):
                    sp.wait_ge(s[f"stored{i}"], 16 + 16 * B * CC // 2)

            @block.scalar
            def _(act):
                for i in range(2 * NP):
                    act.wait_ge(s[f"raw{i % 2}"], 16 * (i // 2 + 1))
                    act.activation(piece(i)[0], stage[:, i % 2, :], ACT.Copy, scale=WSCALE).then_inc(s["hi"], 1)
                act.wait_ge(s["fixed"], 32)
                with act.Fori(0, B) as b:
                    act.wait_ge(s["x_loaded"], b * 32 + 32)
                    for c in range(CC):
                        act.activation(yf[:, c, :], xt[:, c, :], ACT.Sigmoid).then_inc(s["sig"], 1)
                    for n in range(NF):
                        act.wait_ge(s["hid"], b * NF + n + 1)
                        act.activation(h[:, n, :], psh[n % 4][:], ACT.Gelu, bias=b0[:, n:n + 1],
                                       scale=1.0 / WSCALE).then_inc(s["gelu"], 1)
                    for co in range(CC):
                        act.wait_ge(s["e_ps"], b * CC + co + 1)
                        if co >= 2:
                            act.wait_ge(s["xo"], b * CC + co)
                        act.activation(e16[:, co % 2, :], pse[co % 2][:], ACT.Identity, bias=b1[:, co:co + 1],
                                       scale=1.0 / WSCALE).then_inc(s["e16"], 1)

            @block.tensor
            def _(pe):
                pe.sem_inc(s["xo"], 1)
                pe.wait_ge(s["lo"], 2 * NP)
                with pe.Fori(0, B) as b:
                    pe.wait_ge(s["y"], b * CC + CC)
                    for n in range(NF):
                        if n >= 4:
                            pe.wait_ge(s["gelu"], b * NF + n - 3)
                        for c in range(CC):
                            for part in range(2):
                                mm = pe.matmul(psh[n % 4][:], w0[:, part, c, n * P:(n + 1) * P], y[:, c, :],
                                               start=c + part == 0, stop=c == CC - 1 and part == 1)
                        mm.then_inc(s["hid"], 1)
                    pe.wait_ge(s["gelu"], b * NF + NF)
                    for co in range(CC):
                        if co >= 2:
                            pe.wait_ge(s["e16"], b * CC + co - 1)
                        for n in range(NF):
                            for part in range(2):
                                mm = pe.matmul(pse[co % 2][:], w1[:, part, n, co * P:(co + 1) * P], h[:, n, :],
                                               start=n + part == 0, stop=n == NF - 1 and part == 1)
                        mm.then_inc(s["e_ps"], 1)

            @block.vector
            def _(dve):
                for i in range(2):
                    dve.sem_inc(s[f"stored{i}"], 16)
                for i in range(2 * NP):
                    dve.wait_ge(s["hi"], i + 1)
                    hi, lo = piece(i)
                    dve.scalar_tensor_tensor(out=lo, in0=stage[:, i % 2, :], scalar=WSCALE, in1=hi,
                                             op0=ALU.mult, op1=ALU.subtract).then_inc(s["lo"], 1)
                with dve.Fori(0, B) as b:
                    for c in range(CC):
                        dve.wait_ge(s["sig"], b * CC + c + 1)
                        dve.tensor_tensor(y[:, c, :], yf[:, c, :], gt[:, c, :], ALU.mult).then_inc(s["y"], 1)
                    for co in range(CC):
                        dve.wait_ge(s["e16"], b * CC + co + 1)
                        dve.wait_ge(s[f"stored{co % 2}"], b * 32 + 16 * (co // 2) + 16)
                        dve.tensor_tensor(xo[:, co % 2, :], xt[:, co, :], e16[:, co % 2, :],
                                          ALU.add).then_inc(s["xo"], 1)


SCRATCH = {
    "gain": (LAYERS, B, CC, P, T), "x1": (B, CC, P, T), "x2": (B, CC, P, T), "x3": (B, CC, P, T),
    "slot_x": ((SLOT_TILES + 1) * P, C), "slot_y": (SLOT_TILES * P, C),
}


def rotation():
    half = D0 // 2
    inv = np.float32(1.0) / np.float32(10000.0) ** (np.arange(half, dtype=np.float32) / np.float32(half))
    th = np.arange(T, dtype=np.float32)[None, :] * inv[:, None]
    cos, sin = np.cos(th), np.sin(th)
    cos, sin = np.concatenate([cos, cos]), np.concatenate([-sin, sin])
    scale = np.float32(D0 ** -0.5)
    return np.ascontiguousarray(np.stack([cos * scale, sin * scale, cos, sin], 1) / np.float32(WSCALE).astype(np.float32))


def transposed(x):
    return np.ascontiguousarray(np.transpose(x, (0, 2, 1))).reshape(B, CC, P, T)


def layouts(i):
    a = {n: np.asarray(v) for n, v in i.items()}

    def rows(w):
        return np.ascontiguousarray(w.reshape(w.shape[0] // P, P, -1).transpose(1, 0, 2))

    cond = ["L0_cond", "L0_cond2", "L1_cond", "L1_cond2"]
    wu = np.stack([np.stack([a[n + "_" + x] for n in cond]) for x in "wu"])
    wqkv = np.stack([a["L0_attn_W" + x].reshape(CC, P, H0, D0) for x in "qkv"])
    down = np.zeros((E, KI * P, C), np.float32)
    down[:, :I] = a["L0_ffn_down_w"].transpose(0, 2, 1)
    qkv1 = a["L1_attn_w_attn"].reshape(CC, P, 3, CC, P)
    return {
        "xT": transposed(a["x"]),
        "fT": transposed(a["fside_BxSxS_0"]),
        "cond": np.ascontiguousarray(a["cond_512"].reshape(-1)),
        "wu": np.ascontiguousarray(wu.reshape(2, LAYERS, CC, P).transpose(3, 0, 2, 1).reshape(P, 2, CC * LAYERS)),
        "wqkv0": np.ascontiguousarray(wqkv.transpose(3, 2, 0, 1, 4)),
        "wo": np.ascontiguousarray(a["L0_attn_Wo"].reshape(H0, D0, C).transpose(1, 0, 2)),
        "wg": rows(a["L0_attn_Wg"]),
        "rot": rotation(),
        "router": rows(np.ascontiguousarray(a["L0_ffn_router_w"].T)),
        "gate_up": np.ascontiguousarray(np.stack([a["L0_ffn_gate_w"], a["L0_ffn_up_w"]], 1)
                                        .reshape(E, 2, I, CC, P).transpose(4, 0, 1, 3, 2)),
        "down": np.ascontiguousarray(down.reshape(E, KI, P, C).transpose(2, 0, 1, 3)),
        "wqkv1": np.ascontiguousarray(qkv1.transpose(3, 1, 2, 0, 4)),
        "bqkv1": np.ascontiguousarray(a["L1_attn_b_attn"].reshape(3, CC, P).transpose(2, 0, 1)),
        "bv1": np.ascontiguousarray(a["L1_attn_b_attn"].reshape(1, 3, C)[:, 2]),
        "wp1": rows(a["L1_attn_w_proj"]),
        "bp1": np.ascontiguousarray(a["L1_attn_b_proj"].reshape(CC, P).T),
        "w0": rows(np.ascontiguousarray(a["L1_ffn_W0"].T)),
        "b0": np.ascontiguousarray(a["L1_ffn_bias0"].reshape(NF, P).T),
        "w1": rows(np.ascontiguousarray(a["L1_ffn_W1"].T)),
        "b1": np.ascontiguousarray(a["L1_ffn_bias1"].reshape(CC, P).T),
    }


STAGES = [layer0_attn, moe_route, moe_experts, moe_combine, layer1_attn, layer1_ffn]


def program(nc, dram, stages=None):
    with ExitStack() as ctx:
        k = Core(nc, ctx, dram)
        constants(k)
        wkv_setup(k)
        for stage in (stages or STAGES):
            with nc.cleanup_on_exit():
                stage(k)


def kernel(**inputs):
    import concourse.bacc as bacc
    from concourse.bass_utils import run_bass_kernel_spmd

    nc = bacc.Bacc("TRN2", target_bir_lowering=False, num_devices=1)
    arrays, dram = {}, {}
    for name, a in layouts(inputs).items():
        arrays["in_" + name] = a
        dram[name] = nc.dram_tensor("in_" + name, a.shape, mybir.dt.from_np(a.dtype), kind="ExternalInput").ap()
    for name, shape in SCRATCH.items():
        dram[name] = nc.dram_tensor("scratch_" + name, shape, F32).ap()
    dram["out"] = nc.dram_tensor("out_0", (B, CC, P, T), F32, kind="ExternalOutput").ap()
    program(nc, dram)
    out = run_bass_kernel_spmd(nc, [arrays], core_ids=[0]).results[0]["out_0"]
    return np.ascontiguousarray(np.transpose(out.reshape(B, C, T), (0, 2, 1)))
```

```python
from contextlib import ExitStack

import numpy as np

import concourse.bass as bass
from concourse import mybir

ALU = mybir.AluOpType
ACT = mybir.ActivationFunctionType
AX = mybir.AxisListType.X
F32 = mybir.dt.float32
F16 = mybir.dt.float16
BF16 = mybir.dt.bfloat16
I32 = mybir.dt.int32

P = 128
B, T, C = 4, 512, 512
CC = C // P
TT = T // P
LAYERS = 4
NEG = -1e30
EXP30 = float(np.exp(30.0))

H0, D0 = 16, 128
NBLK, BLK = 8, 64
WIN = 64
H1, D1 = 16, 32
HPC = P // D1
E, I = 8, 352
KI = (I + P - 1) // P
NT = B * TT
SLOT_TILES = NT + E - 1
F = 2048
NF = F // P
WSCALE = 64.0


class Tally:

    def __init__(self, sem, start=0):
        self.sem, self.n, self.base = sem, start, 0

    def inc(self, instruction):
        instruction.then_inc(self.sem, 1)
        self.n += 1
        return self.n


def score_columns(j):
    return {3: (0, 0), 2: (1, 0), 0: (1, 384), 1: (2, 0)}[j]


BANK_TILES = ((0, (3,)), (1, (2, 0)), (2, (1,)))


def turned_columns(m):
    return {0: (0, 0), 1: (1, 0), 3: (1, 384), 2: (2, 0)}[m]


class Core:

    def __init__(self, nc, ctx, dram):
        self.nc, self.ctx, self.d = nc, ctx, dram

    def sem(self, name):
        return self.nc.alloc_semaphore(name=name)

    def scratch(self, name, shape):
        return self.nc.dram_tensor(name, shape, F32).ap()


def constants(k):
    nc, ctx = k.nc, k.ctx
    k.ident = ctx.enter_context(nc.sbuf_tensor("ident", [P, P], F32))
    k.ident_b = ctx.enter_context(nc.sbuf_tensor("ident_b", [P, P], BF16))
    k.causal_b = ctx.enter_context(nc.sbuf_tensor("causal_b", [P, P], BF16))
    k.slot = ctx.enter_context(nc.sbuf_tensor("slot", [P, NT], I32))
    k.weight = ctx.enter_context(nc.sbuf_tensor("weight", [P, NT], F32))
    k.tile_expert = ctx.enter_context(nc.sbuf_tensor("tile_expert", [P, SLOT_TILES], I32))
    k.zeros = ctx.enter_context(nc.sbuf_tensor("zeros", [P, C], F32))
    made = k.sem("const_made")
    with nc.Block() as block:

        @block.gpsimd
        def _(pool):
            pool.memset(k.ident[:], 0.0).then_inc(made, 1)
            pool.memset(k.ident_b[:], 0.0).then_inc(made, 1)
            pool.memset(k.causal_b[:], 0.0).then_inc(made, 1)
            pool.memset(k.zeros[:], 0.0).then_inc(made, 1)
            pool.wait_ge(made, 4)
            for m in (k.ident, k.ident_b):
                pool.affine_select(out=m[:], in_=m[:], compare_op=ALU.not_equal, fill=1.0, base=0,
                                   pattern=[[-1, P]], channel_multiplier=1).then_inc(made, 1)
            pool.affine_select(out=k.causal_b[:], in_=k.causal_b[:], compare_op=ALU.is_ge, fill=NEG,
                               base=0, pattern=[[-1, P]], channel_multiplier=1).then_inc(made, 1)


class Wkv:

    def __init__(self, k, ctx, name, tiles):
        nc = k.nc
        self.k, self.tiles = k, tiles

        def sb(n, s):
            return ctx.enter_context(nc.sbuf_tensor(f"{name}_{n}", s, F32))

        self.kt = [sb(f"kt{i}", [P, T]) for i in range(tiles)]
        self.ek_raw, self.ek, self.ekv = sb("ek_raw", [P, T]), sb("ek", [P, T]), sb("ekv", [P, T])
        self.euk_raw, self.euk, self.eukv = sb("euk_raw", [P, T]), sb("euk", [P, T]), sb("eukv", [P, T])
        self.nf, self.df = sb("nf", [P, T + 1]), sb("df", [P, T + 1])
        self.nb, self.db = sb("nb", [P, T]), sb("db", [P, T])
        self.num, self.den = sb("num", [P, T]), sb("den", [P, T])
        self.lnd, self.r0, self.gain = sb("lnd", [P, T]), sb("r0", [P, T]), sb("gain", [P, T])
        self.s = {n: k.sem(f"{name}_{n}") for n in (
            "ek_raw", "ek", "ekv", "euk_raw", "euk", "eukv", "scan", "part", "joined", "den", "ln", "r0",
            "newton", "gain", "stored", "zeroed")}
        self.loaded = [k.sem(f"{name}_loaded{i}") for i in range(tiles)]

    def source(self, b, c):
        return self.k.d["fT"][bass.ds(b, 1), bass.ds(c, 1)].rearrange("a c p n -> (a c p) n")

    def act_load(self, act, tile, b, c, units_done):
        src = self.source(b, c)
        if units_done is not None:
            act.wait_ge(self.s["eukv"], units_done)
        act.dma_start(self.kt[tile][:], src).then_inc(self.loaded[tile], 16)

    def act_prepare(self, act, tile, u, n, p=None, loads=None):
        if p is not None:
            act.wait_ge(self.loaded[tile], loads * 16)
            act.wait_ge(self.s["ek"], p)
            act.activation(self.ek_raw[:], self.kt[tile][:], ACT.Exp).then_inc(self.s["ek_raw"], 1)
        act.wait_ge(self.s["euk"], u)
        act.activation(self.euk_raw[:], self.kt[tile][:], ACT.Exp,
                       bias=self.k.wu[:, 1, bass.ds(n, 1)]).then_inc(self.s["euk_raw"], 1)

    def act_invert(self, act, u):
        act.wait_ge(self.s["den"], u + 1)
        act.activation(self.lnd[:], self.den[:], ACT.Ln).then_inc(self.s["ln"], 1)
        act.wait_ge(self.s["ln"], u + 1)
        act.activation(self.r0[:], self.lnd[:], ACT.Exp, scale=-1.0).then_inc(self.s["r0"], 1)

    def act_store(self, act, u, layer, b, c):
        dst = self.k.d["gain"][layer, bass.ds(b, 1), bass.ds(c, 1)].rearrange("a c p n -> (a c p) n")
        act.wait_ge(self.s["gain"], u + 1)
        act.dma_start(dst, self.gain[:]).then_inc(self.s["stored"], 16)

    def pool_prepare(self, pool, tile, u, p=None):
        s = self.s
        if p is not None:
            pool.wait_ge(s["ek"], p + 1)
            pool.tensor_tensor(self.ekv[:], self.ek[:], self.kt[tile][:], ALU.mult).then_inc(s["ekv"], 1)
        pool.wait_ge(s["euk"], u + 1)
        pool.tensor_tensor(self.eukv[:], self.euk[:], self.kt[tile][:], ALU.mult).then_inc(s["eukv"], 1)

    def join(self, eng, u):
        s = self.s
        eng.wait_ge(s["part"], u + 1)
        eng.tensor_tensor(self.den[:], self.den[:], self.euk[:], ALU.add).then_inc(s["joined"], 1)
        eng.wait_ge(s["eukv"], u + 1)
        eng.tensor_tensor(self.num[:], self.num[:], self.eukv[:], ALU.add).then_inc(s["joined"], 1)

    def dve_zero(self, dve):
        dve.memset(self.nf[:, 0:1], 0.0)
        dve.memset(self.df[:, 0:1], 0.0).then_inc(self.s["zeroed"], 1)
        dve.wait_ge(self.s["zeroed"], 1)

    def dve_prepare(self, dve, u, p=None):
        s = self.s
        if p is not None:
            dve.wait_ge(s["ek_raw"], p + 1)
            dve.tensor_scalar(self.ek[:], self.ek_raw[:], EXP30, None, ALU.min).then_inc(s["ek"], 1)
        dve.wait_ge(s["euk_raw"], u + 1)
        dve.tensor_scalar(self.euk[:], self.euk_raw[:], EXP30, None, ALU.min).then_inc(s["euk"], 1)

    def dve_sums(self, dve, u, b, n, p):
        s = self.s
        dec = self.k.decay[:, bass.ds(b, 1), bass.ds(n, 1)].rearrange("p a n -> p (a n)")
        dect = dec.to_broadcast([P, T])
        if not (isinstance(u, int) and u == 0):
            dve.wait_ge(s["gain"], u)
        for step, (src, fw, bw) in enumerate(((self.ek, self.df, self.db), (self.ekv, self.nf, self.nb))):
            dve.wait_ge(s["ekv" if step else "ek"], p + 1)
            dve.tensor_tensor_scan(fw[:, 1:T + 1], dect, src[:], 0.0, ALU.mult, ALU.add)
            dve.tensor_tensor_scan(bw[:, ::-1], dect, src[:, ::-1], 0.0, ALU.mult, ALU.add).then_inc(s["scan"], 1)
        for step, (out, fw, bw) in enumerate(((self.den, self.df, self.db), (self.num, self.nf, self.nb))):
            dve.wait_ge(s["scan"], u * 2 + 1 + step)
            i = dve.scalar_tensor_tensor(out=out[:], in0=fw[:, 0:T], scalar=dec, in1=bw[:],
                                         op0=ALU.mult, op1=ALU.add)
        i.then_inc(s["part"], 1)

    def dve_guard(self, dve, u):
        dve.wait_ge(self.s["joined"], u * 2 + 2)
        dve.tensor_scalar(self.den[:], self.den[:], 1e-8, None, ALU.max).then_inc(self.s["den"], 1)

    def dve_finish(self, dve, u, b, stores):
        s = self.s
        dve.wait_ge(s["r0"], u + 1)
        dve.tensor_tensor(self.db[:], self.den[:], self.r0[:], ALU.mult).then_inc(s["newton"], 1)
        dve.wait_ge(s["newton"], u * 2 + 1)
        dve.scalar_tensor_tensor(out=self.nb[:], in0=self.db[:], scalar=-2.0, in1=self.r0[:],
                                 op0=ALU.add, op1=ALU.mult).then_inc(s["newton"], 1)
        dve.wait_ge(s["newton"], u * 2 + 2)
        if not (isinstance(stores, int) and stores == 0):
            dve.wait_ge(s["stored"], stores * 16)
        dve.scalar_tensor_tensor(out=self.gain[:], in0=self.num[:], scalar=self.k.negf[:, bass.ds(b, 1)],
                                 in1=self.nb[:], op0=ALU.mult, op1=ALU.mult).then_inc(s["gain"], 1)


def wkv_setup(k):
    nc, d, ctx = k.nc, k.d, k.ctx
    UNITS = CC * LAYERS
    k.wu = ctx.enter_context(nc.sbuf_tensor("wu", [P, 2, UNITS], F32))
    k.decay = ctx.enter_context(nc.sbuf_tensor("decay", [P, B, UNITS], F32))
    k.negf = ctx.enter_context(nc.sbuf_tensor("negf", [P, B], F32))
    with ExitStack() as tmp:
        def sb(n, s):
            return tmp.enter_context(nc.sbuf_tensor("ws_" + n, s, F32))

        cond = sb("cond", [P, B, P])
        csum, tf, halff = sb("csum", [P, B]), sb("tf", [P, B]), sb("halff", [P, B])
        ew, dk = sb("ew", [P, UNITS]), sb("dk", [P, UNITS])
        loaded, act_step, dve_step = k.sem("ws_loaded"), k.sem("ws_act_step"), k.sem("ws_dve_step")
        with nc.Block() as block:

            @block.sync
            def _(sp):
                sp.dma_start(k.wu[:], d["wu"]).then_inc(loaded, 16)
                sp.dma_start(cond[:].rearrange("p b n -> p (b n)"),
                             d["cond"].partition_broadcast(P)).then_inc(loaded, 16)

            @block.scalar
            def _(act):
                act.wait_ge(loaded, 32)
                act.activation(ew[:], k.wu[:, 0, :], ACT.Exp).then_inc(act_step, 1)
                act.wait_ge(act_step, 1)
                act.activation(dk[:], ew[:], ACT.Exp, scale=-1.0).then_inc(act_step, 1)
                act.wait_ge(dve_step, 1)
                act.activation(tf[:], csum[:], ACT.Sigmoid).then_inc(act_step, 1)
                act.preload_act_table_set("natural_log_exp_and_others")

            @block.vector
            def _(dve):
                dve.wait_ge(loaded, 32)
                dve.tensor_reduce(csum[:], cond[:], AX, ALU.add).then_inc(dve_step, 1)
                dve.wait_ge(act_step, 3)
                dve.tensor_scalar(halff[:], tf[:], 0.5, 0.5, ALU.mult, ALU.add).then_inc(dve_step, 1)
                dve.tensor_scalar(k.negf[:], tf[:], -0.2, -0.8, ALU.mult, ALU.add).then_inc(dve_step, 1)
                dve.wait_ge(dve_step, 3)
                for i in range(B):
                    dve.tensor_scalar(k.decay[:, i, :], dk[:], halff[:, i:i + 1], None,
                                      ALU.mult).then_inc(dve_step, 1)
                dve.wait_ge(dve_step, 3 + B)


def layer0_attn(k):
    nc, d = k.nc, k.d
    G = H0 // CC
    with ExitStack() as ctx:
        def sb(n, s, dt=F32):
            return ctx.enter_context(nc.sbuf_tensor("a0_" + n, s, dt))

        wraw = sb("wraw", [P, 3, CC, D0])
        w16 = sb("w16", [P, 2, 2, 3, CC, D0], F16)
        wo16 = sb("wo16", [P, 2, CC, G, C], F16)
        wg = sb("wg", [P, CC, 3 * H0])
        wg16 = sb("wg16", [P, 2, CC, 3 * H0], F16)
        rot = sb("rot", [P, 4, T])
        xc = sb("xc", [P, T])
        sg = sb("sg", [P, T])
        yf = sb("yf", [P, T])
        y16 = sb("y16", [P, 2, CC, T], F16)
        ynext = sb("ynext", [P, 2, CC, T], F16)
        of = sb("of", [P, T])
        o16 = sb("o16", [P, 2, 2, G, T], F16)
        acc = sb("acc", [P, CC, T])
        ra = sb("ra", [P, 2, T])
        rb = sb("rb", [P, 2, T])
        qk = sb("qk", [P, 2, T])
        ksum = sb("ksum", [P, NBLK])
        v = sb("v", [P, 2, TT, D0])
        gate_raw = sb("gate_raw", [P, TT, 3 * H0])
        gate = sb("gate", [P, H0, 3, TT])
        seen = sb("seen", [P, TT])
        wmask = sb("wmask", [P, 3 * BLK])
        cmask = sb("cmask", [P, TT, NBLK])
        nmax = sb("nmax", [P, 2, TT])
        cmax = sb("cmax", [P, TT])
        sums = sb("sums", [P, 3, TT])
        rsum = sb("rsum", [P, 3, TT])
        coef = sb("coef", [P, 3, TT])
        ef = sb("ef", [P, 3, 512])
        sw = sb("sw", [P, TT, 3 * BLK])
        ewn = sb("ewn", [P, TT, 3 * BLK])
        sc = sb("sc", [P, TT, NBLK])
        sc2 = sb("sc2", [P, TT, NBLK])
        ec = sb("ec", [P, TT, NBLK])
        pc = sb("pc", [P, TT, NBLK])
        pt = sb("pt", [P, 3, 512])
        tt_ = sb("tt_", [P, 3, 512])
        ps = [ctx.enter_context(nc.psum_tensor(f"ps0_s{i}", [P, 512], F32)) for i in range(3)]
        psq = [ctx.enter_context(nc.psum_tensor(f"ps0_q{i}", [P, 512], F32)) for i in range(2)]
        psv = ctx.enter_context(nc.psum_tensor("ps0_v", [P, 512], F32))
        pso = ctx.enter_context(nc.psum_tensor("ps0_o", [P, 512], F32))
        psg = ctx.enter_context(nc.psum_tensor("ps0_g", [P, 512], F32))
        s = {n: k.sem("a0_" + n) for n in (
            "const", "wraw", "w64", "whi", "w_ready0", "w_ready1", "w_kept0", "w_kept1", "rot", "wg_loaded", "wg64", "wg_hi", "wg_lo",
            "x_loaded", "sig_step", "sig", "yf", "yhi", "ylo", "y_here", "gates_raw", "gates_step",
            "gates_sig", "gates", "qproj", "cosed", "swapped", "roped", "q_sb", "ksum", "vproj", "v_sb", "scores",
            "nmax", "expd", "cmp_step", "cmp_e", "coef", "p_step", "p", "turned", "t_sb", "pv", "of", "o_hi", "o_lo",
            "wo_raw0", "wo_raw1", "wo64", "wo_hi", "wo_lo", "out_ps", "acc", "acc_loaded", "x1_stored", "zeroed")}
        CMP_STEPS = 5
        wkv = Wkv(k, ctx, "wkv0", 2)
        wo_raw = (acc, sb("wo_raw", [P, G, C]))
        PER = 3

        def cols(t, j, lo=0, hi=None):
            bank, c0 = score_columns(j)
            hi = P * (j + 1) if hi is None else hi
            return t[bank][:, c0 + lo:c0 + hi] if isinstance(t, list) else t[:, bank, c0 + lo:c0 + hi]

        def win(t, j):
            return cols(t, j, max(0, P * j - WIN))

        def wcols(t, j):
            lo = 0 if j else WIN
            return t[:, j, lo:] if len(t.shape) == 3 else t[:, lo:]

        def ynew(part, c, n):
            if isinstance(n, int) and n < CC:
                return y16[:, part, c, :]
            return ynext[:, part, bass.ds(c, 1), :].rearrange("p a n -> p (a n)")

        def wo_part(part, c):
            return wo16[:, part, bass.ds(c, 1)].rearrange("p a h n -> p (a h) n")

        def o_part(group, part, i):
            return o16[:, bass.ds(group, 1), part, i, :].rearrange("p a n -> p (a n)")

        def group_units(b, c):
            return (b * CC + c) * PER + CC, (b * CC + c) * 2 + CC

        kept = nc.dram_tensor("wqkv0_split", [H0 + 1] + list(w16.shape[:1]) + list(w16.shape[2:]), F16)

        def pairs(b, c, i):
            return b * (H0 // 2) + c * (G // 2) + (i // 2 + 1)

        def run(eng, group, last, after_first=lambda: None):
            group(0, 0, True, False)
            with eng.Fori(1, CC) as c:
                group(0, c, False, False)
            after_first()
            with eng.Fori(1, B) as b:
                group(b, 0, True, True)
                with eng.Fori(1, CC) as c:
                    group(b, c, False, False)
            last()

        with nc.Block() as block:

            @block.sync
            def _(sp):
                def weights(h):
                    src = d["wqkv0"][bass.ds(h, 1)].rearrange("a p k c n -> p (a k) c n")
                    sp.dma_start(wraw[:], src).then_inc(s["wraw"], 16)

                def keep(h, i):
                    dst = kept[bass.ds(h, 1)].rearrange("a p m k c n -> p (a m) k c n")
                    sp.dma_start(dst, w16[:, i]).then_inc(s[f"w_kept{i}"], 16)

                def fetch(g, h, i):
                    src = kept[bass.ds(h, 1)].rearrange("a p m k c n -> p (a m) k c n")
                    sp.wait_ge(s["vproj"], g - 1)
                    sp.dma_start(w16[:, i], src).then_inc(s[f"w_ready{i}"], 16)

                def all_kept():
                    for i in range(2):
                        sp.wait_ge(s[f"w_kept{i}"], 16 * (H0 // 2 + 1 - i))

                def x_chunk(b, c, n):
                    src = d["xT"][bass.ds(b, 1), bass.ds(c, 1)].rearrange("a c p n -> (a c p) n")
                    sp.wait_ge(s["sig"], n)
                    sp.dma_start(xc[:], src).then_inc(s["x_loaded"], 16)

                def move_y(b):
                    sp.wait_ge(s["vproj"], b * H0)
                    sp.dma_start(y16[:], ynext[:]).then_inc(s["y_here"], 16)

                def residual(b, co, n):
                    src = d["xT"][bass.ds(b, 1), co].rearrange("a p n -> (a p) n")
                    if n is not None:
                        sp.wait_ge(s["x1_stored"], n * 16)
                    sp.dma_start(acc[:, co, :], src).then_inc(s["acc_loaded"], 16)

                def zero_slots(it):
                    rows = (SLOT_TILES + 1) * P // (B * CC)
                    dst = d["slot_x"][bass.ds(it * rows, rows), :].rearrange("(p r) c -> p r c", r=2)
                    sp.dma_start(dst, k.zeros[0:rows // 2, :].unsqueeze(1).to_broadcast([rows // 2, 2, C])
                                 ).then_inc(s["zeroed"], 16)

                def store(b, co):
                    dst = d["x1"][bass.ds(b, 1), co].rearrange("a p n -> (a p) n")
                    sp.wait_ge(s["acc"], (b * CC + (CC - 1)) * CC + co + 2)
                    sp.dma_start(dst, acc[:, co, :]).then_inc(s["x1_stored"], 16)

                def group(b, c, first, output_before):
                    if output_before:
                        move_y(b)
                    for i in range(G):
                        if i == 0:
                            x_chunk((b + 1) % B, c, (b + 1) * CC + c)
                        if isinstance(b, int):
                            other = (i + 1) % 2
                            sp.wait_ge(s[f"w_ready{other}"], 16 * pairs(b, c, i + 1))
                            weights((c * G + (i + 2)) % H0)
                            keep(c * G + (i + 1), other)
                        else:
                            fetch(b * H0 + c * G + (i + 2), (c * G + (i + 2)) % H0, i % 2)
                        if output_before:
                            store(b - 1, i)
                            residual(b, i, (b - 1) * CC + (i + 1))
                        if i == 2:
                            zero_slots(b * CC + c)

                def wo_load(c):
                    sp.dma_start(wo_raw[c % 2][:], d["wo"][:, c * G:(c + 1) * G]).then_inc(s[f"wo_raw{c % 2}"], 16)

                sp.dma_start(wg[:], d["wg"]).then_inc(s["wg_loaded"], 16)
                x_chunk(0, 0, 0)
                weights(0)
                sp.dma_start(rot[:], d["rot"]).then_inc(s["rot"], 16)
                wo_load(0)
                wo_load(1)
                x_chunk(0, 1, 1)
                sp.wait_ge(s["w_ready0"], 16)
                weights(1)
                keep(0, 0)
                for c in range(2, CC):
                    x_chunk(0, c, c)
                    sp.wait_ge(s["wo_lo"], c - 1)
                    wo_load(c)
                sp.wait_ge(s["wo_lo"], CC - 1)
                for co in range(CC):
                    residual(0, co, None)
                run(sp, group, lambda: [store(B - 1, co) for co in range(CC)], all_kept)
                for i in range(2):
                    sp.wait_ge(s[f"w_ready{i}"], 16 * (B * H0 // 2 + 1))
                sp.wait_ge(s["x1_stored"], 16 * B * CC)
                sp.wait_ge(s["zeroed"], 16 * B * CC)

            @block.gpsimd
            def _(pool):
                pool.memset(wmask[:], 0.0).then_inc(s["const"], 1)
                pool.memset(cmask[:], 0.0).then_inc(s["const"], 1)
                pool.memset(seen[:], 1.0 / BLK).then_inc(s["const"], 1)
                pool.wait_ge(s["const"], 3)
                pool.affine_select(out=wmask[:], in_=wmask[:], compare_op=ALU.is_ge, fill=NEG, base=0,
                                   pattern=[[1, 3 * BLK]], channel_multiplier=-1).then_inc(s["const"], 1)
                pool.wait_ge(s["const"], 4)
                pool.affine_select(out=wmask[:], in_=wmask[:], compare_op=ALU.is_ge, fill=NEG, base=WIN,
                                   pattern=[[-1, 3 * BLK]], channel_multiplier=1).then_inc(s["const"], 1)
                pool.affine_select(out=cmask[:], in_=cmask[:], compare_op=ALU.is_ge, fill=NEG, base=1 - BLK,
                                   pattern=[[P, TT], [-BLK, NBLK]], channel_multiplier=1).then_inc(s["const"], 1)
                pool.affine_select(out=seen[:], in_=seen[:], compare_op=ALU.is_ge, fill=0.0, base=1 - BLK,
                                   pattern=[[P, TT]], channel_multiplier=1).then_inc(s["const"], 1)

                def y_low(c, n):
                    pool.wait_ge(s["yhi"], n + 1)
                    pool.tensor_tensor(ynew(1, c, n), yf[:], ynew(0, c, n), ALU.subtract).then_inc(s["ylo"], 1)

                def o_low(g, group, i):
                    pool.wait_ge(s["o_hi"], g + 1)
                    pool.tensor_tensor(o_part(group, 1, i), of[:], o_part(group, 0, i), ALU.subtract).then_inc(s["o_lo"], 1)

                def split(g, i):
                    pool.wait_ge(s["whi"], g + 1)
                    pool.tensor_tensor(w16[:, i, 1], wraw[:], w16[:, i, 0], ALU.subtract).then_inc(s[f"w_ready{i}"], 16)

                def rope(g, n):
                    pool.wait_ge(s["swapped"], g * 2 + n + 1)
                    pool.tensor_tensor(rb[:, n, :], rb[:, n, :], rot[:, 2 * n + 1, :],
                                       ALU.mult).then_inc(s["roped"], 1)
                    pool.wait_ge(s["cosed"], g * 2 + n + 1)
                    pool.wait_ge(s["roped"], g * 2 + n + 1)
                    pool.tensor_tensor(qk[:, n, :], ra[:, n, :], rb[:, n, :], ALU.add).then_inc(s["q_sb"], 1)

                pool.wait_ge(s["wg_hi"], 1)
                pool.tensor_tensor(wg16[:, 1], wg[:], wg16[:, 0], ALU.subtract).then_inc(s["wg_lo"], 1)
                wkv.pool_prepare(pool, 0, 0, 0)
                for c in range(CC):
                    wkv.pool_prepare(pool, (c + 1) % 2, c + 1, c + 1)
                    if c < 2:
                        split(c, c)
                    if c == CC - 1:
                        y_low(c, c)
                        pool.wait_ge(s["ylo"], CC)
                        pool.sem_inc(s["y_here"], 16)
                    pool.wait_ge(s["wo_hi"], c + 1)
                    pool.tensor_tensor(wo_part(1, c), wo_raw[c % 2][:], wo_part(0, c),
                                       ALU.subtract).then_inc(s["wo_lo"], 1)
                    if c < CC - 1:
                        y_low(c, c)

                def group(b, c, first, output_before):
                    u, p = group_units(b, c)
                    for i in range(G):
                        g = b * H0 + c * G + i
                        rope(g, 1)
                        if i == 1:
                            y_low(c, (b + 1) * CC + c)
                        if i == 0 and (output_before or not first):
                            o_low(g - 1, (b * CC + c + 1) % 2, G - 1)
                        if i < PER:
                            wkv.join(pool, u + i)
                        if i:
                            o_low(g - 1, (b * CC + c) % 2, i - 1)
                        if i == 0:
                            wkv.pool_prepare(pool, 1, u + 1, p + 1)
                        if i == 1:
                            wkv.pool_prepare(pool, 1, u + 2)
                        if i == 3:
                            wkv.pool_prepare(pool, 0, u + 3, p + 2)
                        rope(g + 1, 0)
                        if isinstance(b, int):
                            split(g + 2, i % 2)

                rope(0, 0)
                run(pool, group, lambda: o_low(B * H0 - 1, (B * CC - 1) % 2, G - 1))

            @block.scalar
            def _(act):
                def split(g, i):
                    act.wait_ge(s["wraw"], g * 16 + 16)
                    act.activation(wraw[:], wraw[:], ACT.Copy, scale=WSCALE).then_inc(s["w64"], 1)
                    act.wait_ge(s["w64"], g + 1)
                    act.activation(w16[:, i, 0], wraw[:], ACT.Copy).then_inc(s["whi"], 1)

                def sigmoid(out, x, steps, before, done, scale=-1.0):
                    act.activation(out, x, ACT.Exp, scale=scale).then_inc(steps, 1)
                    act.wait_ge(steps, before + 1)
                    act.activation(out, out, ACT.Ln, bias=1.0).then_inc(steps, 1)
                    act.wait_ge(steps, before + 2)
                    act.activation(out, out, ACT.Exp, scale=-1.0).then_inc(done, 1)

                def y_sigmoid(n):
                    act.wait_ge(s["x_loaded"], n * 16 + 16)
                    act.wait_ge(s["yf"], n)
                    sigmoid(sg[:], xc[:], s["sig_step"], n * 2, s["sig"])

                def y_high(c, n):
                    act.wait_ge(s["yf"], n + 1)
                    act.activation(ynew(0, c, n), yf[:], ACT.Copy).then_inc(s["yhi"], 1)

                for tile in range(2):
                    wkv.act_load(act, tile, 0, tile, None)
                act.wait_ge(s["wg_loaded"], 16)
                act.activation(wg[:], wg[:], ACT.Copy, scale=WSCALE).then_inc(s["wg64"], 1)
                act.wait_ge(s["wg64"], 1)
                act.activation(wg16[:, 0], wg[:], ACT.Copy).then_inc(s["wg_hi"], 1)
                wkv.act_prepare(act, 0, 0, 0, 0, 1)
                for c in range(CC):
                    y_sigmoid(c)
                    wkv.act_load(act, c % 2, *((0, c + 2) if c + 2 < CC else (1 - c % 2, 0)), c + 1)
                    wkv.act_prepare(act, (c + 1) % 2, c + 1, (c + 1) % CC * LAYERS, c + 1, (c + 1) // 2 + 1)
                    wkv.act_invert(act, c)
                    if c < 2:
                        split(c, c)
                    if c == CC - 1:
                        y_high(c, c)
                    act.wait_ge(s[f"wo_raw{c % 2}"], c // 2 * 16 + 16)
                    act.activation(wo_raw[c % 2][:], wo_raw[c % 2][:], ACT.Copy, scale=WSCALE).then_inc(s["wo64"], 1)
                    act.wait_ge(s["wo64"], c + 1)
                    act.activation(wo_part(0, c), wo_raw[c % 2][:], ACT.Copy).then_inc(s["wo_hi"], 1)
                    if c < CC - 1:
                        y_high(c, c)

                def swap(g, n):
                    act.wait_ge(s["cosed"], g * 2 + n + 1)
                    act.activation(rb[0:64, n, :], psq[n][64:P, :], ACT.Copy)
                    act.activation(rb[64:P, n, :], psq[n][0:64, :], ACT.Copy).then_inc(s["swapped"], 1)

                def exps(g):
                    for bank, tiles in BANK_TILES:
                        act.wait_ge(s["nmax"], g * 3 + bank + 1)
                        for j in tiles:
                            act.activation(cols(ef, j), cols(ps, j), ACT.Exp, bias=nmax[:, 0, j:j + 1],
                                           accum_out=sums[:, 1, j:j + 1]).then_inc(s["expd"], 1)
                            act.activation(wcols(ewn, j), wcols(sw, j), ACT.Exp, bias=nmax[:, 1, j:j + 1],
                                           scale=-1.0, accum_out=sums[:, 2, j:j + 1]).then_inc(s["expd"], 1)
                    act.wait_ge(s["cmp_step"], g * CMP_STEPS + 2)
                    act.activation(ec[:], sc2[:], ACT.Exp).then_inc(s["cmp_e"], 1)

                def turn(g, group, i):
                    for m in range(3):
                        act.wait_ge(s["turned"], g * 3 + m + 1)
                        w = 256 if m == 2 else 512
                        act.activation(tt_[:, m, 0:w], ps[m][:, 0:w], ACT.Copy).then_inc(s["t_sb"], 1)
                    act.wait_ge(s["pv"], g + 1)
                    act.wait_ge(s["o_lo"], g)
                    act.activation(of[:], pso[:], ACT.Copy).then_inc(s["of"], 1)
                    act.wait_ge(s["of"], g + 1)
                    act.activation(o_part(group, 0, i), of[:], ACT.Copy).then_inc(s["o_hi"], 1)

                def group(b, c, first, output_before):
                    u, p = group_units(b, c)
                    for i in range(G):
                        g = b * H0 + c * G + i
                        if first and i == 0:
                            act.wait_ge(s["gates_raw"], b + 1)
                            sigmoid(gate_raw[:], psg[:, 0:TT * 3 * H0].rearrange("p (t n) -> p t n", t=TT),
                                    s["gates_step"], b * 2, s["gates_sig"], -1.0 / WSCALE)
                        swap(g, 1)
                        act.wait_ge(s["vproj"], g + 1)
                        act.activation(v[:, i % 2].rearrange("p t n -> p (t n)"), psv[:], ACT.Copy,
                                       scale=1.0 / WSCALE).then_inc(s["v_sb"], 1)
                        if i or output_before or not first:
                            turn(g - 1, (b * CC + c + (i == 0)) % 2, (i + G - 1) % G)
                        it = b * CC + c
                        if i == 0:
                            wkv.act_prepare(act, 1, u + 1, c * LAYERS + 1, p + 1, it + 3)
                        if i == 1:
                            wkv.act_prepare(act, 1, u + 2, c * LAYERS + 2)
                            act.wait_ge(s["y_here"], b * 16 + 16)
                            y_high(c, (b + 1) * CC + c)
                        if i == 3:
                            wkv.act_prepare(act, 0, u + 3, (c + 1) % CC * LAYERS, p + 2, it + 4)
                        exps(g)
                        swap(g + 1, 0)
                        if i < PER:
                            wkv.act_invert(act, u + i)
                        if isinstance(b, int):
                            act.wait_ge(s[f"w_kept{i % 2}"], 16 * pairs(b, c, i))
                            split(g + 2, i % 2)
                        if i == 0:
                            y_sigmoid((b + 1) * CC + c)
                            wkv.act_load(act, 0, ((it + 1) // CC + 1) % B, (it + 1) % CC, u + 1)
                        if i == 2:
                            wkv.act_store(act, u + 1, 1, b, c)
                            wkv.act_load(act, 1, (it + 1) // CC % B, (it + 1) % CC, u + 3)
                        if i == 3:
                            wkv.act_store(act, u + 2, 2, b, c)

                swap(0, 0)
                run(act, group, lambda: turn(B * H0 - 1, (B * CC - 1) % 2, G - 1))
                act.wait_ge(wkv.s["stored"], 16 * 2 * B * CC)
                for tile, loads in enumerate((B * CC + 3, B * CC + 3)):
                    act.wait_ge(wkv.loaded[tile], loads * 16)

            @block.tensor
            def _(pe):
                PARTS = ((0, 0), (0, 1), (1, 0))

                def gates(b):
                    pe.wait_ge(s["y_here"], b * 16 + 16)
                    for t in range(TT):
                        for c in range(CC):
                            for n, (yp, wp) in enumerate(PARTS):
                                mm = pe.matmul(psg[:, t * 48:t * 48 + 48], y16[:, yp, c, t * P:(t + 1) * P],
                                               wg16[:, wp, c, :], start=c + n == 0, stop=c == CC - 1 and n == 2)
                    mm.then_inc(s["gates_raw"], 1)

                def project(g, i, ready):
                    pe.wait_ge(s[f"w_ready{i % 2}"], ready)
                    for n in range(2):
                        for c in range(CC):
                            for m, (yp, wp) in enumerate(PARTS):
                                mm = pe.matmul(psq[n][:], w16[:, i % 2, wp, n, c, :], y16[:, yp, c, :],
                                               start=c + m == 0, stop=c == CC - 1 and m == 2)
                        mm.then_inc(s["qproj"], 1)
                    pe.wait_ge(s["v_sb"], g)
                    for t in range(TT):
                        for c in range(CC):
                            for m, (yp, wp) in enumerate(PARTS):
                                mm = pe.matmul(psv[:, t * D0:(t + 1) * D0], y16[:, yp, c, t * P:(t + 1) * P],
                                               w16[:, i % 2, wp, 2, c, :], start=c + m == 0, stop=c == CC - 1 and m == 2)
                    mm.then_inc(s["vproj"], 1)

                def scores(g):
                    pe.wait_ge(s["q_sb"], g * 2 + 2)
                    for bank, tiles in BANK_TILES:
                        for j in tiles:
                            pe.matmul(cols(ps, j), qk[:, 0, j * P:(j + 1) * P], qk[:, 1, 0:P * (j + 1)],
                                      start=True, stop=False)
                            mm = pe.matmul(cols(ps, j, P * j), k.ident_b[:], k.causal_b[:],
                                           start=False, stop=True)
                        if bank == 2:
                            pe.wait_ge(s["ksum"], g + 1)
                            for j in range(TT):
                                mm = pe.matmul(ps[2][:, 256 + j * NBLK:256 + (j + 1) * NBLK],
                                               qk[:, 0, j * P:(j + 1) * P], ksum[:], start=True, stop=True)
                        mm.then_inc(s["scores"], 1)

                def values(g, i):
                    for bank, tiles in ((0, (0,)), (1, (1, 3)), (2, (2,))):
                        if bank == 0:
                            pe.wait_ge(s["p"], g * TT + TT)
                        for m in tiles:
                            _, c0 = turned_columns(m)
                            for j in range(m, TT):
                                mm = pe.transpose(ps[bank][:, c0 + (j - m) * P:c0 + (j - m + 1) * P],
                                                  cols(pt, j, m * P, (m + 1) * P), k.ident[:])
                        mm.then_inc(s["turned"], 1)
                    for n, m in enumerate((0, 1, 3, 2)):
                        bank, c0 = turned_columns(m)
                        if n == 0:
                            pe.wait_ge(s["of"], g)
                        pe.wait_ge(s["t_sb"], g * 3 + bank + 1)
                        mm = pe.matmul(pso[:, m * P:], v[:, i % 2, m, :], tt_[:, bank, c0:c0 + T - m * P],
                                       start=n == 0, stop=n == TT - 1)
                    mm.then_inc(s["pv"], 1)

                def output(group, og, c, co):
                    if co == 0:
                        pe.wait_ge(s["o_lo"], group * G + G)
                    pe.wait_ge(s["acc"], group * CC + co + 1)
                    for h in range(G):
                        for m, (op, wp) in enumerate(PARTS):
                            mm = pe.matmul(psg[:], wo16[:, wp, bass.ds(c, 1), h, co * P:(co + 1) * P]
                                           .rearrange("p a n -> p (a n)"),
                                           o_part(og, op, h), start=h + m == 0, stop=h == G - 1 and m == 2)
                    mm.then_inc(s["out_ps"], 1)

                def group(b, c, first, output_before):
                    it = b * CC + c
                    og, oc = (it + 1) % 2, (c + (CC - 1)) % CC
                    for i in range(G):
                        g = b * H0 + c * G + i
                        before = output_before or not first
                        if first and i == 0:
                            if output_before:
                                pe.wait_ge(s["acc"], (it - 1) * CC + 1)
                            gates(b)
                        project(g, i, 16 * pairs(b, c, i))
                        if i and before:
                            output(it - 1, og, oc, i)
                        if i or before:
                            values(g - 1, i + G - 1)
                        scores(g)
                        if i == 0 and before:
                            if first:
                                pe.wait_ge(s["gates_sig"], b + 1)
                            output(it - 1, og, oc, 0)

                def last():
                    pe.sem_inc(s["qproj"], 1)
                    values(B * H0 - 1, G - 1)
                    for co in range(CC):
                        output(B * CC - 1, (B * CC - 1) % 2, CC - 1, co)

                pe.wait_ge(s["wg_lo"], 1)
                run(pe, group, last)

            @block.vector
            def _(dve):
                wkv.dve_zero(dve)
                dve.sem_inc(s["acc"], 1)

                def condition(n):
                    dve.wait_ge(s["sig"], n + 1)
                    dve.wait_ge(s["ylo"], n)
                    dve.tensor_tensor(yf[:], sg[:], wkv.gain[:], ALU.mult).then_inc(s["yf"], 1)

                wkv.dve_prepare(dve, 0, 0)
                for c in range(CC):
                    wkv.dve_sums(dve, c, 0, c * LAYERS, c)
                    wkv.join(dve, c)
                    wkv.dve_guard(dve, c)
                    wkv.dve_prepare(dve, c + 1, c + 1)
                    wkv.dve_finish(dve, c, 0, 0)
                    dve.wait_ge(wkv.s["gain"], c + 1)
                    condition(c)
                dve.wait_ge(s["const"], 7)
                dve.wait_ge(s["rot"], 16)

                def gates(b):
                    dve.wait_ge(s["gates_sig"], b + 1)
                    dve.tensor_copy(gate[:].rearrange("p h k t -> p t k h"),
                                    gate_raw[:].rearrange("p t (k h) -> p t k h", k=3)).then_inc(s["gates"], 1)
                    dve.wait_ge(s["gates"], b * 2 + 1)
                    dve.tensor_tensor(gate[:, :, 0, :], gate[:, :, 0, :],
                                      seen[:].unsqueeze(1).to_broadcast([P, H0, TT]), ALU.mult).then_inc(s["gates"], 1)

                def rope(g, n):
                    dve.wait_ge(s["qproj"], g * 2 + n + 1)
                    dve.wait_ge(s["q_sb"], g * 2 + n)
                    dve.tensor_tensor(ra[:, n, :], psq[n][:], rot[:, 2 * n, :], ALU.mult).then_inc(s["cosed"], 1)

                def sum_keys(g):
                    dve.wait_ge(s["q_sb"], g * 2 + 2)
                    dve.tensor_reduce(ksum[:], qk[:, 1, :].rearrange("p (m n) -> p m n", n=BLK), AX,
                                      ALU.add).then_inc(s["ksum"], 1)

                def softmax(b, g, h, between):
                    c = g * CMP_STEPS
                    for bank, tiles in BANK_TILES:
                        dve.wait_ge(s["scores"], g * 3 + bank + 1)
                        for j in tiles:
                            dve.tensor_reduce(nmax[:, 0, j:j + 1], cols(ps, j), AX, ALU.max, negate=True)
                            i = dve.tensor_tensor_reduce(out=wcols(sw, j), in0=win(ps, j), in1=wcols(wmask, j),
                                                         scale=-1.0, scalar=3.0e38, op0=ALU.add, op1=ALU.min,
                                                         accum_out=nmax[:, 1, j:j + 1])
                        if bank == 2:
                            i = dve.scalar_tensor_tensor(
                                out=sc[:], in0=ps[2][:, 256:256 + TT * NBLK].rearrange("p (t m) -> p t m", t=TT),
                                scalar=1.0 / BLK, in1=cmask[:], op0=ALU.mult, op1=ALU.add)
                        i.then_inc(s["nmax"], 1)
                    dve.wait_ge(s["nmax"], g * 3 + 3)
                    dve.tensor_reduce(cmax[:], sc[:], AX, ALU.max).then_inc(s["cmp_step"], 1)
                    dve.wait_ge(s["cmp_step"], c + 1)
                    dve.tensor_tensor(sc2[:], sc[:], cmax[:].unsqueeze(2).to_broadcast([P, TT, NBLK]),
                                      ALU.subtract).then_inc(s["cmp_step"], 1)
                    between()
                    dve.wait_ge(s["cmp_e"], g + 1)
                    dve.tensor_reduce(sums[:, 0, :], ec[:], AX, ALU.add).then_inc(s["cmp_step"], 1)
                    dve.wait_ge(s["cmp_step"], c + 3)
                    dve.wait_ge(s["expd"], g * 2 * TT + 2 * TT)
                    dve.wait_ge(s["gates"], b * 2 + 2)
                    dve.reciprocal(rsum[:], sums[:]).then_inc(s["cmp_step"], 1)
                    dve.wait_ge(s["cmp_step"], c + 4)
                    dve.tensor_tensor(coef[:], rsum[:], gate[:, bass.ds(h, 1)].rearrange("p a k t -> p (a k) t"),
                                      ALU.mult).then_inc(s["cmp_step"], 1)
                    dve.wait_ge(s["cmp_step"], c + 5)
                    dve.tensor_tensor(pc[:], ec[:], coef[:, 0, :].unsqueeze(2).to_broadcast([P, TT, NBLK]),
                                      ALU.mult).then_inc(s["coef"], 1)
                    dve.wait_ge(s["coef"], g + 1)
                    for n, j in enumerate((3, 2, 1, 0)):
                        dve.scalar_tensor_tensor(
                            out=cols(pt, j).rearrange("p (m n) -> p m n", n=BLK),
                            in0=cols(ef, j).rearrange("p (m n) -> p m n", n=BLK), scalar=coef[:, 1, j:j + 1],
                            in1=pc[:, j, 0:2 * (j + 1)].unsqueeze(2).to_broadcast([P, 2 * (j + 1), BLK]),
                            op0=ALU.mult, op1=ALU.add).then_inc(s["p_step"], 1)
                    for n, j in enumerate((3, 2, 1, 0)):
                        dve.wait_ge(s["p_step"], g * TT + n + 1)
                        dve.scalar_tensor_tensor(out=win(pt, j), in0=wcols(ewn, j), scalar=coef[:, 2, j:j + 1],
                                                 in1=win(pt, j), op0=ALU.mult, op1=ALU.add).then_inc(s["p"], 1)

                def output(group, co, loads):
                    dve.wait_ge(s["out_ps"], group * CC + co + 1)
                    dve.wait_ge(s["acc_loaded"], loads * 16)
                    dve.scalar_tensor_tensor(out=acc[:, co, :], in0=psg[:], scalar=1.0 / WSCALE, in1=acc[:, co, :],
                                             op0=ALU.mult, op1=ALU.add).then_inc(s["acc"], 1)

                def group(b, c, first, output_before):
                    u, p = group_units(b, c)
                    bn, it = (b + 1) % B, b * CC + c
                    for i in range(G):
                        g = b * H0 + c * G + i
                        if first and i == 0:
                            gates(b)
                        rope(g, 1)
                        if i == 0:
                            wkv.dve_sums(dve, u, bn, c * LAYERS, p)
                        if i == 1:
                            wkv.dve_finish(dve, u, bn, it * 2)
                            dve.wait_ge(wkv.s["gain"], u + 1)
                            condition((b + 1) * CC + c)
                            wkv.dve_sums(dve, u + 1, b, c * LAYERS + 1, p + 1)
                        if i == 2:
                            dve.wait_ge(s["yf"], (b + 1) * CC + c + 1)
                            wkv.dve_finish(dve, u + 1, b, it * 2)
                            wkv.dve_sums(dve, u + 2, b, c * LAYERS + 2, p + 1)
                        if i == 3:
                            wkv.dve_finish(dve, u + 2, b, it * 2 + 1)

                        def between():
                            if i == 0 and (output_before or not first):
                                output(it - 1, 0, b * CC if first else b * CC + CC)
                            if i < PER:
                                wkv.dve_guard(dve, u + i)
                            if i == 0:
                                wkv.dve_prepare(dve, u + 1, p + 1)
                            if i == 1:
                                wkv.dve_prepare(dve, u + 2)
                            if i == 3:
                                wkv.dve_prepare(dve, u + 3, p + 2)
                            rope(g + 1, 0)

                        if i and (output_before or not first):
                            output(it - 1, i, b * CC if first else b * CC + CC)
                        sum_keys(g)
                        softmax(b, g, c * G + i, between)

                rope(0, 0)
                run(dve, group, lambda: [output(B * CC - 1, co, B * CC) for co in range(CC)])


class ExpertWeights:

    def __init__(self, k, ctx):
        self.gate_up = ctx.enter_context(k.nc.sbuf_tensor("gate_up", [P, E, 2, CC, I], F32))
        self.down = ctx.enter_context(k.nc.sbuf_tensor("down", [P, E, KI, C], F32))
        self.loaded = [k.sem(f"expert_loaded{e}") for e in range(E)]


def moe_and_attention(k):
    with ExitStack() as ctx:
        w = ExpertWeights(k, ctx)
        moe_route(k, w)
        moe_experts(k, w)
    with ExitStack() as ctx:
        w = Layer1Weights(k, ctx)
        moe_combine(k, w)
        layer1_attn(k, w)


def moe_route(k, w):
    nc, d = k.nc, k.d
    with ExitStack() as ctx:
        def sb(n, s, dt=F32):
            return ctx.enter_context(nc.sbuf_tensor("mr_" + n, s, dt))

        wr = sb("wr", [P, CC, E])
        xt = sb("xt", [P, CC, T])
        gt = sb("gt", [P, CC, T])
        yt = sb("yt", [P, CC, T])
        rows = sb("rows", [P, NT, C])
        logits = sb("logits", [P, NT, E])
        top = sb("top", [P, NT, 8])
        first = sb("first", [P, E])
        pick = sb("pick", [P, NT, E])
        best = sb("best", [P, NT])
        onehot = sb("onehot", [P, NT, E])
        before = sb("before", [P, NT + 1, E])
        diff = sb("diff", [P, NT])
        ones = sb("ones", [P, P])
        prior = sb("prior", [P, P])
        steps = sb("steps", [P, E, NT])
        over = sb("over", [P, E, NT])
        tiles = sb("tiles", [P, E])
        count = sb("count", [P, E])
        ends = sb("ends", [P, E])
        base = sb("base", [P, E])
        place = sb("place", [P, NT, E])
        slotf = sb("slotf", [P, NT])
        tile_no = sb("tile_no", [P, SLOT_TILES, E])
        past = sb("past", [P, SLOT_TILES, E])
        expertf = sb("expertf", [P, SLOT_TILES])
        psr = ctx.enter_context(nc.psum_tensor("psr_l", [P, 512], F32))
        pst = [ctx.enter_context(nc.psum_tensor(f"psr_t{i}", [P, 512], F32)) for i in range(2)]
        pss = ctx.enter_context(nc.psum_tensor("psr_s", [P, 512], F32))
        s = {n: k.sem("mr_" + n) for n in (
            "router", "x_loaded", "const", "sig", "y", "logits_ps", "logits", "rows_ps",
            "rows", "math", "sums", "exp", "slots", "scattered")}
        with nc.Block() as block:

            @block.sync
            def _(sp):
                sp.dma_start(wr[:], d["router"]).then_inc(s["router"], 16)
                for b in range(B):
                    if b:
                        sp.wait_ge(s["sig"], b * CC)
                    sp.dma_start(xt[:], d["x1"][b].rearrange("c p n -> p c n")).then_inc(s["x_loaded"], 16)
                    if b:
                        sp.wait_ge(s["y"], b * CC)
                    sp.dma_start(gt[:], d["gain"][1, b].rearrange("c p n -> p c n")).then_inc(s["x_loaded"], 16)
                for e in range(E):
                    sp.dma_start(w.gate_up[:, e], d["gate_up"][:, e]).then_inc(w.loaded[e], 16)
                    sp.dma_start(w.down[:, e], d["down"][:, e]).then_inc(w.loaded[e], 16)

            @block.gpsimd
            def _(pool):
                pool.memset(ones[:], 1.0).then_inc(s["const"], 1)
                pool.memset(prior[:], 1.0).then_inc(s["const"], 1)
                pool.iota(first[:], pattern=[[-1, E]], base=E, channel_multiplier=0,
                          allow_small_or_imprecise_dtypes=True).then_inc(s["const"], 1)
                pool.iota(steps[:], pattern=[[0, E], [P, NT]], base=0, channel_multiplier=0,
                          allow_small_or_imprecise_dtypes=True).then_inc(s["const"], 1)
                pool.iota(tile_no[:], pattern=[[1, SLOT_TILES], [0, E]], base=0, channel_multiplier=0,
                          allow_small_or_imprecise_dtypes=True).then_inc(s["const"], 1)
                pool.wait_ge(s["const"], 5)
                pool.affine_select(out=prior[:], in_=prior[:], compare_op=ALU.is_gt, fill=0.0, base=0,
                                   pattern=[[1, P]], channel_multiplier=-1).then_inc(s["const"], 1)
                pool.wait_ge(s["slots"], 1)
                pool.wait_ge(s["rows"], NT)
                for i in range(NT):
                    pool.indirect_dma_start(d["slot_x"], bass.IndirectOffsetOnAxis(ap=k.slot[:, i:i + 1], axis=0),
                                            rows[:, i, :], None).then_inc(s["scattered"], 16)
                pool.wait_ge(s["scattered"], 16 * NT)

            @block.scalar
            def _(act):
                with act.Fori(0, B) as b:
                    act.wait_ge(s["x_loaded"], b * 32 + 32)
                    for c in range(CC):
                        act.activation(yt[:, c, :], xt[:, c, :], ACT.Sigmoid).then_inc(s["sig"], 1)
                    for t in range(TT):
                        act.wait_ge(s["rows_ps"], b * TT + t + 1)
                        act.activation(rows[:, bass.ds(b * TT + t, 1), :].rearrange("p a n -> p (a n)"),
                                       pst[t % 2][:], ACT.Copy).then_inc(s["rows"], 1)
                act.wait_ge(s["math"], 1)
                act.activation(diff[:], diff[:], ACT.Exp).then_inc(s["exp"], 1)

            @block.tensor
            def _(pe):
                pe.wait_ge(s["router"], 16)
                with pe.Fori(0, B) as b:
                    pe.wait_ge(s["y"], b * CC + CC)
                    for t in range(TT):
                        for c in range(CC):
                            mm = pe.matmul(psr[:, t * E:(t + 1) * E], yt[:, c, t * P:(t + 1) * P], wr[:, c, :],
                                           start=c == 0, stop=c == CC - 1)
                    mm.then_inc(s["logits_ps"], 1)
                    for t in range(TT):
                        if t >= 2:
                            pe.wait_ge(s["rows"], b * TT + t - 1)
                        for c in range(CC):
                            mm = pe.transpose(pst[t % 2][:, c * P:(c + 1) * P], yt[:, c, t * P:(t + 1) * P], k.ident[:])
                        mm.then_inc(s["rows_ps"], 1)
                pe.wait_ge(s["math"], 2)
                pe.wait_ge(s["const"], 6)
                pe.matmul(pss[:, 0:NT * E], prior[:], onehot[:].rearrange("p t e -> p (t e)"), start=True, stop=False)
                pe.matmul(pss[:, 0:NT * E], ones[:], before[:, 0:NT, :].rearrange("p t e -> p (t e)"),
                          start=False, stop=True)
                pe.matmul(pss[:, NT * E:NT * E + E], ones[:], before[:, NT, :], start=True,
                          stop=True).then_inc(s["sums"], 1)

            @block.vector
            def _(dve):
                with dve.Fori(0, B) as b:
                    for c in range(CC):
                        dve.wait_ge(s["sig"], b * CC + c + 1)
                        dve.tensor_tensor(yt[:, c, :], yt[:, c, :], gt[:, c, :], ALU.mult).then_inc(s["y"], 1)
                    dve.wait_ge(s["logits_ps"], b + 1)
                    dve.tensor_copy(logits[:, bass.ds(b * TT, TT), :],
                                    psr[:, 0:TT * E].rearrange("p (t e) -> p t e", t=TT)).then_inc(s["logits"], 1)
                dve.wait_ge(s["const"], 6)
                dve.wait_ge(s["logits"], B)
                for i in range(NT):
                    m = dve.max(top[:, i, :], logits[:, i, :])
                step = Tally(k.sem("mr_step"))

                def then(ins):
                    dve.wait_ge(step.sem, step.inc(ins))

                def wide(a, n=E):
                    return a.unsqueeze(2).to_broadcast([P, a.shape[1], n])

                then(m)
                dve.tensor_tensor(diff[:], top[:, :, 1], top[:, :, 0], ALU.subtract).then_inc(s["math"], 1)
                then(dve.tensor_tensor(pick[:], logits[:], wide(top[:, :, 0]), ALU.is_equal))
                then(dve.tensor_tensor(pick[:], pick[:], first[:].unsqueeze(1).to_broadcast([P, NT, E]), ALU.mult))
                then(dve.tensor_reduce(best[:], pick[:], AX, ALU.max))
                then(dve.memset(before[:, 0, :], 0.0))
                then(dve.tensor_tensor(onehot[:], wide(best[:]), first[:].unsqueeze(1).to_broadcast([P, NT, E]),
                                       ALU.is_equal))
                for i in range(NT):
                    then(dve.tensor_tensor(before[:, i + 1, :], before[:, i, :], onehot[:, i, :], ALU.add))
                dve.wait_ge(s["exp"], 1)
                then(dve.tensor_scalar(diff[:], diff[:], 1.0, None, ALU.add))
                dve.reciprocal(k.weight[:], diff[:]).then_inc(s["math"], 1)
                dve.wait_ge(s["sums"], 1)
                then(dve.tensor_copy(count[:], pss[:, NT * E:NT * E + E]))
                then(dve.tensor_tensor(over[:], wide(count[:], NT), steps[:], ALU.is_gt))
                then(dve.tensor_reduce(tiles[:], over[:], AX, ALU.add))
                then(dve.tensor_tensor_scan(ends[:], ones[:, 0:E], tiles[:], 0.0, ALU.mult, ALU.add))
                then(dve.tensor_tensor(base[:], ends[:], tiles[:], ALU.subtract))
                then(dve.tensor_scalar(base[:], base[:], float(P), None, ALU.mult))
                then(dve.tensor_tensor(place[:], pss[:, 0:NT * E].rearrange("p (t e) -> p t e", t=NT),
                                       base[:].unsqueeze(1).to_broadcast([P, NT, E]), ALU.add))
                then(dve.tensor_tensor(place[:], place[:], onehot[:], ALU.mult))
                then(dve.tensor_reduce(slotf[:], place[:], AX, ALU.add))
                dve.tensor_copy(k.slot[:], slotf[:]).then_inc(s["slots"], 1)
                then(dve.tensor_tensor(past[:], tile_no[:], ends[:].unsqueeze(1).to_broadcast([P, SLOT_TILES, E]),
                                       ALU.is_ge))
                then(dve.tensor_reduce(expertf[:], past[:], AX, ALU.add))
                then(dve.tensor_scalar(expertf[:], expertf[:], float(E - 1), None, ALU.min))
                then(dve.tensor_copy(k.tile_expert[:], expertf[:]))


def moe_experts(k, w):
    nc, d = k.nc, k.d
    with ExitStack() as ctx:
        def sb(n, s, dt=F32):
            return ctx.enter_context(nc.sbuf_tensor("me_" + n, s, dt))

        xin = sb("xin", [P, 2, C])
        xT = sb("xT", [P, 2, C])
        sg = sb("sg", [P, I])
        a = sb("a", [P, 2, KI * P])
        aT = sb("aT", [P, KI * P])
        yo = sb("yo", [P, 2, C])
        psx = ctx.enter_context(nc.psum_tensor("pse_x", [P, 512], F32))
        psg = ctx.enter_context(nc.psum_tensor("pse_g", [P, 512], F32))
        psu = ctx.enter_context(nc.psum_tensor("pse_u", [P, 512], F32))
        psa = ctx.enter_context(nc.psum_tensor("pse_a", [P, 512], F32))
        psd = ctx.enter_context(nc.psum_tensor("pse_d", [P, 512], F32))
        s = {n: k.sem("me_" + n) for n in (
            "experts", "x0", "x1", "x_ps", "xT", "gu", "silu", "a", "a_pad", "a_ps", "aT", "down", "y", "stored0",
            "stored1")}
        last = SLOT_TILES - 1
        with nc.Block() as block:

            @block.sync
            def _(sp):
                def load(j, i, dyn):
                    src = d["slot_x"][bass.ds(j * P, P), :] if dyn else d["slot_x"][j * P:(j + 1) * P, :]
                    if dyn:
                        sp.wait_ge(s["x_ps"], j - 1)
                    sp.dma_start(xin[:, i, :], src).then_inc(s[f"x{i}"], 16)

                def store(j, i, dyn):
                    dst = d["slot_y"][bass.ds(j * P, P), :] if dyn else d["slot_y"][j * P:(j + 1) * P, :]
                    sp.wait_ge(s["y"], j + 1)
                    sp.dma_start(dst, yo[:, i, :]).then_inc(s[f"stored{i}"], 16)

                load(0, 0, False)
                load(1, 1, False)
                with sp.Fori(1, last // 2 + 1) as m:
                    for i in range(2):
                        load(m * 2 + i, i, True)
                        store(m * 2 + (i - 2), i, True)
                store(last, last % 2, False)
                for i in range(2):
                    sp.wait_ge(s[f"stored{i}"], 16 + 16 * ((SLOT_TILES + 1 - i) // 2))

            @block.gpsimd
            def _(pool):
                for e in range(E):
                    pool.wait_ge(w.loaded[e], 32)
                    pool.sem_inc(s["experts"], 1)

            @block.tensor
            def _(pe):
                pe.wait_ge(s["a_pad"], 1)

                def turn_x(j, i, first):
                    pe.wait_ge(s[f"x{i}"], (j // 2 if isinstance(j, int) else (j - i) // 2) * 16 + 16)
                    if not first:
                        pe.wait_ge(s["xT"], j)
                    for c in range(CC):
                        mm = pe.transpose(psx[:, c * P:(c + 1) * P], xin[:, i, c * P:(c + 1) * P], k.ident[:])
                    mm.then_inc(s["x_ps"], 1)

                def gate_up(j, i):
                    e = pe.value_load(k.tile_expert[0:1, bass.ds(j, 1)], min_val=0, max_val=E - 1)
                    pe.wait_ge(s["experts"], e + 1)
                    pe.wait_ge(s["xT"], j + 1)
                    for n, ps in enumerate((psg, psu)):
                        for c in range(CC):
                            mm = pe.matmul(ps[:, 0:I], xT[:, i, c * P:(c + 1) * P],
                                           w.gate_up[:, bass.ds(e, 1), n, c, :].rearrange("p a n -> p (a n)"),
                                           start=c == 0, stop=c == CC - 1)
                    mm.then_inc(s["gu"], 1)

                def turn_a(j, i):
                    pe.wait_ge(s["a"], j + 1)
                    for c in range(KI):
                        mm = pe.transpose(psa[:, c * P:(c + 1) * P], a[:, i, c * P:(c + 1) * P], k.ident[:])
                    mm.then_inc(s["a_ps"], 1)

                def down(j, i, first):
                    e = pe.value_load(k.tile_expert[0:1, bass.ds(j, 1)], min_val=0, max_val=E - 1)
                    pe.wait_ge(s["aT"], j + 1)
                    if not first:
                        pe.wait_ge(s["y"], j)
                    for c in range(KI):
                        mm = pe.matmul(psd[:], aT[:, c * P:(c + 1) * P],
                                       w.down[:, bass.ds(e, 1), c, :].rearrange("p a n -> p (a n)"),
                                       start=c == 0, stop=c == KI - 1)
                    mm.then_inc(s["down"], 1)

                turn_x(0, 0, True)
                gate_up(0, 0)
                turn_x(1, 1, False)
                def step(j, i, first):
                    turn_a(j - 1, 1 - i)
                    gate_up(j, i)
                    turn_x(j + 1, 1 - i, False)
                    down(j - 1, 1 - i, first)

                step(1, 1, True)
                step(2, 0, False)
                with pe.Fori(2, last // 2 + 1) as m:
                    step(m * 2 - 1, 1, False)
                    step(m * 2, 0, False)
                turn_a(last, last % 2)
                down(last, last % 2, False)

            @block.scalar
            def _(act):
                def take_x(j, i):
                    act.wait_ge(s["x_ps"], j + 1)
                    act.activation(xT[:, i, :], psx[:], ACT.Copy).then_inc(s["xT"], 1)

                def silu(j):
                    act.wait_ge(s["gu"], j + 1)
                    act.activation(sg[:], psg[:, 0:I], ACT.Silu).then_inc(s["silu"], 1)

                take_x(0, 0)
                silu(0)
                take_x(1, 1)
                with act.Fori(1, last // 2 + 1) as m:
                    silu(m * 2 - 1)
                    take_x(m * 2, 0)
                    silu(m * 2)
                    take_x(m * 2 + 1, 1)

            @block.vector
            def _(dve):
                for i in range(2):
                    dve.sem_inc(s[f"stored{i}"], 16)
                dve.memset(a[:], 0.0).then_inc(s["a_pad"], 1)
                dve.wait_ge(s["a_pad"], 1)

                def mul(j, i):
                    dve.wait_ge(s["silu"], j + 1)
                    dve.tensor_tensor(a[:, i, 0:I], sg[:], psu[:, 0:I], ALU.mult).then_inc(s["a"], 1)

                def take_a(j):
                    dve.wait_ge(s["a_ps"], j + 1)
                    dve.tensor_copy(aT[:], psa[:, 0:KI * P]).then_inc(s["aT"], 1)

                def out(j, i, half):
                    dve.wait_ge(s["down"], j + 1)
                    dve.wait_ge(s[f"stored{i}"], half * 16 + 16)
                    dve.tensor_copy(yo[:, i, :], psd[:]).then_inc(s["y"], 1)

                mul(0, 0)
                with dve.Fori(1, last // 2 + 1) as m:
                    take_a(m * 2 - 2)
                    mul(m * 2 - 1, 1)
                    out(m * 2 - 2, 0, m - 1)
                    take_a(m * 2 - 1)
                    mul(m * 2, 0)
                    out(m * 2 - 1, 1, m - 1)
                take_a(last)
                out(last, last % 2, last // 2)


def moe_combine(k, w):
    nc, d = k.nc, k.d
    with ExitStack() as ctx:
        def sb(n, s, dt=F32):
            return ctx.enter_context(nc.sbuf_tensor("mc_" + n, s, dt))

        got = sb("got", [P, NT, C])
        yw = sb("yw", [P, 2, C])
        xt = sb("xt", [P, 2, CC, T])
        ps = [ctx.enter_context(nc.psum_tensor(f"psc_{i}", [P, 512], F32)) for i in range(2)]
        s = {n: k.sem("mc_" + n) for n in ("x0", "x1", "weighted", "turned", "x2", "stored")}
        gathered = [k.sem(f"mc_gathered{b}") for b in range(B)]
        with nc.Block() as block:

            @block.gpsimd
            def _(pool):
                for i in range(NT):
                    pool.indirect_dma_start(got[:, i, :], None, d["slot_y"],
                                            bass.IndirectOffsetOnAxis(ap=k.slot[:, i:i + 1], axis=0)
                                            ).then_inc(gathered[i // TT], 16)
                w.pool_split(pool)

            @block.scalar
            def _(act):
                w.act_split(act)

            @block.sync
            def _(sp):
                for b in range(B):
                    if b >= 2:
                        sp.wait_ge(s["stored"], 16 * (b - 1))
                    sp.dma_start(xt[:, b % 2], d["x1"][b].rearrange("c p n -> p c n")).then_inc(s[f"x{b % 2}"], 16)
                    if b >= 1:
                        sp.wait_ge(s["x2"], TT * b)
                        sp.dma_start(d["x2"][b - 1].rearrange("c p n -> p c n"), xt[:, (b - 1) % 2]).then_inc(s["stored"], 16)
                sp.wait_ge(s["x2"], TT * B)
                sp.dma_start(d["x2"][B - 1].rearrange("c p n -> p c n"), xt[:, (B - 1) % 2]).then_inc(s["stored"], 16)
                sp.wait_ge(s["stored"], 16 * B)

            @block.tensor
            def _(pe):
                for i in range(NT):
                    pe.wait_ge(s["weighted"], i + 1)
                    if i >= 2:
                        pe.wait_ge(s["x2"], i - 1)
                    for c in range(CC):
                        mm = pe.transpose(ps[i % 2][:, c * P:(c + 1) * P], yw[:, i % 2, c * P:(c + 1) * P], k.ident[:])
                    mm.then_inc(s["turned"], 1)

            @block.vector
            def _(dve):
                def weigh(i):
                    dve.wait_ge(gathered[i // TT], 16 * TT)
                    if i >= 2:
                        dve.wait_ge(s["turned"], i - 1)
                    dve.tensor_scalar(yw[:, i % 2, :], got[:, i, :], k.weight[:, i:i + 1], None,
                                      ALU.mult).then_inc(s["weighted"], 1)

                weigh(0)
                for i in range(NT):
                    if i + 1 < NT:
                        weigh(i + 1)
                    b, t = divmod(i, TT)
                    if t == 0:
                        dve.wait_ge(s[f"x{b % 2}"], 16 * (b // 2 + 1))
                    dve.wait_ge(s["turned"], i + 1)
                    x = xt[:, b % 2, :, t * P:(t + 1) * P]
                    dve.tensor_tensor(x, ps[i % 2][:].rearrange("p (c n) -> p c n", c=CC), x, ALU.add).then_inc(s["x2"], 1)


class Layer1Weights:

    def __init__(self, k, ctx):
        def sb(n, s, dt=F32):
            return ctx.enter_context(k.nc.sbuf_tensor("w1_" + n, s, dt))

        self.k = k
        self.raw = sb("raw", [P, 2, 3, CC, P])
        self.w16 = sb("w16", [P, 2, CC, 3, CC, P], F16)
        self.wp = sb("wp", [P, CC, C])
        self.wp16 = sb("wp16", [P, 2, CC, C], F16)
        self.s = {n: k.sem("w1_" + n) for n in ("raw0", "raw1", "w64", "whi", "wlo")}

    def act_split(self, act):
        s, d = self.s, self.k.d

        def load(n):
            if n < CC:
                if n >= 2:
                    act.wait_ge(s["wlo"], n - 1)
                act.dma_start(self.raw[:, n % 2], d["wqkv1"][n]).then_inc(s[f"raw{n % 2}"], 16)

        act.dma_start(self.wp[:], d["wp1"]).then_inc(s["raw0"], 16)
        load(0)
        load(1)
        for n in range(CC):
            act.wait_ge(s[f"raw{n % 2}"], (n // 2 + 1 + (n % 2 == 0)) * 16)
            src = self.raw[:, n % 2]
            act.activation(src, src, ACT.Copy, scale=WSCALE).then_inc(s["w64"], 1)
            act.wait_ge(s["w64"], n + 1)
            act.activation(self.w16[:, 0, n], src, ACT.Copy).then_inc(s["whi"], 1)
            load(n + 2)
        act.activation(self.wp[:], self.wp[:], ACT.Copy, scale=WSCALE).then_inc(s["w64"], 1)
        act.wait_ge(s["w64"], CC + 1)
        act.activation(self.wp16[:, 0], self.wp[:], ACT.Copy).then_inc(s["whi"], 1)

    def pool_split(self, pool):
        s = self.s
        for n in range(CC):
            pool.wait_ge(s["whi"], n + 1)
            pool.tensor_tensor(self.w16[:, 1, n], self.raw[:, n % 2], self.w16[:, 0, n],
                               ALU.subtract).then_inc(s["wlo"], 1)
        pool.wait_ge(s["whi"], CC + 1)
        pool.tensor_tensor(self.wp16[:, 1], self.wp[:], self.wp16[:, 0], ALU.subtract).then_inc(s["wlo"], 1)


def layer1_attn(k, w):
    nc, d = k.nc, k.d
    with ExitStack() as ctx:
        def sb(n, s, dt=F32):
            return ctx.enter_context(nc.sbuf_tensor("a1_" + n, s, dt))

        w16, wp16 = w.w16, w.wp16
        bqk = sb("bqk", [P, 3, CC])
        bq = sb("bq", [P, CC])
        bv = sb("bv", [P, C])
        bp = sb("bp", [P, CC])
        xc = sb("xc", [P, T])
        gc = sb("gc", [P, T])
        sg = sb("sg", [P, T])
        yf = sb("yf", [P, T])
        y16 = sb("y16", [P, 2, CC, T], F16)
        ynext = sb("ynext", [P, 2, CC, T], F16)
        qkf = sb("qkf", [P, 2, T])
        qk16 = sb("qk16", [P, 2, 2, T], F16)
        stacks = sb("stacks", [P, 2, 2, HPC, T], F16)
        STACKS = ((0, 0, 1), (0, 1, 0))
        parts = nc.dram_tensor("qk1_parts", [2, 2, P, T], F16)
        SROWS = 3 * D1
        vf = sb("vf", [P, TT, P])
        v16 = sb("v16", [P, 2, 2, TT, P], F16)
        nmax = sb("nmax", [P, 2, TT])
        sums = sb("sums", [P, 2, TT])
        rsum = sb("rsum", [P, 2, TT])
        ef = sb("ef", [P, 2, 3, 512])
        t16 = sb("t16", [P, 2, 2, 3, 512], F16)
        ob = sb("ob", [P, 2, TT, P])
        ot16 = sb("ot16", [P, 2, CC, T], F16)
        x3 = sb("x3", [P, CC, T])
        ps = [[ctx.enter_context(nc.psum_tensor(f"ps1_{a}{i}", [P, 512], F32)) for i in range(3)] for a in range(2)]
        pso = ctx.enter_context(nc.psum_tensor("ps1_o", [P, 512], F32))
        psp = ctx.enter_context(nc.psum_tensor("ps1_p", [P, 512], F32))
        s = {n: k.sem("a1_" + n) for n in (
            "fixed", "biased", "first_x", "first_gain", "x_loaded", "sig_step", "sig", "yf", "yhi", "ylo", "y_here",
            "bq", "qproj", "q", "kproj", "k", "qk_low", "parts_out", "stacked", "vproj", "vf", "vhi", "vlo", "scores", "nmax", "expd",
            "turned", "thi", "tlo", "pv", "rsum", "o", "ot_ps", "ot_hi", "ot_lo", "proj", "x3", "x3_loaded", "x3_stored")}
        SCALE = float(np.float32(1.0) / np.sqrt(np.float32(D1)))
        PARTS = ((0, 0), (0, 1), (1, 0))
        wkv = Wkv(k, ctx, "wkv3", 1)
        LAYER = 3
        AHEAD = CC + 1

        def cols(t, j, lo=0, hi=None):
            bank, c0 = score_columns(j)
            hi = P * (j + 1) if hi is None else hi
            return t[bank][:, c0 + lo:c0 + hi] if isinstance(t, list) else t[:, bank, c0 + lo:c0 + hi]

        def chunk_after(b, q, n):
            return (b + (q + n) // CC) % B, (q + n) % CC

        def y_of(n):
            return y16 if isinstance(n, int) and n < CC else ynext

        with nc.Block() as block:

            @block.sync
            def _(sp):
                def xg(b, c, n):
                    x = d["x2"][bass.ds(b, 1), c].rearrange("a p n -> (a p) n")
                    g = d["gain"][2, bass.ds(b, 1), c].rearrange("a p n -> (a p) n")
                    if not (isinstance(n, int) and n == CC):
                        sp.wait_ge(s["yf"], n)
                    sp.dma_start(xc[:], x).then_inc(s["x_loaded"], 16)
                    sp.dma_start(gc[:], g).then_inc(s["x_loaded"], 16)

                def residual(b):
                    x = d["x2"][bass.ds(b, 1)].rearrange("a c p n -> p (a c) n")
                    if not isinstance(b, int):
                        sp.wait_ge(s["x3_stored"], b * 16)
                    sp.dma_start(x3[:], x).then_inc(s["x3_loaded"], 16)

                def store(b):
                    dst = d["x3"][bass.ds(b, 1)].rearrange("a c p n -> p (a c) n")
                    sp.wait_ge(s["x3"], b * CC + CC)
                    sp.dma_start(dst, x3[:]).then_inc(s["x3_stored"], 16)

                def stack(n, q, kind):
                    sp.wait_ge(s["qk_low"], n * 2 + kind + 1)
                    sp.dma_start(parts[kind].rearrange("m p n -> p m n"), qk16[:, kind]).then_inc(s["parts_out"], 16)
                    sp.wait_ge(s["parts_out"], (n * 2 + kind + 1) * 16)
                    for row, part in enumerate(STACKS[kind]):
                        sp.dma_start(stacks[row * D1:(row + 1) * D1, q % 2, kind],
                                     parts[kind, part].rearrange("(i r) n -> r i n", i=HPC)).then_inc(s["stacked"], 16)

                def batch(b, first):
                    for q in range(CC):
                        for kind in range(2):
                            stack(b * CC + q + 1, q + 1, kind)
                        bn, cn = chunk_after(b, q, AHEAD + 1)
                        xg(bn, cn, b * CC + q + (AHEAD + 1))
                        if q == 0 and not first:
                            store(b - 1)
                        if q == 1:
                            residual(b)
                        if q == 2:
                            sp.wait_ge(s["vproj"], b * CC + CC)
                            sp.dma_start(y16[:], ynext[:]).then_inc(s["y_here"], 16)

                sp.dma_start(x3[:], d["x2"][0].rearrange("c p n -> p c n")).then_inc(s["first_x"], 16)
                for half in range(2):
                    sp.dma_start(ef[:, half, 0:2, :], d["gain"][2, 0, 2 * half:2 * half + 2].rearrange("c p n -> p c n")
                                 ).then_inc(s["first_gain"], 16)
                sp.dma_start(bqk[:], d["bqkv1"]).then_inc(s["fixed"], 16)
                sp.dma_start(bv[:], d["bv1"].partition_broadcast(P)).then_inc(s["fixed"], 16)
                sp.dma_start(bp[:], d["bp1"]).then_inc(s["fixed"], 16)
                xg(1, 0, CC)
                xg(1, 1, CC + 1)
                for kind in range(2):
                    stack(0, 0, kind)
                batch(0, True)
                with sp.Fori(1, B) as b:
                    batch(b, False)
                store(B - 1)
                sp.wait_ge(s["x3_stored"], 16 * B)
                sp.wait_ge(s["x_loaded"], 32 * (B * CC + AHEAD + 1 - CC))
                sp.wait_ge(s["stacked"], (B * CC + 1) * 16 * 6)

            @block.gpsimd
            def _(pool):
                def y_low(c, n):
                    pool.wait_ge(s["yhi"], n + 1)
                    y = y_of(n)
                    pool.tensor_tensor(y[:, 1, c, :], yf[:], y[:, 0, c, :], ALU.subtract).then_inc(s["ylo"], 1)

                def v_low(n, q):
                    pool.wait_ge(s["vhi"], n + 1)
                    pool.tensor_tensor(v16[:, q % 2, 1], vf[:], v16[:, q % 2, 0], ALU.subtract).then_inc(s["vlo"], 1)

                def qk_low(n, kind):
                    pool.wait_ge(s["k" if kind else "q"], n + 1)
                    pool.tensor_tensor(qk16[:, kind, 1], qkf[:, kind], qk16[:, kind, 0],
                                       ALU.subtract).then_inc(s["qk_low"], 1)

                wkv.pool_prepare(pool, 0, 0, 0)
                for n in range(CC):
                    y_low(n, n)
                pool.wait_ge(s["ylo"], CC)
                pool.sem_inc(s["y_here"], 16)
                y_low(0, CC)
                qk_low(0, 0)
                qk_low(0, 1)
                v_low(0, 0)

                def batch(b, first):
                    for q in range(CC):
                        it = b * CC + q
                        wkv.join(pool, it)
                        qk_low(it + 1, 0)
                        y_low(chunk_after(0, q, AHEAD)[1], it + AHEAD)
                        qk_low(it + 1, 1)
                        v_low(it + 1, q + 1)
                        wkv.pool_prepare(pool, 0, it + 1, it + 1)

                batch(0, True)
                with pool.Fori(1, B) as b:
                    batch(b, False)

            @block.scalar
            def _(act):
                def y_sigmoid(n):
                    if isinstance(n, int) and n < CC:
                        x = x3[:, n, :]
                        act.wait_ge(s["first_x"], 16)
                    else:
                        x = xc[:]
                        act.wait_ge(s["x_loaded"], n * 32 - 32 * (CC - 1))
                    act.activation(sg[:], x, ACT.Exp, scale=-1.0).then_inc(s["sig_step"], 1)
                    act.wait_ge(s["sig_step"], n * 2 + 1)
                    act.activation(sg[:], sg[:], ACT.Ln, bias=1.0).then_inc(s["sig_step"], 1)
                    act.wait_ge(s["sig_step"], n * 2 + 2)
                    act.activation(sg[:], sg[:], ACT.Exp, scale=-1.0).then_inc(s["sig"], 1)

                def y_high(c, n):
                    act.wait_ge(s["yf"], n + 1)
                    act.activation(y_of(n)[:, 0, c, :], yf[:], ACT.Copy).then_inc(s["yhi"], 1)

                def take_q(n, q):
                    act.wait_ge(s["qproj"], n + 1)
                    act.activation(qk16[:, 0, 0], psp[:], ACT.Identity, bias=bq[:, q:q + 1], scale=SCALE / WSCALE)
                    act.activation(qkf[:, 0], psp[:], ACT.Identity, bias=bq[:, q:q + 1],
                                   scale=SCALE / WSCALE).then_inc(s["q"], 1)

                def take_k(n, q):
                    act.wait_ge(s["kproj"], n + 1)
                    act.activation(qk16[:, 1, 0], psp[:], ACT.Identity, bias=bqk[:, 1, q:q + 1], scale=1.0 / WSCALE)
                    act.activation(qkf[:, 1], psp[:], ACT.Identity, bias=bqk[:, 1, q:q + 1],
                                   scale=1.0 / WSCALE).then_inc(s["k"], 1)

                def v_high(n, q):
                    act.wait_ge(s["vf"], n + 1)
                    act.activation(v16[:, q % 2, 0], vf[:], ACT.Copy).then_inc(s["vhi"], 1)

                def ot_high(n, q):
                    act.wait_ge(s["ot_ps"], n + 1)
                    act.activation(ot16[:, 0, q, :], psp[:], ACT.Copy).then_inc(s["ot_hi"], 1)

                def exps(h, i):
                    for bank, tiles in BANK_TILES:
                        act.wait_ge(s["nmax"], h * 3 + bank + 1)
                        for j in tiles:
                            act.activation(cols(ef[:, i % 2], j), cols(ps[i % 2], j), ACT.Exp,
                                           bias=nmax[:, i % 2, j:j + 1],
                                           accum_out=sums[:, i % 2, j:j + 1]).then_inc(s["expd"], 1)

                def turned_high(h, i):
                    for bank, width in ((0, 512), (1, 512), (2, 256)):
                        act.wait_ge(s["turned"], h * 3 + bank + 1)
                        act.activation(t16[:, i % 2, 0, bank, 0:width], ps[i % 2][bank][:, 0:width],
                                       ACT.Copy).then_inc(s["thi"], 1)

                act.preload_act_table_set("natural_log_exp_and_others")
                wkv.act_load(act, 0, 0, 0, None)
                y_sigmoid(0)
                wkv.act_prepare(act, 0, 0, LAYER, 0, 1)
                y_high(0, 0)
                for n in range(1, CC):
                    y_sigmoid(n)
                    y_high(n, n)
                y_sigmoid(CC)
                y_high(0, CC)
                act.wait_ge(s["bq"], 1)
                take_q(0, 0)
                take_k(0, 0)
                v_high(0, 0)
                exps(0, 0)

                def batch(b, first):
                    for q in range(CC):
                        it = b * CC + q
                        for i in range(HPC):
                            h = b * H1 + (q * HPC + i)
                            if i == 1 and (q or not first):
                                ot_high(it - 1, (q - 1) % CC)
                            turned_high(h, i)
                            exps(h + 1, i + 1)
                            if i == 0:
                                y_sigmoid(it + AHEAD)
                                take_q(it + 1, (q + 1) % CC)
                            if i == 1:
                                if q == CC - 1:
                                    act.wait_ge(s["y_here"], b * 16 + 32)
                                y_high((q + AHEAD) % CC, it + AHEAD)
                                take_k(it + 1, (q + 1) % CC)
                                wkv.act_invert(act, it)
                                wkv.act_load(act, 0, *chunk_after(b, q, 1), it + 1)
                            if i == 2:
                                v_high(it + 1, q + 1)
                            if i == 3:
                                bn, cn = chunk_after(b, q, 1)
                                wkv.act_prepare(act, 0, it + 1, cn * LAYERS + LAYER, it + 1, it + 2)
                                wkv.act_store(act, it, LAYER, b, q)

                batch(0, True)
                with act.Fori(1, B) as b:
                    batch(b, False)
                act.wait_ge(s["ot_ps"], B * CC)
                act.activation(ot16[:, 0, CC - 1, :], psp[:], ACT.Copy).then_inc(s["ot_hi"], 1)
                act.wait_ge(wkv.s["stored"], 16 * B * CC)
                act.wait_ge(wkv.loaded[0], 16 * (B * CC + 1))

            @block.tensor
            def _(pe):
                def project_qk(n, q, kind):
                    for c in range(CC):
                        for m, (yp, wpart) in enumerate(PARTS):
                            mm = pe.matmul(psp[:], w16[:, wpart, q, kind, c, :], y16[:, yp, c, :],
                                           start=c + m == 0, stop=c == CC - 1 and m == 2)
                    mm.then_inc(s["kproj" if kind else "qproj"], 1)

                def project_v(n, q):
                    for t in range(TT):
                        for c in range(CC):
                            for m, (yp, wpart) in enumerate(PARTS):
                                mm = pe.matmul(psp[:, t * P:(t + 1) * P], y16[:, yp, c, t * P:(t + 1) * P],
                                               w16[:, wpart, q, 2, c, :], start=c + m == 0,
                                               stop=c == CC - 1 and m == 2)
                    mm.then_inc(s["vproj"], 1)

                def scores(h, q, i):
                    a, b = ((qkf[0:D1, 0], qkf[0:D1, 1]) if i == 0 else
                            (stacks[0:SROWS, q % 2, 0, i], stacks[0:SROWS, q % 2, 1, i]))
                    for bank, tiles in BANK_TILES:
                        for j in tiles:
                            pe.matmul(cols(ps[i % 2], j), a[:, j * P:(j + 1) * P], b[:, 0:P * (j + 1)],
                                      start=True, stop=False)
                            mm = pe.matmul(cols(ps[i % 2], j, P * j), k.ident_b[:], k.causal_b[:],
                                           start=False, stop=True)
                        mm.then_inc(s["scores"], 1)

                def turn(h, i):
                    pe.wait_ge(s["expd"], h * TT + TT)
                    for bank, tiles in ((0, (0,)), (1, (1, 3)), (2, (2,))):
                        for m in tiles:
                            _, c0 = turned_columns(m)
                            for j in range(m, TT):
                                mm = pe.transpose(ps[i % 2][bank][:, c0 + (j - m) * P:c0 + (j - m + 1) * P],
                                                  cols(ef[:, i % 2], j, m * P, (m + 1) * P), k.ident[:])
                        mm.then_inc(s["turned"], 1)

                def values(h, q, i):
                    if not (isinstance(h, int) and h == 0):
                        pe.wait_ge(s["o"], h)
                    for j in range(TT):
                        for m in range(j + 1):
                            bank, c0 = turned_columns(m)
                            for n, (tp, vp) in enumerate(PARTS):
                                mm = pe.matmul(pso[:, j * D1:(j + 1) * D1],
                                               t16[:, i % 2, tp, bank, c0 + (j - m) * P:c0 + (j - m + 1) * P],
                                               v16[:, q % 2, vp, m, i * D1:(i + 1) * D1],
                                               start=m + n == 0, stop=m == j and n == 2)
                    mm.then_inc(s["pv"], 1)

                def turn_output(n, q):
                    pe.wait_ge(s["o"], n * HPC + HPC)
                    for t in range(TT):
                        mm = pe.transpose(psp[:, t * P:(t + 1) * P], ob[:, q % 2, t, :], k.ident[:])
                    mm.then_inc(s["ot_ps"], 1)

                def output(co):
                    for c in range(CC):
                        for n, (op, wpart) in enumerate(PARTS):
                            mm = pe.matmul(psp[:], wp16[:, wpart, c, co * P:(co + 1) * P], ot16[:, op, c, :],
                                           start=c + n == 0, stop=c == CC - 1 and n == 2)
                    mm.then_inc(s["proj"], 1)

                pe.wait_ge(s["y_here"], 16)
                project_qk(0, 0, 0)
                pe.wait_ge(s["q"], 1)
                project_qk(0, 0, 1)
                pe.wait_ge(s["k"], 1)
                project_v(0, 0)
                scores(0, 0, 0)

                def batch(b, first):
                    for q in range(CC):
                        it = b * CC + q
                        qn = (q + 1) % CC
                        for i in range(HPC):
                            h = b * H1 + (q * HPC + i)
                            last_output = i == 3 and q == 0 and not first
                            if last_output:
                                pe.wait_ge(s["vf"], it + 2)
                                output(0)
                            pe.wait_ge(s["tlo"], h * 3)
                            if i < HPC - 1:
                                if i == 0:
                                    pe.wait_ge(s["stacked"], (it + 1) * 16 * 6)
                                scores(h + 1, q, i + 1)
                            else:
                                scores(h + 1, q + 1, 0)
                            if i == 1 and (q or not first):
                                pe.wait_ge(s["q"], it + 2)
                                turn_output(it - 1, q + 1)
                            if last_output:
                                pe.wait_ge(s["x3"], (b - 1) * CC + 1)
                                output(1)
                            turn(h, i)
                            if last_output:
                                pe.wait_ge(s["x3"], (b - 1) * CC + 2)
                                output(2)
                            if i == 1:
                                pe.wait_ge(s["vlo"], it + 1)
                            if i or q or not first:
                                values(h - 1, q if i else q + 1, (i - 1) % HPC)
                            if i == 0:
                                if q == CC - 1:
                                    pe.wait_ge(s["y_here"], b * 16 + 32)
                                if q == 1 and not first:
                                    pe.wait_ge(s["x3"], b * CC)
                                else:
                                    pe.wait_ge(s["vf"], it + 1)
                                project_qk(it + 1, qn, 0)
                            if i == 1:
                                if q or not first:
                                    pe.wait_ge(s["ot_lo"], it)
                                else:
                                    pe.wait_ge(s["q"], it + 2)
                                project_qk(it + 1, qn, 1)
                            if i == 2:
                                pe.wait_ge(s["k"], it + 2)
                                if q == 2:
                                    pe.wait_ge(s["ylo"], b * CC + 2 * CC)
                                project_v(it + 1, qn)
                            if last_output:
                                pe.wait_ge(s["x3"], (b - 1) * CC + 3)
                                output(3)

                batch(0, True)
                with pe.Fori(1, B) as b:
                    batch(b, False)
                pe.wait_ge(s["tlo"], B * H1 * 3)
                values(B * H1 - 1, CC - 1, HPC - 1)
                pe.wait_ge(s["vf"], B * CC + 1)
                turn_output(B * CC - 1, CC - 1)
                pe.wait_ge(s["ot_lo"], B * CC)
                for co in range(CC):
                    if co:
                        pe.wait_ge(s["x3"], (B - 1) * CC + co)
                    output(co)

            @block.vector
            def _(dve):
                wkv.dve_zero(dve)

                def condition(n):
                    dve.wait_ge(s["sig"], n + 1)
                    if not (isinstance(n, int) and n == 0):
                        dve.wait_ge(s["ylo"], n)
                    if isinstance(n, int) and n < CC:
                        gain = ef[:, n // 2, n % 2, :]
                        dve.wait_ge(s["first_gain"], 32)
                    else:
                        gain = gc[:]
                    dve.tensor_tensor(yf[:], sg[:], gain, ALU.mult).then_inc(s["yf"], 1)

                def take_v(n, q):
                    dve.wait_ge(s["vproj"], n + 1)
                    if not (isinstance(n, int) and n == 0):
                        dve.wait_ge(s["vlo"], n)
                    dve.scalar_tensor_tensor(out=vf[:], in0=psp[:].rearrange("p (t n) -> p t n", t=TT),
                                             scalar=1.0 / WSCALE,
                                             in1=bv[:, q * P:(q + 1) * P].unsqueeze(1).to_broadcast([P, TT, P]),
                                             op0=ALU.mult, op1=ALU.add).then_inc(s["vf"], 1)

                def maxima(h, i):
                    for bank, tiles in BANK_TILES:
                        dve.wait_ge(s["scores"], h * 3 + bank + 1)
                        for j in tiles:
                            m = dve.tensor_reduce(nmax[:, i % 2, j:j + 1], cols(ps[i % 2], j), AX, ALU.max, negate=True)
                        m.then_inc(s["nmax"], 1)

                def turned_low(h, i):
                    for bank, width in ((0, 512), (1, 512), (2, 256)):
                        dve.wait_ge(s["thi"], h * 3 + bank + 1)
                        dve.tensor_tensor(t16[:, i % 2, 1, bank, 0:width], ps[i % 2][bank][:, 0:width],
                                          t16[:, i % 2, 0, bank, 0:width], ALU.subtract).then_inc(s["tlo"], 1)
                    if not isinstance(h, int) or h >= 2:
                        dve.wait_ge(s["o"], h - 1)
                    dve.reciprocal(rsum[:, i % 2, :], sums[:, i % 2, :]).then_inc(s["rsum"], 1)

                def out(h, q, i):
                    dve.wait_ge(s["pv"], h + 1)
                    dve.wait_ge(s["rsum"], h + 1)
                    dve.tensor_tensor(ob[:, q % 2, :, i * D1:(i + 1) * D1],
                                      pso[:, 0:P].rearrange("p (t n) -> p t n", t=TT),
                                      rsum[:, i % 2, :].unsqueeze(2).to_broadcast([P, TT, D1]),
                                      ALU.mult).then_inc(s["o"], 1)

                def ot_low(n, q):
                    dve.wait_ge(s["ot_hi"], n + 1)
                    dve.tensor_tensor(ot16[:, 1, q, :], psp[:], ot16[:, 0, q, :], ALU.subtract).then_inc(s["ot_lo"], 1)

                def output(b, co):
                    dve.wait_ge(s["proj"], b * CC + co + 1)
                    if co == 0:
                        dve.wait_ge(s["biased"], b * 2 + 2)
                    dve.scalar_tensor_tensor(out=x3[:, co, :], in0=psp[:], scalar=1.0 / WSCALE,
                                             in1=x3[:, co, :], op0=ALU.mult, op1=ALU.add).then_inc(s["x3"], 1)

                def add_bias(b, first):
                    dve.wait_ge(s["x3_loaded"], b * 16 + 16)
                    for co in range(first, first + 2):
                        i = dve.tensor_scalar(x3[:, co, :], x3[:, co, :], bp[:, co:co + 1], None, ALU.add)
                    i.then_inc(s["biased"], 1)

                for n in range(CC + 1):
                    condition(n)
                    if n == 0:
                        wkv.dve_prepare(dve, 0, 0)
                dve.wait_ge(s["fixed"], 48)
                dve.tensor_scalar(bq[:], bqk[:, 0, :], SCALE, None, ALU.mult).then_inc(s["bq"], 1)
                take_v(0, 0)
                maxima(0, 0)

                def batch(b, first):
                    for q in range(CC):
                        it = b * CC + q
                        for i in range(HPC):
                            h = b * H1 + (q * HPC + i)
                            last_output = i == 3 and q == 0 and not first
                            if last_output:
                                output(b - 1, 0)
                            if i == 1 and (q or not first):
                                ot_low(it - 1, (q - 1) % CC)
                            maxima(h + 1, i + 1)
                            if last_output:
                                output(b - 1, 1)
                            turned_low(h, i)
                            if last_output:
                                output(b - 1, 2)
                            if i or q or not first:
                                out(h - 1, q if i else q + 1, (i - 1) % HPC)
                            if i == 0:
                                wkv.dve_sums(dve, it, b, q * LAYERS + LAYER, it)
                                condition(it + AHEAD)
                            if i == 1:
                                wkv.dve_guard(dve, it)
                            if i == 2:
                                take_v(it + 1, (q + 1) % CC)
                                wkv.dve_finish(dve, it, b, it)
                            if last_output:
                                output(b - 1, 3)
                            if i == 3:
                                wkv.dve_prepare(dve, it + 1, it + 1)
                                if q >= 2:
                                    add_bias(b, (q - 2) * 2)

                batch(0, True)
                with dve.Fori(1, B) as b:
                    batch(b, False)
                out(B * H1 - 1, CC - 1, HPC - 1)
                ot_low(B * CC - 1, CC - 1)
                for co in range(CC):
                    output(B - 1, co)


def layer1_ffn(k):
    nc, d = k.nc, k.d
    with ExitStack() as ctx:
        def sb(n, s, dt=F32):
            return ctx.enter_context(nc.sbuf_tensor("f_" + n, s, dt))

        NQ = 4
        HN, CN = F // NQ, C // NQ
        PIECE = CC * HN
        stage = sb("stage", [P, 3, PIECE])
        w0 = sb("w0", [P, 2, NQ, CC, HN], F16)
        w1 = sb("w1", [P, 2, NQ, NF, CN], F16)
        b0 = sb("b0", [P, NF])
        b1 = sb("b1", [P, CC])
        xt = sb("xt", [P, 2, CC, T])
        gt = sb("gt", [P, CC, T])
        yf = sb("yf", [P, CC, T])
        y = sb("y", [P, CC, T], F16)
        h = sb("h", [P, NF, T], F16)
        e16 = sb("e16", [P, 2, T], F16)
        xo = sb("xo", [P, 2, T])
        psh = [ctx.enter_context(nc.psum_tensor(f"psf_h{i}", [P, 512], F32)) for i in range(4)]
        pse = [ctx.enter_context(nc.psum_tensor(f"psf_e{i}", [P, 512], F32)) for i in range(2)]
        s = {n: k.sem("f_" + n) for n in (
            "fixed", "raw0", "raw1", "raw2", "hi", "lo", "x_loaded", "sig", "y", "hid", "gelu", "e_ps", "e16", "xo",
            "stored0", "stored1")}

        def raw_piece(i):
            return stage[:, i % 3, :].rearrange("p (k n) -> p k n", k=CC if i < NQ else NF)

        def split_piece(i, part):
            return w0[:, part, i] if i < NQ else w1[:, part, i - NQ]

        def batch_x(b):
            return xt[:, bass.ds(b % 2, 1)].rearrange("p a c n -> p (a c) n")

        with nc.Block() as block:

            @block.sync
            def _(sp):
                def raw(i):
                    src = d["w0"][:, :, i * HN:(i + 1) * HN] if i < NQ else d["w1"][:, :, (i - NQ) * CN:(i - NQ + 1) * CN]
                    if i >= 3:
                        sp.wait_ge(s["lo"], i - 2)
                    sp.dma_start(raw_piece(i), src).then_inc(s[f"raw{i % 3}"], 16)

                def load(b, n):
                    xsrc = d["x3"][bass.ds(b, 1)].rearrange("a c p n -> p (a c) n")
                    gsrc = d["gain"][3, bass.ds(b, 1)].rearrange("a c p n -> p (a c) n")
                    dst = batch_x(n)
                    if not isinstance(n, int):
                        sp.wait_ge(s["xo"], n * CC - CC)
                    sp.dma_start(dst, xsrc).then_inc(s["x_loaded"], 16)
                    if not isinstance(n, int) or n:
                        sp.wait_ge(s["y"], n * CC)
                    sp.dma_start(gt[:], gsrc).then_inc(s["x_loaded"], 16)

                def store(b):
                    for co in range(CC):
                        dst = d["out"][bass.ds(b, 1), co].rearrange("a p n -> (a p) n")
                        sp.wait_ge(s["xo"], b * CC + co + 1)
                        sp.dma_start(dst, xo[:, co % 2, :]).then_inc(s[f"stored{co % 2}"], 16)

                load(0, 0)
                sp.dma_start(b0[:], d["b0"]).then_inc(s["fixed"], 16)
                sp.dma_start(b1[:], d["b1"]).then_inc(s["fixed"], 16)
                for i in range(2 * NQ):
                    raw(i)
                load(1, 1)
                with sp.Fori(0, B - 2) as b:
                    store(b)
                    load(b + 2, b + 2)
                store(B - 2)
                store(B - 1)
                for i in range(2):
                    sp.wait_ge(s[f"stored{i}"], 16 * (1 + B * CC // 2))

            @block.scalar
            def _(act):
                def high(i):
                    act.wait_ge(s[f"raw{i % 3}"], 16 * (i // 3 + 1))
                    act.activation(split_piece(i, 0), raw_piece(i), ACT.Copy, scale=WSCALE).then_inc(s["hi"], 1)

                def sigmoid(b):
                    src = batch_x(b)
                    act.wait_ge(s["x_loaded"], b * 32 + 32)
                    for c in range(CC):
                        act.activation(yf[:, c, :], src[:, c, :], ACT.Sigmoid).then_inc(s["sig"], 1)

                def gelu(b, n):
                    act.wait_ge(s["hid"], b * NF + n + 1)
                    act.activation(h[:, n, :], psh[n % 4][:], ACT.Gelu, bias=b0[:, n:n + 1],
                                   scale=1.0 / WSCALE).then_inc(s["gelu"], 1)

                def outputs(b):
                    for co in range(CC):
                        act.wait_ge(s["e_ps"], b * CC + co + 1)
                        if co >= 2 or not isinstance(b, int) or b:
                            act.wait_ge(s["xo"], b * CC + co - 1)
                        act.activation(e16[:, co % 2, :], pse[co % 2][:], ACT.Identity, bias=b1[:, co:co + 1],
                                       scale=1.0 / WSCALE).then_inc(s["e16"], 1)

                sigmoid(0)
                high(0)
                act.wait_ge(s["fixed"], 32)
                for i in range(1, 2 * NQ):
                    high(i)
                    if i < NQ:
                        for n in range(4 * (i - 1), 4 * i):
                            gelu(0, n)
                    elif i == NQ:
                        for n in range(4 * (NQ - 1), 4 * NQ):
                            gelu(0, n)
                sigmoid(1)
                outputs(0)
                with act.Fori(1, B - 1) as b:
                    for n in range(NF):
                        gelu(b, n)
                    sigmoid(b + 1)
                    outputs(b)
                for n in range(NF):
                    gelu(B - 1, n)
                outputs(B - 1)

            @block.tensor
            def _(pe):
                def batch(b, first):
                    pe.wait_ge(s["y"], b * CC + CC)
                    for n in range(NF):
                        if first and n % 4 == 0:
                            pe.wait_ge(s["lo"], n // 4 + 1)
                        if n >= 4:
                            pe.wait_ge(s["gelu"], b * NF + n - 3)
                        q, r = divmod(n, 4)
                        for c in range(CC):
                            for part in range(2):
                                mm = pe.matmul(psh[n % 4][:], w0[:, part, q, c, r * P:(r + 1) * P], y[:, c, :],
                                               start=c + part == 0, stop=c == CC - 1 and part == 1)
                        mm.then_inc(s["hid"], 1)
                    for co in range(CC):
                        if first:
                            pe.wait_ge(s["lo"], NQ + co + 1)
                        if co >= 2 or not first:
                            pe.wait_ge(s["e16"], b * CC + co - 1)
                        for n in range(NF):
                            if co == 0:
                                pe.wait_ge(s["gelu"], b * NF + n + 1)
                            for part in range(2):
                                mm = pe.matmul(pse[co % 2][:], w1[:, part, co, n, :], h[:, n, :],
                                               start=n + part == 0, stop=n == NF - 1 and part == 1)
                        mm.then_inc(s["e_ps"], 1)

                batch(0, True)
                with pe.Fori(1, B) as b:
                    batch(b, False)

            @block.vector
            def _(dve):
                def low(i):
                    dve.wait_ge(s["hi"], i + 1)
                    dve.scalar_tensor_tensor(out=split_piece(i, 1), in0=raw_piece(i), scalar=WSCALE,
                                             in1=split_piece(i, 0), op0=ALU.mult,
                                             op1=ALU.subtract).then_inc(s["lo"], 1)

                def condition(b, first):
                    if not first:
                        dve.wait_ge(s["hid"], b * NF)
                    for c in range(CC):
                        dve.wait_ge(s["sig"], b * CC + c + 1)
                        dve.tensor_tensor(y[:, c, :], yf[:, c, :], gt[:, c, :], ALU.mult).then_inc(s["y"], 1)

                def outputs(b):
                    src = batch_x(b)
                    for co in range(CC):
                        dve.wait_ge(s["e16"], b * CC + co + 1)
                        dve.wait_ge(s[f"stored{co % 2}"], b * 32 + 16 * (co // 2) + 16)
                        dve.tensor_tensor(xo[:, co % 2, :], src[:, co, :], e16[:, co % 2, :],
                                          ALU.add).then_inc(s["xo"], 1)

                for i in range(2):
                    dve.sem_inc(s[f"stored{i}"], 16)
                condition(0, True)
                for i in range(2 * NQ):
                    low(i)
                condition(1, False)
                outputs(0)
                with dve.Fori(1, B - 1) as b:
                    condition(b + 1, False)
                    outputs(b)
                outputs(B - 1)


SCRATCH = {
    "gain": (LAYERS, B, CC, P, T), "x1": (B, CC, P, T), "x2": (B, CC, P, T), "x3": (B, CC, P, T),
    "slot_x": ((SLOT_TILES + 1) * P, C), "slot_y": (SLOT_TILES * P, C),
}


def rotation():
    half = D0 // 2
    inv = np.float32(1.0) / np.float32(10000.0) ** (np.arange(half, dtype=np.float32) / np.float32(half))
    th = np.arange(T, dtype=np.float32)[None, :] * inv[:, None]
    cos, sin = np.cos(th), np.sin(th)
    cos, sin = np.concatenate([cos, cos]), np.concatenate([-sin, sin])
    scale = np.float32(D0 ** -0.5)
    return np.ascontiguousarray(np.stack([cos * scale, sin * scale, cos, sin], 1) / np.float32(WSCALE).astype(np.float32))


def transposed(x):
    return np.ascontiguousarray(np.transpose(x, (0, 2, 1))).reshape(B, CC, P, T)


def layouts(i):
    a = {n: np.asarray(v) for n, v in i.items()}

    def rows(w):
        return np.ascontiguousarray(w.reshape(w.shape[0] // P, P, -1).transpose(1, 0, 2))

    cond = ["L0_cond", "L0_cond2", "L1_cond", "L1_cond2"]
    wu = np.stack([np.stack([a[n + "_" + x] for n in cond]) for x in "wu"])
    wqkv = np.stack([a["L0_attn_W" + x].reshape(CC, P, H0, D0) for x in "qkv"])
    down = np.zeros((E, KI * P, C), np.float32)
    down[:, :I] = a["L0_ffn_down_w"].transpose(0, 2, 1)
    qkv1 = a["L1_attn_w_attn"].reshape(CC, P, 3, CC, P)
    return {
        "xT": transposed(a["x"]),
        "fT": transposed(a["fside_BxSxS_0"]),
        "cond": np.ascontiguousarray(a["cond_512"].reshape(-1)),
        "wu": np.ascontiguousarray(wu.reshape(2, LAYERS, CC, P).transpose(3, 0, 2, 1).reshape(P, 2, CC * LAYERS)),
        "wqkv0": np.ascontiguousarray(wqkv.transpose(3, 2, 0, 1, 4)),
        "wo": np.ascontiguousarray(a["L0_attn_Wo"].reshape(H0, D0, C).transpose(1, 0, 2)),
        "wg": rows(a["L0_attn_Wg"]),
        "rot": rotation(),
        "router": rows(np.ascontiguousarray(a["L0_ffn_router_w"].T)),
        "gate_up": np.ascontiguousarray(np.stack([a["L0_ffn_gate_w"], a["L0_ffn_up_w"]], 1)
                                        .reshape(E, 2, I, CC, P).transpose(4, 0, 1, 3, 2)),
        "down": np.ascontiguousarray(down.reshape(E, KI, P, C).transpose(2, 0, 1, 3)),
        "wqkv1": np.ascontiguousarray(qkv1.transpose(3, 1, 2, 0, 4)),
        "bqkv1": np.ascontiguousarray(a["L1_attn_b_attn"].reshape(3, CC, P).transpose(2, 0, 1)),
        "bv1": np.ascontiguousarray(a["L1_attn_b_attn"].reshape(1, 3, C)[:, 2]),
        "wp1": rows(a["L1_attn_w_proj"]),
        "bp1": np.ascontiguousarray(a["L1_attn_b_proj"].reshape(CC, P).T),
        "w0": rows(np.ascontiguousarray(a["L1_ffn_W0"].T)),
        "b0": np.ascontiguousarray(a["L1_ffn_bias0"].reshape(NF, P).T),
        "w1": rows(np.ascontiguousarray(a["L1_ffn_W1"].T)),
        "b1": np.ascontiguousarray(a["L1_ffn_bias1"].reshape(CC, P).T),
    }


STAGES = [layer0_attn, moe_and_attention, layer1_ffn]


def program(nc, dram, stages=None):
    with ExitStack() as ctx:
        k = Core(nc, ctx, dram)
        constants(k)
        wkv_setup(k)
        for stage in (stages or STAGES):
            with nc.cleanup_on_exit():
                stage(k)


def kernel(**inputs):
    import concourse.bacc as bacc
    from concourse.bass_utils import run_bass_kernel_spmd

    nc = bacc.Bacc("TRN2", target_bir_lowering=False, num_devices=1)
    arrays, dram = {}, {}
    for name, a in layouts(inputs).items():
        arrays["in_" + name] = a
        dram[name] = nc.dram_tensor("in_" + name, a.shape, mybir.dt.from_np(a.dtype), kind="ExternalInput").ap()
    for name, shape in SCRATCH.items():
        dram[name] = nc.dram_tensor("scratch_" + name, shape, F32).ap()
    dram["out"] = nc.dram_tensor("out_0", (B, CC, P, T), F32, kind="ExternalOutput").ap()
    program(nc, dram)
    out = run_bass_kernel_spmd(nc, [arrays], core_ids=[0]).results[0]["out_0"]
    return np.ascontiguousarray(np.transpose(out.reshape(B, C, T), (0, 2, 1)))
```
